# Optimizing a Trainium2 kernel written in Bass

```python
import numpy as np
import jax
import jax.numpy as jnp

def _softmax(x, axis=-1):
    return jax.nn.softmax(x, axis=axis)

def _gelu(x):
    return jax.nn.gelu(x, approximate=True)

def _silu(x):
    return jax.nn.silu(x)

def _sigmoid(x):
    return jax.nn.sigmoid(x)

def _layernorm(x, axis=-1, eps=1e-05):
    m = jnp.mean(x, axis=axis, keepdims=True)
    v = jnp.var(x, axis=axis, keepdims=True)
    return (x - m) / jnp.sqrt(v + eps)

def _scatter_add(tgt, idx, src, axis=0):
    return tgt.at[idx].add(src)

def _segment_sum(src, seg, n):
    return jax.ops.segment_sum(src, seg, n)
kernel_name = 'mk_vit_tower_d2_tok_img768_r4_87f92d'

def setup_inputs(seed: int=0):
    np.random.seed(seed)
    _w = jnp.asarray

    def _rec_inputs():
        import jax
        import jax.numpy as jnp
        _rk = jax.random.key(seed)
        x = -0.00016672 + 0.999947 * jax.random.normal(jax.random.fold_in(_rk, 1), (32, 96, 96, 3), jnp.float32)
        return x
    x = _rec_inputs()

    def _L0_tok_setup():
        import jax, jax.numpy as jnp
        import numpy as np
        PATCH = 16
        HIDDEN = 192

        def extract_patches(x, p):
            B, H, W, C = x.shape
            Hp, Wp = (H // p, W // p)
            x = x.reshape(B, Hp, p, Wp, p, C)
            x = x.transpose(0, 1, 3, 2, 4, 5)
            return x.reshape(B, Hp * Wp, p * p * C)
        key = jax.random.key(seed)
        k1, k2, k3, k4, k5 = jax.random.split(key, 5)
        B, H, W, C = (64, 96, 96, 3)
        num_patches = (H // PATCH) ** 2
        patch_dim = PATCH * PATCH * C
        contactMap = jax.random.normal(k1, (B, H, W, C), dtype=jnp.float32)
        W_proj = jax.random.normal(k2, (patch_dim, HIDDEN), dtype=jnp.float32) * (1.0 / np.sqrt(patch_dim))
        b_proj = jnp.zeros((HIDDEN,), dtype=jnp.float32)
        cls_token = jax.random.normal(k3, (1, 1, HIDDEN), dtype=jnp.float32) * 0.05
        pos_embedding = jax.random.normal(k4, (num_patches + 1, HIDDEN), dtype=jnp.float32) * 0.05
        return {'contactMap': contactMap, 'W_proj': W_proj, 'b_proj': b_proj, 'cls_token': cls_token, 'pos_embedding': pos_embedding}
    _L0_tok_all = _L0_tok_setup()
    _L0_tok_in = {k: v for k, v in _L0_tok_all.items() if k in ('W_proj', 'b_proj', 'cls_token', 'pos_embedding')}
    del _L0_tok_all

    def _L0_attn_setup():
        import jax, jax.numpy as jnp
        import numpy as np
        import math
        LATENT_RANK = 64
        NUM_HEADS = 12
        HEAD_DIM = 64
        key = jax.random.key(seed)
        k1, k2, k3, k4, k5 = jax.random.split(key, 5)
        b, n, h = (8, 256, 192)
        r, nh = (LATENT_RANK, NUM_HEADS)
        std = 0.02
        return {'hidden_states': jax.random.normal(k1, (b, n, h), dtype=jnp.float32), 'basis_w': jax.random.normal(k2, (r, h), dtype=jnp.float32) * std, 'core': jax.random.normal(k3, (r, r), dtype=jnp.float32) * std, 'head_residual': jax.random.normal(k4, (nh, r, r), dtype=jnp.float32) * (std / 10.0), 'value_w': jax.random.normal(k5, (h, h), dtype=jnp.float32) * std, 'value_b': jnp.zeros((h,), dtype=jnp.float32)}
    _L0_attn_all = _L0_attn_setup()
    _L0_attn_in = {k: v for k, v in _L0_attn_all.items() if k in ('basis_w', 'core', 'head_residual', 'value_w', 'value_b')}
    del _L0_attn_all

    def _L0_ffn_setup():
        import jax, jax.numpy as jnp
        import numpy as np
        B, S, H, D, E = (4, 512, 192, 256, 8)
        TOP_K = 2
        EPS = 1e-08
        LN_EPS = 1e-05

        def _gelu(t):
            return jax.nn.gelu(t, approximate=False)

        def _layer_norm(t, gamma, beta):
            mu = jnp.mean(t, axis=-1, keepdims=True)
            var = jnp.mean(jnp.square(t - mu), axis=-1, keepdims=True)
            return (t - mu) * jax.lax.rsqrt(var + LN_EPS) * gamma + beta
        key = jax.random.key(seed)
        ks = jax.random.split(key, 8)
        x = jax.random.normal(ks[0], (B, S, H), dtype=jnp.float32)
        w1 = jax.random.normal(ks[1], (H, H // 2), dtype=jnp.float32) * 0.02
        b1 = jnp.zeros((H // 2,), dtype=jnp.float32)
        w2 = jax.random.normal(ks[2], (H // 2, E), dtype=jnp.float32) * 0.02
        b2 = jnp.zeros((E,), dtype=jnp.float32)
        a_dn = float(np.sqrt(6.0 / (H + D)))
        a_up = float(np.sqrt(6.0 / (D + H)))
        down_w = jax.random.uniform(ks[3], (E, H, D), dtype=jnp.float32, minval=-a_dn, maxval=a_dn)
        down_b = jnp.zeros((E, D), dtype=jnp.float32)
        up_w = jax.random.uniform(ks[4], (E, D, H), dtype=jnp.float32, minval=-a_up, maxval=a_up)
        gamma = jnp.ones((H,), dtype=jnp.float32)
        beta = jnp.zeros((H,), dtype=jnp.float32)
        return {'x': x, 'w1': w1, 'b1': b1, 'w2': w2, 'b2': b2, 'down_w': down_w, 'down_b': down_b, 'up_w': up_w, 'gamma': gamma, 'beta': beta}
    _L0_ffn_all = _L0_ffn_setup()
    _L0_ffn_in = {k: v for k, v in _L0_ffn_all.items() if k in ('w1', 'b1', 'w2', 'b2', 'down_w', 'down_b', 'up_w', 'gamma', 'beta')}
    del _L0_ffn_all

    def _L1_attn_setup():
        import jax, jax.numpy as jnp
        import numpy as np
        B, N, D = (4, 2048, 192)
        H, DH = (12, 64)
        INNER = H * DH
        key = jax.random.key(seed)
        k0, k1, k2 = jax.random.split(key, 3)
        return {'x': jax.random.normal(k0, (B, N, D), dtype=jnp.float32), 'w_qkv': jax.random.normal(k1, (D, INNER), dtype=jnp.float32) * 0.02, 'temp': jnp.ones((H, 1), dtype=jnp.float32), 'w_out': jax.random.normal(k2, (INNER, D), dtype=jnp.float32) * 0.02, 'b_out': jnp.zeros((D,), dtype=jnp.float32)}
    _L1_attn_all = _L1_attn_setup()
    _L1_attn_in = {k: v for k, v in _L1_attn_all.items() if k in ('w_qkv', 'temp', 'w_out', 'b_out')}
    del _L1_attn_all

    def _L1_ffn_setup():
        import jax, jax.numpy as jnp
        import numpy as np
        B, S, D = (4, 256, 192)
        E = 8
        H = 192
        HS = 768
        TOPK_ROUTED = 2
        key = jax.random.key(seed)
        ks = jax.random.split(key, 10)
        w = lambda k, shape: jax.random.normal(k, shape, dtype=jnp.float32) * 0.02
        return {'x': jax.random.normal(ks[0], (B, S, D), dtype=jnp.float32), 'router_w': w(ks[1], (D, E)), 'w_gate': w(ks[2], (E, D, H)), 'w_up': w(ks[3], (E, D, H)), 'w_down': w(ks[4], (E, H, D)), 'ws_gate': w(ks[5], (D, HS)), 'ws_up': w(ks[6], (D, HS)), 'ws_down': w(ks[7], (HS, D)), 'sg_w': w(ks[8], (D, 1)), 'sg_b': jnp.zeros((1,), jnp.float32)}
    _L1_ffn_all = _L1_ffn_setup()
    _L1_ffn_in = {k: v for k, v in _L1_ffn_all.items() if k in ('router_w', 'w_gate', 'w_up', 'w_down', 'ws_gate', 'ws_up', 'ws_down', 'sg_w', 'sg_b')}
    del _L1_ffn_all
    return {'x': x, 'L0_tok_W_proj': _L0_tok_in['W_proj'], 'L0_tok_b_proj': _L0_tok_in['b_proj'], 'L0_tok_cls_token': _L0_tok_in['cls_token'], 'L0_tok_pos_embedding': _L0_tok_in['pos_embedding'], 'L0_attn_basis_w': _L0_attn_in['basis_w'], 'L0_attn_core': _L0_attn_in['core'], 'L0_attn_head_residual': _L0_attn_in['head_residual'], 'L0_attn_value_w': _L0_attn_in['value_w'], 'L0_attn_value_b': _L0_attn_in['value_b'], 'L0_ffn_w1': _L0_ffn_in['w1'], 'L0_ffn_b1': _L0_ffn_in['b1'], 'L0_ffn_w2': _L0_ffn_in['w2'], 'L0_ffn_b2': _L0_ffn_in['b2'], 'L0_ffn_down_w': _L0_ffn_in['down_w'], 'L0_ffn_down_b': _L0_ffn_in['down_b'], 'L0_ffn_up_w': _L0_ffn_in['up_w'], 'L0_ffn_gamma': _L0_ffn_in['gamma'], 'L0_ffn_beta': _L0_ffn_in['beta'], 'L1_attn_w_qkv': _L1_attn_in['w_qkv'], 'L1_attn_temp': _L1_attn_in['temp'], 'L1_attn_w_out': _L1_attn_in['w_out'], 'L1_attn_b_out': _L1_attn_in['b_out'], 'L1_ffn_router_w': _L1_ffn_in['router_w'], 'L1_ffn_w_gate': _L1_ffn_in['w_gate'], 'L1_ffn_w_up': _L1_ffn_in['w_up'], 'L1_ffn_w_down': _L1_ffn_in['w_down'], 'L1_ffn_ws_gate': _L1_ffn_in['ws_gate'], 'L1_ffn_ws_up': _L1_ffn_in['ws_up'], 'L1_ffn_ws_down': _L1_ffn_in['ws_down'], 'L1_ffn_sg_w': _L1_ffn_in['sg_w'], 'L1_ffn_sg_b': _L1_ffn_in['sg_b']}

def reference(x, L0_tok_W_proj, L0_tok_b_proj, L0_tok_cls_token, L0_tok_pos_embedding, L0_attn_basis_w, L0_attn_core, L0_attn_head_residual, L0_attn_value_w, L0_attn_value_b, L0_ffn_w1, L0_ffn_b1, L0_ffn_w2, L0_ffn_b2, L0_ffn_down_w, L0_ffn_down_b, L0_ffn_up_w, L0_ffn_gamma, L0_ffn_beta, L1_attn_w_qkv, L1_attn_temp, L1_attn_w_out, L1_attn_b_out, L1_ffn_router_w, L1_ffn_w_gate, L1_ffn_w_up, L1_ffn_w_down, L1_ffn_ws_gate, L1_ffn_ws_up, L1_ffn_ws_down, L1_ffn_sg_w, L1_ffn_sg_b):
    import jax
    import jax.numpy as jnp

    def _L0_tok_ref(contactMap, W_proj, b_proj, cls_token, pos_embedding):
        import jax, jax.numpy as jnp
        import numpy as np
        PATCH = 16
        HIDDEN = 192

        def extract_patches(x, p):
            B, H, W, C = x.shape
            Hp, Wp = (H // p, W // p)
            x = x.reshape(B, Hp, p, Wp, p, C)
            x = x.transpose(0, 1, 3, 2, 4, 5)
            return x.reshape(B, Hp * Wp, p * p * C)
        B = contactMap.shape[0]
        patches = extract_patches(contactMap, PATCH)
        enc = jnp.einsum('bnd,dh->bnh', patches, W_proj) + b_proj
        cls = jnp.broadcast_to(cls_token.astype(contactMap.dtype), (B, 1, enc.shape[-1]))
        enc = jnp.concatenate([cls, enc], axis=1)
        return enc + pos_embedding

    def _L0_attn_ref(hidden_states, basis_w, core, head_residual, value_w, value_b):
        import jax, jax.numpy as jnp
        import numpy as np
        import math
        LATENT_RANK = 64
        NUM_HEADS = 12
        HEAD_DIM = 64
        b, n, hidden = hidden_states.shape
        nh, r = (head_residual.shape[0], core.shape[0])
        hd = hidden // nh
        latent = jnp.einsum('bnh,rh->bnr', hidden_states, basis_w)
        centered = head_residual - jnp.mean(head_residual, axis=0, keepdims=True)
        head_mats = core[None, :, :] / float(nh) + centered
        scores = jnp.einsum('bnr,hrs,bms->bhnm', latent, head_mats, latent)
        scores = scores / math.sqrt(float(r))
        probs = jax.nn.softmax(scores, axis=-1)
        v = jnp.einsum('bnh,oh->bno', hidden_states, value_w) + value_b
        v = v.reshape(b, n, nh, hd).transpose(0, 2, 1, 3)
        ctx = jnp.einsum('bhnm,bhmd->bhnd', probs, v)
        ctx = ctx.transpose(0, 2, 1, 3).reshape(b, n, hidden)
        return ctx

    def _L0_ffn_ref(x, w1, b1, w2, b2, down_w, down_b, up_w, gamma, beta):
        import jax, jax.numpy as jnp
        import numpy as np
        B, S, H, D, E = (4, 512, 192, 256, 8)
        TOP_K = 2
        EPS = 1e-08
        LN_EPS = 1e-05

        def _gelu(t):
            return jax.nn.gelu(t, approximate=False)

        def _layer_norm(t, gamma, beta):
            mu = jnp.mean(t, axis=-1, keepdims=True)
            var = jnp.mean(jnp.square(t - mu), axis=-1, keepdims=True)
            return (t - mu) * jax.lax.rsqrt(var + LN_EPS) * gamma + beta
        logits = _gelu(x @ w1 + b1) @ w2 + b2
        routing = jax.nn.softmax(logits, axis=-1)
        topv, topi = jax.lax.top_k(routing, TOP_K)
        sparse = jnp.sum(jax.nn.one_hot(topi, E, dtype=routing.dtype) * topv[..., None], axis=-2)
        sparse = sparse / (jnp.sum(sparse, axis=-1, keepdims=True) + EPS)
        z = _gelu(jnp.einsum('bsh,ehd->bsed', x, down_w) + down_b)
        expert_out = jnp.einsum('bsed,edh->bseh', z, up_w)
        moe_out = jnp.einsum('bseh,bse->bsh', expert_out, sparse)
        return _layer_norm(x + moe_out, gamma, beta)

    def _L1_attn_ref(x, w_qkv, temp, w_out, b_out):
        import jax, jax.numpy as jnp
        import numpy as np
        B, N, D = (4, 2048, 192)
        H, DH = (12, 64)
        INNER = H * DH
        b, n, _ = x.shape
        h = temp.shape[0]
        w = (x @ w_qkv).reshape(b, n, h, -1).transpose(0, 2, 1, 3)
        norm = jnp.sqrt(jnp.sum(w * w, axis=2, keepdims=True))
        w_normed = w / jnp.maximum(norm, 1e-12)
        logits = jnp.sum(w_normed * w_normed, axis=-1) * temp
        Pi = jax.nn.softmax(logits, axis=-1)
        Pi_norm = Pi / (jnp.sum(Pi, axis=-1, keepdims=True) + 1e-08)
        dots = jnp.einsum('bhn,bhnd->bhd', Pi_norm, w * w)[:, :, None, :]
        attn = 1.0 / (1.0 + dots)
        out = -(w * Pi[..., None]) * attn
        out = out.transpose(0, 2, 1, 3).reshape(b, n, -1)
        return out @ w_out + b_out

    def _L1_ffn_ref(x, router_w, w_gate, w_up, w_down, ws_gate, ws_up, ws_down, sg_w, sg_b):
        import jax, jax.numpy as jnp
        import numpy as np
        B, S, D = (4, 256, 192)
        E = 8
        H = 192
        HS = 768
        TOPK_ROUTED = 2
        probs = jax.nn.softmax(x @ router_w, axis=-1)
        gates, idx = jax.lax.top_k(probs, TOPK_ROUTED)
        gates = gates / jnp.sum(gates, axis=-1, keepdims=True)
        n_exp = router_w.shape[1]
        dense_g = jnp.sum(jax.nn.one_hot(idx, n_exp, dtype=x.dtype) * gates[..., None], axis=-2)
        g = jax.nn.silu(jnp.einsum('bsd,edh->bseh', x, w_gate))
        u = jnp.einsum('bsd,edh->bseh', x, w_up)
        expert_out = jnp.einsum('bseh,ehd->bsed', g * u, w_down)
        routed = jnp.einsum('bse,bsed->bsd', dense_g, expert_out)
        shared = jax.nn.silu(x @ ws_gate) * (x @ ws_up) @ ws_down
        alpha = jax.nn.sigmoid(x @ sg_w + sg_b)
        return alpha * shared + (1.0 - alpha) * routed
    h = _L0_tok_ref(x, L0_tok_W_proj, L0_tok_b_proj, L0_tok_cls_token, L0_tok_pos_embedding)
    h = h + _L0_attn_ref(_layernorm(h, axis=-1), L0_attn_basis_w, L0_attn_core, L0_attn_head_residual, L0_attn_value_w, L0_attn_value_b)
    h = h + _L0_ffn_ref(_layernorm(h, axis=-1), L0_ffn_w1, L0_ffn_b1, L0_ffn_w2, L0_ffn_b2, L0_ffn_down_w, L0_ffn_down_b, L0_ffn_up_w, L0_ffn_gamma, L0_ffn_beta)
    h = h + _L1_attn_ref(_layernorm(h, axis=-1), L1_attn_w_qkv, L1_attn_temp, L1_attn_w_out, L1_attn_b_out)
    h = h + _L1_ffn_ref(_layernorm(h, axis=-1), L1_ffn_router_w, L1_ffn_w_gate, L1_ffn_w_up, L1_ffn_w_down, L1_ffn_ws_gate, L1_ffn_ws_up, L1_ffn_ws_down, L1_ffn_sg_w, L1_ffn_sg_b)
    return h

_drawn_inputs = setup_inputs


def setup_inputs(seed=0):
    import zlib

    import numpy as np

    out = dict(_drawn_inputs(seed))
    spreads = {'L0_tok_b_proj': (0.0, 0.1),
     'L0_attn_value_b': (0.0, 0.1),
     'L0_ffn_b1': (0.0, 0.1),
     'L0_ffn_b2': (0.0, 0.1),
     'L0_ffn_down_b': (0.0, 0.347),
     'L0_ffn_gamma': (1.0, 0.2),
     'L0_ffn_beta': (0.0, 0.1),
     'L1_attn_temp': (1.0, 0.6),
     'L1_attn_b_out': (0.0, 0.1)}
    factors = {'L0_attn_basis_w': 8.0,
     'L0_attn_core': 8.0,
     'L0_attn_head_residual': 8.0,
     'L1_attn_w_qkv': 8.0,
     'L1_attn_w_out': 8.0,
     'L1_ffn_router_w': 8.0,
     'L1_ffn_w_gate': 8.0,
     'L1_ffn_w_up': 8.0,
     'L1_ffn_w_down': 8.0,
     'L1_ffn_ws_gate': 8.0,
     'L1_ffn_ws_up': 8.0,
     'L1_ffn_ws_down': 8.0,
     'L1_ffn_sg_w': 8.0}
    for name, (base, spread) in spreads.items():
        noise = np.random.default_rng([zlib.crc32(name.encode()), seed]).standard_normal(out[name].shape)
        drawn = base * np.exp(spread * noise) if base else spread * noise
        out[name] = jnp.asarray(drawn.astype(out[name].dtype))
    for name, factor in factors.items():
        out[name] = (out[name] * factor).astype(out[name].dtype)
    return out
```

```python
from contextlib import ExitStack

import concourse.bass as bass
from concourse import mybir

F32 = mybir.dt.float32
F32R = mybir.dt.float32r
U32 = mybir.dt.uint32
ALU = mybir.AluOpType
ACT = mybir.ActivationFunctionType
X = mybir.AxisListType.X

D = 192
DR = D - 128
NI, NTOK = 32, 37
NC, NP = 4, 4
RT = 2 * NTOK
NT = NP * RT
IMG = 2 * NP
KP = 6
NH, HD, RK = 12, 16, 64
NG, GH = 4, 3
VR = GH * NTOK
E0, T0 = 8, 16
T1R, T1 = 12, 18
QJ = 6
EPS = 1e-5
SELW = 64

C_ID, C_II = 0, 128
C_B = C_II + DR
C_SB = C_B + QJ * NH
C_VM = C_SB + QJ * 128
C_MAB = C_VM + GH
C_IOTA = C_MAB + 2
C_ALL = C_IOTA + E0

NSEL = (E0 + T1R + 1) * 128

SZ_TOK = KP * D
SZ_DN0, SZ_UP0 = T0 * 128, T0 * D
SZ_W1 = 96
SZ_GU = 2 * T1 * 128
SZ_DN1 = T1 * D
SZ_QKV = QJ * 128
SZ_WO = QJ * D
SZ_RT = 10
WST = 1024


STARTS_AT_ONE = {
    "att1_down_done", "ctx_added", "ctx_done", "ffn0_down_done", "ffn0_times_gate", "ffn1_down_done",
    "ffn1_times_up", "norm_xl", "norm_xr_low", "out_scaled", "patches_high", "patches_low",
    "probs_turned", "tok_done", "u_done",
}


class Signal:

    def __init__(self, take, name, per=1, base=0):
        self.take, self.name, self.per, self.held, self.base = take, name, per, None, base

    @property
    def sem(self):
        if self.held is None:
            self.held = self.take(self.name)
        return self.held

    def at(self, c, k):
        return c * self.per + (self.base + k)

    def later(self, chunks):
        return Signal(lambda _: self.sem, self.name, self.per, self.base + chunks * self.per)


def tower(nc, a):
    with ExitStack() as ctx:
        body(nc, a, ctx)


def body(nc, a, ctx):
    def sb(name, shape, dt=F32):
        return ctx.enter_context(nc.sbuf_tensor(name, shape, dt))

    def sem(name):
        return ctx.enter_context(nc.semaphore(name))

    def sig(name, per=1):
        s = Signal(sem, name, per, int(name in STARTS_AT_ONE))
        if s.base:
            ones.append(s)
        return s

    ones = []

    def start_at_one(sp):
        while ones:
            sp.sem_inc(ones.pop().sem, 1)

    banks = ctx.enter_context(nc.psum_tensor("banks", [128, 8, 512], F32))

    const = sb("const", [128, C_ALL])
    selr = sb("selr", [SELW, NSEL], F32R)
    ident = const[:, C_ID:C_ID + 128]
    h = sb("h", [RT, NC * NP, D])
    xn = sb("xn", [RT, NP, D + DR])
    stats = sb("stats", [RT, NP, 6])
    mv = sb("mv", [RT, NP, 2])
    rstd = sb("rstd", [RT, NP])
    mhalf = sb("mhalf", [RT, NP])
    xh = sb("xh", [128, NT], F32R)
    xl = sb("xl", [128, NT], F32R)
    xr = sb("xr", [128, NT], F32R)
    rows = sb("rows", [RT, 6, D])
    cols = sb("cols", [128, 32])

    big = sb("big", [128, 4 * SZ_GU + 2 * SZ_DN1], F32R)
    mid = sb("mid", [128, 4 * SZ_QKV + 2 * SZ_WO], F32R)
    small = sb("small", [128, 4 * SZ_W1 + 4 * SZ_RT], F32R)
    w2s = sb("w2s", [96, E0])
    wstage = sb("wstage", [128, 2, WST])
    work = sb("work", [128, 7340])
    wx = 3 * QJ * NT
    zg = work[:, wx:wx + 2 * NT].rearrange("q (s t) -> q s t", s=2)
    acc_sb = work[:, wx + 2 * NT:wx + 4 * NT].rearrange("q (s t) -> q s t", s=2)
    zbuf = work[:, 0:2 * NT].rearrange("q (s t) -> q s t", s=2)
    g1 = work[0:96, 2 * NT:3 * NT]
    y0 = work[0:RT, 3 * NT:3 * NT + NP * D].rearrange("q (p f) -> q p f", p=NP)
    zh = sb("zh", [128, 2, NT], F32R)
    zl = sb("zl", [128, 2, NT], F32R)
    gT = sb("gT", [SELW, NT], F32R)
    gx = sb("gx", [RT, NP, SELW])
    rt = sb("rt", [RT, 8, NP, 10])
    ri = sb("ri", [RT, NP, 8], U32)

    def kparts(t, base, n):
        return [t[:, base + i * n:base + (i + 1) * n] for i in range(4)]

    def weave(eng, out, parts, cs, mov, start, stop):
        H, L, RH, RL = parts
        mh, ml, mr = mov
        seq = [(H, mh), (L, mh), (RH, mr), (RL, mr), (H, ml)]
        for i, (w, m) in enumerate(seq):
            ins = eng.matmul(out, w[:, cs], m, start=start and i == 0, stop=stop and i == len(seq) - 1)
        return ins

    dma_w = [sem("stage0_loaded"), sem("stage1_loaded")]
    hi_done, lo_done = sem("weights_high_done"), sem("weights_low_done")
    const_in = sem("const_in")

    class Piece:
        def __init__(self, src, n, high, low):
            self.src, self.n, self.high, self.low = src, n, high, low

    def pieces_of(src, n, tensor, base_h, base_l):
        out = []
        for o in range(0, n, WST):
            m = min(WST, n - o)
            out.append(Piece(src[:, o:o + m], m, tensor[:, base_h + o:base_h + o + m],
                             tensor[:, base_l + o:base_l + o + m]))
        return out

    def rem_piece(src, nt, tensor, base):
        v = tensor[:, base:base + nt * 128].rearrange("p (t s f) -> p t s f", s=2, f=DR)
        m = WST // DR
        return [Piece(src[:, o * DR:min(o + m, nt) * DR], (min(o + m, nt) - o) * DR,
                      v[:, o:min(o + m, nt), 0, :], v[:, o:min(o + m, nt), 1, :]) for o in range(0, nt, m)]

    up0_main = 4 * SZ_DN0
    up0_rem = up0_main + 2 * T0 * 128
    dn1_main = 4 * SZ_GU
    dn1_rem = dn1_main + 2 * T1 * 128
    wo_main = 4 * SZ_QKV
    wo_rem = wo_main + 2 * QJ * 128

    tok_p = pieces_of(a["w_tok"], SZ_TOK, mid, 0, SZ_TOK)
    atw_p = pieces_of(a["w_att0_k"], 128 + 128, mid, 2 * SZ_TOK, 2 * SZ_TOK + 256) + \
        pieces_of(a["w_att0_r"], 256, mid, 2 * SZ_TOK + 512, 2 * SZ_TOK + 768)
    val = mid[:, 2 * SZ_TOK + 1024:2 * SZ_TOK + 1024 + 4 * D]
    atv_p = pieces_of(a["w_val_k"], D, val, 0, D) + pieces_of(a["w_val_r"], D, val, 2 * D, 3 * D)
    ffn0_p = pieces_of(a["w_dn0_k"], SZ_DN0, big, 0, SZ_DN0) + \
        pieces_of(a["w_dn0_r"], SZ_DN0, big, 2 * SZ_DN0, 3 * SZ_DN0) + \
        pieces_of(a["w_up0_m"], T0 * 128, big, up0_main, up0_main + T0 * 128) + \
        rem_piece(a["w_up0_r"], T0, big, up0_rem) + \
        pieces_of(a["w_w1_k"], SZ_W1, small, 0, SZ_W1) + \
        pieces_of(a["w_w1_r"], SZ_W1, small, 2 * SZ_W1, 3 * SZ_W1)
    att1_p = pieces_of(a["w_qkv_k"], SZ_QKV, mid, 0, SZ_QKV) + \
        pieces_of(a["w_qkv_r"], SZ_QKV, mid, 2 * SZ_QKV, 3 * SZ_QKV) + \
        pieces_of(a["w_wo_m"], QJ * 128, mid, wo_main, wo_main + QJ * 128) + \
        rem_piece(a["w_wo_r"], QJ, mid, wo_rem)
    ffn1_p = pieces_of(a["w_gu_k"], SZ_GU, big, 0, SZ_GU) + \
        pieces_of(a["w_gu_r"], SZ_GU, big, 2 * SZ_GU, 3 * SZ_GU) + \
        pieces_of(a["w_dn1_m"], T1 * 128, big, dn1_main, dn1_main + T1 * 128) + \
        rem_piece(a["w_dn1_r"], T1, big, dn1_rem) + \
        pieces_of(a["w_rt_k"], SZ_RT, small, 4 * SZ_W1, 4 * SZ_W1 + SZ_RT) + \
        pieces_of(a["w_rt_r"], SZ_RT, small, 4 * SZ_W1 + 2 * SZ_RT, 4 * SZ_W1 + 3 * SZ_RT)
    order = [tok_p + atw_p + atv_p + ffn0_p, [], att1_p, ffn1_p]
    first = []
    n = 0
    for ps in order:
        first.append(n)
        n += len(ps)

    def load_pieces(eng, ps, n0):
        for i, p in enumerate(ps):
            n = n0 + i
            if n >= 2:
                eng.wait_ge(hi_done, n - 1)
                eng.wait_ge(lo_done, n - 1)
            eng.dma_start(wstage[:, n % 2, 0:p.n], p.src).then_inc(dma_w[n % 2], 16)

    def stage_like(n, p):
        v = wstage[:, n % 2, 0:p.n]
        return v.rearrange("p (t f) -> p t f", f=DR) if len(p.high.shape) == 3 else v

    def split_high(eng, ps, n0):
        for i, p in enumerate(ps):
            n = n0 + i
            eng.wait_ge(dma_w[n % 2], 16 * (n // 2 + 1))
            eng.activation(p.high, stage_like(n, p), ACT.Copy).then_inc(hi_done, 1)

    def split_low(eng, ps, n0):
        for i, p in enumerate(ps):
            n = n0 + i
            eng.wait_ge(hi_done, n + 1)
            eng.tensor_tensor(p.low, stage_like(n, p), p.high.bitcast(F32), ALU.subtract).then_inc(lo_done, 1)

    ROWS = ["pos", "bproj", "vb", "gamma", "beta", "bout"]
    row = {n: rows[:, i, :] for i, n in enumerate(ROWS)}

    mbd = work[:, 0:NH * 128].rearrange("p (h r) -> p h r", h=NH)
    hrt = work[:, 1536:1536 + NH * RK].rearrange("p (h r) -> p h r", h=NH)
    coret = work[:, 2304:2304 + RK]
    hmean = work[:, 2368:2368 + RK]
    ctmp = work[:, 2432:2432 + RK]
    b2r = sb("b2r", [RT, E0])
    sgb = sb("sgb", [RT, 1])
    tempc = sb("tempc", [NH, 1])
    cfix = sem("rows_base_in")
    setup = sem("setup_vec")
    setup_pool = sem("setup_pool")
    selr_done = sem("selectors_rounded")

    with nc.Block() as block:
        @block.sync
        def _(sp):
            sp.dma_start(const[:], a["const"]).then_inc(const_in, 16)
            sp.dma_start(hrt[0:64], a["hrt"]).then_inc(const_in, 16)
            sp.dma_start(hrt[64:128], a["hrt"]).then_inc(const_in, 16)
            sp.dma_start(coret[0:64], a["coret"]).then_inc(const_in, 16)
            sp.dma_start(coret[64:128], a["coret"]).then_inc(const_in, 16)
            sp.dma_start(work[0:SELW, 2500:2500 + NSEL], a["sel"]).then_inc(const_in, 16)
            sp.dma_start(cols[:], a["cols"]).then_inc(const_in, 16)
            sp.dma_start(w2s[:], a["w_w2"]).then_inc(const_in, 16)
            sp.dma_start(tempc[:], a["temp"]).then_inc(const_in, 16)
            sp.dma_start(rows[0:NTOK, 0, :], a["pos"]).then_inc(const_in, 16)
            sp.dma_start(rows[NTOK:RT, 0, :], a["pos"]).then_inc(const_in, 16)
            for i, n in ((2, "vb"), (3, "gamma"), (4, "beta"), (5, "bout")):
                sp.dma_start(rows[:, i, :], a[n].partition_broadcast(RT)).then_inc(const_in, 16)
            sp.dma_start(b2r[:], a["b2"].partition_broadcast(RT)).then_inc(const_in, 16)
            sp.dma_start(sgb[:], a["sgb"].partition_broadcast(RT)).then_inc(const_in, 16)
            sp.dma_start(rows[:, 1, :], a["bproj"].partition_broadcast(RT)).then_inc(cfix, 16)
            sp.wait_ge(cfix, 16)
            sp.dma_start(rows[0:1, 1, :], a["cls"]).then_inc(const_in, 16)
            sp.dma_start(rows[NTOK:NTOK + 1, 1, :], a["cls"]).then_inc(const_in, 16)

        NCONST = 16 * 19

        @block.vector
        def _(dve):
            dve.memset(mbd, 0.0).then_inc(setup, 1)
            dve.memset(mhalf[:], -0.5).then_inc(setup, 1)
            dve.memset(gx[:], 0.0).then_inc(setup, 1)
            dve.wait_ge(const_in, NCONST)
            dve.tensor_reduce(hmean, hrt.rearrange("p h r -> p r h"), X, ALU.add).then_inc(setup, 1)
            dve.wait_ge(setup, 4)
            dve.tensor_tensor(ctmp, coret, hmean, ALU.subtract).then_inc(setup, 1)
            dve.wait_ge(setup, 5)
            dve.tensor_scalar(ctmp, ctmp, 1.0 / NH, None, ALU.mult).then_inc(setup, 1)
            dve.wait_ge(setup, 6)
            dve.tensor_tensor(hrt, hrt, ctmp.unsqueeze(1).to_broadcast([128, NH, RK]), ALU.add).then_inc(setup, 1)
            dve.wait_ge(setup, 7)
            for i in range(2):
                s = slice(64 * i, 64 * i + 64)
                dve.tensor_scalar(mbd[s, :, s], hrt[s], RK ** -0.5, None, ALU.mult).then_inc(setup, 1)
            dve.tensor_tensor(row["pos"], row["pos"], row["bproj"], ALU.add).then_inc(setup, 1)
            dve.tensor_copy(selr[:], work[0:SELW, 2500:2500 + NSEL]).then_inc(selr_done, 1)

        @block.gpsimd
        def _(pool):
            pool.memset(gT[:].bitcast(F32), 0.0).then_inc(setup_pool, 1)

    def hc(c, p=None):
        if p is None:
            return h[:, bass.ds(c * NP, NP), :]
        return h[:, c * NP + p, :] if isinstance(c, int) else h[:, bass.ds(c * NP + p, 1), :].rearrange("a b d -> a (b d)")

    def prep_signals(tag):
        return dict(st=sig(tag + "_stats", NP), tw=sig(tag + "_normed_twice", 1), mv=sig(tag + "_meanvar", NP), ve=sig(tag + "_vareps", 1),
                    rs=sig(tag + "_rstd", 1), xn=sig(tag + "_normed", NP), tf=sig(tag + "_turned", 2),
                    xh=sig(tag + "_xh", 1), xl=sig(tag + "_xl", 1), rh=sig(tag + "_xr_high", 1),
                    rl=sig(tag + "_xr_low", 1))

    def plain(eng):
        eng.sem_inc(wait_taken, 1)

    wait_taken = sem("wait_taken")
    PREP = prep_signals("norm")

    def new_prep(block_no):
        return {k: s.later(NC * block_no) for k, s in PREP.items()}

    def prep_dve(dve, s, c, h_ready, xn_free, split=True):
        for p in range(NP):
            dve.bn_stats(stats[:, p, :], hc(c, p)).then_inc(s["st"].sem, 1)
        for p in range(NP):
            dve.wait_ge(s["st"].sem, s["st"].at(c, p + 1))
            plain(dve)
            dve.bn_aggr(mv[:, p, :], stats[:, p, :]).then_inc(s["mv"].sem, 1)
        dve.wait_ge(s["mv"].sem, s["mv"].at(c, NP))
        dve.tensor_scalar(rstd[:], mv[:, :, 1], EPS, None, ALU.add).then_inc(s["ve"].sem, 1)
        dve.wait_ge(s["rs"].sem, s["rs"].at(c, 1))
        for p in range(NP):
            dve.tensor_scalar(xn[:, p, 0:D], hc(c, p), mv[:, p, 0:1], rstd[:, p:p + 1],
                              ALU.subtract, ALU.mult).then_inc(s["xn"].sem, 1)

    def prep_pool(pool, s, c):
        pool.wait_ge(s["ve"].sem, s["ve"].at(c, 1))
        pool.tensor_tensor(rstd[:], rstd[:], mhalf[:], ALU.pow).then_inc(s["rs"].sem, 1)

    def prep_pe(pe, s, c, b0, b1):
        for p in range(NP):
            pe.wait_ge(s["xn"].sem, s["xn"].at(c, p + 1))
            m0 = pe.transpose(banks[:, b0, p * RT:(p + 1) * RT], xn[:, p, 0:128], ident[0:RT, 0:RT])
        m0.then_inc(s["tf"].sem, 1)
        pe.wait_ge(s["tw"].sem, s["tw"].at(c, 1))
        for p in range(NP):
            m1 = pe.transpose(banks[:, b1, p * RT:(p + 1) * RT], xn[:, p, 128:D + DR], ident[0:RT, 0:RT])
        m1.then_inc(s["tf"].sem, 1)

    def halves(v):
        return v.rearrange("q (p s n) -> q s p n", p=NP, s=2)

    def prep_split_act(act, s, c, b0, b1, by_half=False):
        f = halves if by_half else (lambda v: v)
        g = (lambda v: v.rearrange("q (s p n) -> q s p n", p=NP, s=2)) if by_half else (lambda v: v)
        act.wait_ge(s["xn"].sem, s["xn"].at(c, NP))
        act.activation(xn[:, :, D:D + DR], xn[:, :, 128:D], ACT.Copy).then_inc(s["tw"].sem, 1)
        act.wait_ge(s["tf"].sem, s["tf"].at(c, 1))
        act.activation(g(xh[:]), f(banks[:, b0, 0:NT]), ACT.Copy).then_inc(s["xh"].sem, 1)
        act.wait_ge(s["tf"].sem, s["tf"].at(c, 2))
        act.activation(g(xr[:]), f(banks[:, b1, 0:NT]), ACT.Copy).then_inc(s["rh"].sem, 1)

    def prep_split_dve(dve, s, c, b0, b1, by_half=False):
        f = halves if by_half else (lambda v: v)
        g = (lambda v: v.rearrange("q (s p n) -> q s p n", p=NP, s=2)) if by_half else (lambda v: v)
        dve.wait_ge(s["xh"].sem, s["xh"].at(c, 1))
        dve.tensor_tensor(g(xl[:]), f(banks[:, b0, 0:NT]), g(xh[:].bitcast(F32)), ALU.subtract).then_inc(s["xl"].sem, 1)
        dve.wait_ge(s["rh"].sem, s["rh"].at(c, 1))
        dve.tensor_tensor(g(xr[64:128]), f(banks[64:128, b1, 0:NT]), g(xr[64:128].bitcast(F32)),
                          ALU.subtract).then_inc(s["rl"].sem, 1)

    def prep_wait(pe, s, c):
        pe.wait_ge(s["xh"].sem, s["xh"].at(c, 1))
        pe.wait_ge(s["xl"].sem, s["xl"].at(c, 1))
        pe.wait_ge(s["rh"].sem, s["rh"].at(c, 1))
        pe.wait_ge(s["rl"].sem, s["rl"].at(c, 1))

    wt_h, wt_l = mid[:, 0:SZ_TOK], mid[:, SZ_TOK:2 * SZ_TOK]
    bw = kparts(mid, 2 * SZ_TOK, 256)
    vw = kparts(val, 0, D)

    xs = work[:, 1536:1536 + KP * NT]
    o = 1536 + KP * NT
    lat = work[:, o:o + 148]
    lbd = work[:, o + 148:o + 148 + NT].rearrange("q (p t) -> q p t", p=NP)
    sx = work[:, o + 444:o + 444 + 888].rearrange("q (s f) -> q s f", s=2)
    pts = work[:, o + 1332:o + 1332 + NT].rearrange("q (g t) -> q g t", g=NG)
    vbd = work[:, o + 1628:o + 1628 + 384]
    uc = work[:, o + 2012:o + 2012 + D]
    sm = work[:, o + 2204:o + 2204 + 4 * NH].rearrange("q (s f) -> q s f", s=4)
    bo = up0_rem + T0 * 128
    xsh, xsl = big[:, bo:bo + KP * NT], big[:, bo + KP * NT:bo + 2 * KP * NT]
    uh = work[:, o + 2252:o + 2252 + KP * NT].rearrange("q (p h n) -> q p h n", p=NP, h=NH)

    xrep = big[:, bo + 2 * KP * NT:bo + 2 * KP * NT + 3 * IMG * VR].rearrange("q (k i m) -> q k i m", k=3, i=IMG)

    def repeat(eng, k, src):
        v = src[:].bitcast(F32).rearrange("q (i n) -> q i n", i=IMG).unsqueeze(2).to_broadcast([128, IMG, GH, NTOK])
        return v, xrep[:, k].rearrange("q i (r n) -> q i r n", r=GH)

    rep_done = [sig(n + "_repeated") for n in ("xh", "xl", "xr")]
    P1 = new_prep(0)
    x_in, x_hi, x_lo = sem("patches_in"), sig("patches_high"), sig("patches_low")
    tok_done, h0_done = sig("tok_done", 2), sig("tok_added", 2)
    lat_done, lat_ev = sig("latent_done"), sig("latent_out", 3)
    lbd_zero = sem("latent_blocks_zero")
    u_done, u_ev = sig("u_done", 4), sig("u_out", 4)
    s_done, mx_done, sub_done = sig("scores_done", NP), sig("score_max", NP), sig("scores_less_max", NP)
    e_done, sum_done, rec_done = sig("exp_done", NP), sig("prob_sum", NP), sig("prob_recip", NP)
    pt_done, pt_ev = sig("probs_turned", NP), sig("probs_turned_out", NP)
    v_done, v_ev = sig("values_done", NP), sig("values_out", NP)
    c_done, c_a, c_b, c_n, c_h = (sig("ctx_done", NP), sig("ctx_first_image", NP), sig("ctx_both", NP),
                                  sig("ctx_normed", NP), sig("ctx_added", NP))
    vb_done = sig("value_bias_added")

    with nc.Block() as block:
        @block.sync
        def _(sp):
            start_at_one(sp)
            load_pieces(sp, order[0][:len(tok_p)], 0)
            load_pieces(sp, order[0][len(tok_p):], len(tok_p))

        @block.gpsimd
        def _(pool):
            with pool.Fori(0, NC) as c:
                pool.wait_ge(x_hi.sem, x_hi.at(c, 0))
                pool.wait_ge(x_lo.sem, x_lo.at(c, 0))
                pool.dma_start(xs, a["patches"][bass.ds(c * 128, 128), :]).then_inc(x_in, 16)
                prep_pool(pool, P1, c)
                pool.wait_ge(P1["xn"].sem, P1["xn"].at(c, NP))
                pool.tensor_tensor(hc(c), hc(c), row["vb"].unsqueeze(1).to_broadcast([RT, NP, D]),
                                   ALU.add).then_inc(vb_done.sem, 1)
                src, dst = repeat(pool, 2, xr)
                pool.wait_ge(P1["rh"].sem, P1["rh"].at(c, 1))
                pool.wait_ge(P1["rl"].sem, P1["rl"].at(c, 1))
                plain(pool)
                pool.tensor_copy(dst, src).then_inc(rep_done[2].sem, 1)

        @block.scalar
        def _(act):
            split_high(act, order[0], 0)
            with act.Fori(0, NC) as c:
                act.wait_ge(x_in, c * 16 + 16)
                act.wait_ge(tok_done.sem, tok_done.at(c, 0))
                act.activation(xsh, xs, ACT.Copy).then_inc(x_hi.sem, 1)
                act.wait_ge(u_done.sem, u_done.at(c, 0))
                prep_split_act(act, P1, c, 0, 1, True)
                src, dst = repeat(act, 0, xh)
                act.wait_ge(P1["xh"].sem, P1["xh"].at(c, 1))
                act.activation(dst, src, ACT.Copy).then_inc(rep_done[0].sem, 1)
                act.wait_ge(lat_done.sem, lat_done.at(c, 1))
                act.wait_ge(c_done.sem, c_done.at(c, 0))
                act.activation(lat, banks[:, 2, 0:148], ACT.Copy).then_inc(lat_ev.sem, 1)
                for i in range(2):
                    s = slice(64 * i, 64 * i + 64)
                    if i == 0:
                        act.wait_ge(lbd_zero, 1)
                    act.activation(lbd[s, :, NTOK * i:NTOK * (i + 1)],
                                   banks[s, 2, 0:148].rearrange("q (p n) -> q p n", p=NP),
                                   ACT.Copy).then_inc(lat_ev.sem, 1)
                for k in range(4):
                    act.wait_ge(u_done.sem, u_done.at(c, k + 1))
                    act.activation(uh[:, :, GH * k:GH * (k + 1), :],
                                   banks[:, 4 + k, 0:444].rearrange("q (h p n) -> q p h n", h=GH, p=NP),
                                   ACT.Copy).then_inc(u_ev.sem, 1)
                for p in range(NP):
                    act.wait_ge(sub_done.sem, sub_done.at(c, p + 1))
                    act.activation(sx[0:RT, p % 2], sx[0:RT, p % 2], ACT.Exp).then_inc(e_done.sem, 1)
                    act.wait_ge(pt_done.sem, pt_done.at(c, p + 1))
                    if p:
                        act.wait_ge(c_done.sem, c_done.at(c, p))
                    act.activation(pts[0:VR], banks[0:VR, 6, 0:NT].rearrange("q (g t) -> q g t", g=NG),
                                   ACT.Copy).then_inc(pt_ev.sem, 1)
                    act.wait_ge(c_done.sem, c_done.at(c, p + 1))
                    act.wait_ge(c_h.sem, c_h.at(c, p))
                    act.activation(uc[0:RT], banks[0:RT, 7, 0:D], ACT.Copy,
                                   scale=const[0:RT, C_MAB:C_MAB + 1]).then_inc(c_a.sem, 1)

        @block.vector
        def _(dve):
            dve.memset(lbd, 0.0).then_inc(lbd_zero, 1)
            split_low(dve, order[0], 0)
            with dve.Fori(0, NC) as c:
                dve.wait_ge(x_hi.sem, x_hi.at(c, 1))
                dve.tensor_tensor(xsl, xs, xsh.bitcast(F32), ALU.subtract).then_inc(x_lo.sem, 1)
                for i in range(2):
                    dve.wait_ge(tok_done.sem, tok_done.at(c, i + 1))
                    dve.tensor_tensor(h[:, bass.ds(c * NP + 2 * i, 2), :],
                                      banks[0:RT, i, 0:2 * D].rearrange("q (p f) -> q p f", p=2),
                                      row["pos"].unsqueeze(1).to_broadcast([RT, 2, D]),
                                      ALU.add).then_inc(h0_done.sem, 1)
                dve.wait_ge(h0_done.sem, h0_done.at(c, 2))
                plain(dve)
                prep_dve(dve, P1, c, None, None)
                prep_split_dve(dve, P1, c, 0, 1, True)
                src, dst = repeat(dve, 1, xl)
                dve.wait_ge(P1["xl"].sem, P1["xl"].at(c, 1))
                dve.tensor_copy(dst, src).then_inc(rep_done[1].sem, 1)

                def values(p):
                    dve.wait_ge(v_done.sem, v_done.at(c, p + 1))
                    if p:
                        dve.wait_ge(c_done.sem, c_done.at(c, p))
                    dve.tensor_tensor(vbd[0:VR].rearrange("q (g h d) -> q g h d", h=GH, d=HD),
                                      banks[0:VR, 3, 0:2 * D].rearrange("q (g h d) -> q g h d", h=GH, d=HD),
                                      const[0:VR, C_VM:C_VM + GH].unsqueeze(1).unsqueeze(3).to_broadcast([VR, 2 * NG, GH, HD]),
                                      ALU.mult).then_inc(v_ev.sem, 1)

                for p in range(NP):
                    S = banks[0:RT, 4 + p % 2, 0:444].rearrange("q (h m) -> q h m", h=NH)
                    dve.wait_ge(s_done.sem, s_done.at(c, p + 1))
                    dve.tensor_reduce(sm[0:RT, 0], S, X, ALU.max).then_inc(mx_done.sem, 1)
                    dve.wait_ge(mx_done.sem, mx_done.at(c, p + 1))
                    sxp = sx[0:RT, p % 2].rearrange("q (h m) -> q h m", h=NH)
                    dve.wait_ge(pt_done.sem, pt_done.at(c, max(p - 1, 0)))
                    dve.tensor_tensor(sxp, S, sm[0:RT, 0].unsqueeze(2).to_broadcast([RT, NH, NTOK]),
                                      ALU.subtract).then_inc(sub_done.sem, 1)
                    values(p)
                    dve.wait_ge(e_done.sem, e_done.at(c, p + 1))
                    dve.tensor_reduce(sm[0:RT, 1], sxp, X, ALU.add).then_inc(sum_done.sem, 1)
                    dve.wait_ge(sum_done.sem, sum_done.at(c, p + 1))
                    dve.reciprocal(sm[0:RT, 2], sm[0:RT, 1]).then_inc(rec_done.sem, 1)
                    dve.wait_ge(c_a.sem, c_a.at(c, p + 1))
                    dve.scalar_tensor_tensor(uc[0:RT], banks[0:RT, 7, D:2 * D], const[0:RT, C_MAB + 1:C_MAB + 2],
                                             uc[0:RT], ALU.mult, ALU.add).then_inc(c_b.sem, 1)
                    dve.wait_ge(c_b.sem, c_b.at(c, p + 1))
                    dve.wait_ge(rec_done.sem, rec_done.at(c, p + 1))
                    u3 = uc[0:RT].rearrange("q (h d) -> q h d", h=NH)
                    dve.tensor_tensor(u3, u3, sm[0:RT, 2].unsqueeze(2).to_broadcast([RT, NH, HD]),
                                      ALU.mult).then_inc(c_n.sem, 1)
                    dve.wait_ge(c_n.sem, c_n.at(c, p + 1))
                    dve.wait_ge(vb_done.sem, vb_done.at(c, 1))
                    dve.tensor_tensor(hc(c, p), hc(c, p), uc[0:RT], ALU.add).then_inc(c_h.sem, 1)

        @block.tensor
        def _(pe):
            pe.wait_ge(lo_done, len(order[0]) if False else len(tok_p))
            with pe.Fori(0, NC) as c:
                pe.wait_ge(P1["xl"].sem, P1["xl"].at(c, 0))
                pe.wait_ge(P1["rl"].sem, P1["rl"].at(c, 0))
                for p in range(NP):
                    out = banks[0:RT, p // 2, D * (p % 2):D * (p % 2) + D]
                    if p == 0:
                        pe.wait_ge(x_hi.sem, x_hi.at(c, 1))
                        pe.wait_ge(x_lo.sem, x_lo.at(c, 1))
                    for k in range(KP):
                        s = slice(k * NT + p * RT, k * NT + (p + 1) * RT)
                        w = slice(k * D, (k + 1) * D)
                        pe.matmul(out, xsh[:, s], wt_h[:, w], start=(k == 0), stop=False)
                        pe.matmul(out, xsh[:, s], wt_l[:, w], start=False, stop=False)
                        mm = pe.matmul(out, xsl[:, s], wt_h[:, w], start=False, stop=(k == KP - 1))
                    if p % 2:
                        mm.then_inc(tok_done.sem, 1)
                pe.wait_ge(h0_done.sem, h0_done.at(c, 2))
                prep_pe(pe, P1, c, 0, 1)
                prep_wait(pe, P1, c)
                pe.wait_ge(lo_done, len(tok_p) + len(atw_p) + len(atv_p))
                n2 = NP * NTOK
                for i in range(2):
                    t = slice(n2 * i, n2 * (i + 1))
                    mm = weave(pe, banks[:, 2, 0:n2], bw, slice(128 * i, 128 * i + 128),
                               (xh[:, t], xl[:, t], xr[:, t]), i == 0, i == 1)
                mm.then_inc(lat_done.sem, 1)
                pe.wait_ge(lat_ev.sem, lat_ev.at(c, 3))
                pe.wait_ge(c_h.sem, c_h.at(c, 0))
                for hd in range(NH):
                    mm = pe.matmul(banks[:, 4 + hd // GH, 148 * (hd % GH):148 * (hd % GH) + 148],
                                   mbd[:, hd, :], lat, start=True, stop=True)
                    if hd % GH == GH - 1:
                        mm.then_inc(u_done.sem, 1)

                def scores(p):
                    if p >= 2:
                        pe.wait_ge(sub_done.sem, sub_done.at(c, p - 1))
                    pe.matmul(banks[0:RT, 4 + p % 2, 0:444], lbd[:, p, :], uh[:, p],
                              start=True, stop=True).then_inc(s_done.sem, 1)

                def values(p):
                    if p:
                        pe.wait_ge(v_ev.sem, v_ev.at(c, p))
                    for i in range(2):
                        rep = [xrep[:, k, NP * i + p, :] for k in range(3)]
                        H, L, RH, RL = vw
                        seq = [(rep[0], H), (rep[0], L), (rep[2], RH), (rep[2], RL), (rep[1], H)]
                        for k, (st, m) in enumerate(seq):
                            mm = pe.matmul(banks[0:VR, 3, D * i:D * i + D], st, m, start=(k == 0), stop=(k == 4))
                    mm.then_inc(v_done.sem, 1)

                pe.wait_ge(u_ev.sem, u_ev.at(c, 4))
                scores(0)
                for r in rep_done:
                    pe.wait_ge(r.sem, r.at(c, 1))
                values(0)
                for p in range(NP):
                    if p + 1 < NP:
                        scores(p + 1)
                    pe.wait_ge(e_done.sem, e_done.at(c, p + 1))
                    if p:
                        pe.wait_ge(pt_ev.sem, pt_ev.at(c, p))
                    for g in range(NG):
                        mm = pe.transpose(banks[0:VR, 6, RT * g:RT * g + RT],
                                          sx[0:RT, p % 2, VR * g:VR * (g + 1)], ident[0:RT, 0:RT])
                    mm.then_inc(pt_done.sem, 1)
                    pe.wait_ge(pt_ev.sem, pt_ev.at(c, p + 1))
                    pe.wait_ge(v_ev.sem, v_ev.at(c, p + 1))
                    if p:
                        pe.wait_ge(c_b.sem, c_b.at(c, p))
                    out = banks[0:RT, 7, 0:2 * D].rearrange("q (i g f) -> q i g f", i=2, g=NG)
                    vv = vbd[0:VR].rearrange("q (i g f) -> q i g f", i=2, g=NG)
                    for g in range(NG):
                        mm = pe.matmul(out[:, :, g, :], pts[0:VR, g, :], vv[:, :, g, :], start=True, stop=True)
                    mm.then_inc(c_done.sem, 1)
                    if p + 1 < NP:
                        values(p + 1)

    def gates_dve(dve, S, c, bank, first_layer):
        n = NP * 8
        lg, ex, pr, tp = (rt[:, i, :, 0:8] for i in range(4))
        m0, m1 = rt[:, 4, :, 0:8], rt[:, 5, :, 0:8]
        idf = rt[:, 6, :, 0:2]
        one = [rt[:, 7, :, i:i + 1] for i in range(6)]
        count = [0]

        def link(ins):
            count[0] += 1
            ins.then_inc(S["gv"].sem, 1)
            dve.wait_ge(S["gv"].sem, S["gv"].at(c, count[0]))

        def w8(v):
            return v.to_broadcast([RT, NP, 8])
        io = const[0:RT, C_IOTA:C_IOTA + 8].unsqueeze(1).to_broadcast([RT, NP, 8])
        lp = banks[0:RT, bank, 0:NP * 10].rearrange("q (p e) -> q p e", p=NP)
        dve.wait_ge(S["lg"].sem, S["lg"].at(c, 1))
        if first_layer:
            link(dve.tensor_tensor(lg, lp[:, :, 0:8], b2r[:].unsqueeze(1).to_broadcast([RT, NP, 8]), ALU.add))
        else:
            link(dve.tensor_copy(lg, lp[:, :, 0:8]))
            link(dve.tensor_scalar(one[4], lp[:, :, 8:9], sgb[:, 0:1], -1.0, ALU.add, ALU.mult))
        plain(dve)
        for p in range(NP):
            dve.max(tp[:, p, :], lg[:, p, :]).then_inc(S["gv"].sem, 1)
            count[0] += 1
        dve.wait_ge(S["gv"].sem, S["gv"].at(c, count[0]))
        plain(dve)
        for p in range(NP):
            dve.max_index(ri[:, p, :], tp[:, p, :], lg[:, p, :]).then_inc(S["gv"].sem, 1)
            count[0] += 1
        dve.tensor_tensor(ex, lg, w8(tp[:, :, 0:1]), ALU.subtract).then_inc(S["gs"].sem, 1)
        dve.wait_ge(S["gv"].sem, S["gv"].at(c, count[0]))
        link(dve.tensor_copy(idf, ri[:, :, 0:2]))
        link(dve.tensor_tensor(m0, io, w8(idf[:, :, 0:1]), ALU.is_equal))
        link(dve.tensor_tensor(m1, io, w8(idf[:, :, 1:2]), ALU.is_equal))
        link(dve.tensor_tensor(m0, m0, m1, ALU.add))
        dve.wait_ge(S["ge"].sem, S["ge"].at(c, 1))
        link(dve.tensor_reduce(one[0], ex, X, ALU.add))
        link(dve.reciprocal(one[1], one[0]))
        link(dve.tensor_tensor(pr, ex, w8(one[1]), ALU.mult))
        link(dve.tensor_tensor(pr, pr, m0, ALU.mult))
        link(dve.tensor_reduce(one[2], pr, X, ALU.add))
        if first_layer:
            link(dve.tensor_scalar(one[2], one[2], 1e-8, None, ALU.add))
        link(dve.reciprocal(one[3], one[2]))
        if not first_layer:
            link(dve.tensor_scalar(one[4], one[4], 1.0, None, ALU.add))
            link(dve.reciprocal(one[5], one[4]))
            link(dve.tensor_scalar(one[4], one[5], -1.0, 1.0, ALU.mult, ALU.add))
            link(dve.tensor_tensor(one[3], one[3], one[4], ALU.mult))
        for i in range(2):
            dve.tensor_tensor(gx[:, :, 32 * i:32 * i + 8], pr, w8(one[3]), ALU.mult).then_inc(S["gx"].sem, 1)
            if not first_layer:
                dve.tensor_copy(gx[:, :, 32 * i + 8:32 * i + 9], one[5]).then_inc(S["gx"].sem, 1)
        assert count[0] == S["gv"].per, count[0]

    def gates_act(act, S, c, first_layer):
        act.wait_ge(S["gs"].sem, S["gs"].at(c, 1))
        if not first_layer:
            act.activation(rt[:, 7, :, 4:5], rt[:, 7, :, 4:5], ACT.Exp).then_inc(S["ga"].sem, 1)
            act.wait_ge(S["ga"].sem, S["ga"].at(c, 1))
        act.activation(rt[:, 1, :, 0:8], rt[:, 1, :, 0:8], ACT.Exp).then_inc(S["ge"].sem, 1)

    def gates_pe(pe, S, c, bank):
        pe.wait_ge(S["gx"].sem, S["gx"].at(c, S["gx"].per))
        plain(pe)
        for p in range(NP):
            mm = pe.transpose(banks[0:SELW, bank, RT * p:RT * p + RT], gx[:, p, :], ident[0:RT, 0:RT])
        mm.then_inc(S["gt"].sem, 1)

    def gates_out(dve, S, c, bank):
        dve.wait_ge(S["gt"].sem, S["gt"].at(c, 1))
        dve.tensor_copy(gT[:], banks[0:SELW, bank, 0:NT]).then_inc(S["gh"].sem, 1)
        dve.wait_ge(S["gh"].sem, S["gh"].at(c, 1))
        dve.tensor_tensor(gT[32:64], banks[32:64, bank, 0:NT], gT[32:64].bitcast(F32),
                          ALU.subtract).then_inc(S["gl"].sem, 1)

    def post_act(act, S, c):
        act.wait_ge(S["ac"].sem, S["ac"].at(c, 1))
        for i in range(2):
            act.activation(acc_sb[:, i, :], banks[:, i, 0:NT], ACT.Copy).then_inc(S["ae"].sem, 1)

    def post_pe(pe, S, c, bank):
        pe.wait_ge(S["ae"].sem, S["ae"].at(c, 2))
        for q in range(2):
            for p in (2 * q, 2 * q + 1):
                t = slice(RT * p, RT * p + RT)
                o = D * (p % 2)
                pe.transpose(banks[0:RT, bank + q, o:o + 128], acc_sb[:, 0, t], ident)
                mm = pe.matmul(banks[0:RT, bank + q, o + 128:o + D], acc_sb[:, 1, t],
                               const[:, C_II:C_II + DR], start=True, stop=True)
            mm.then_inc(S["po"].sem, 1)

    def new_mix(tag, nt, gv, gxn):
        return dict(lg=sig(tag + "_logits"), gv=sig(tag + "_gate_steps", gv), gs=sig(tag + "_logits_less_max"),
                    ge=sig(tag + "_gate_exp"), ga=sig(tag + "_alpha_exp"), gx=sig(tag + "_gates", gxn),
                    gt=sig(tag + "_gates_turned"), gh=sig(tag + "_gates_high"), gl=sig(tag + "_gates_low"),
                    hd=sig(tag + "_hidden", nt), ac=sig(tag + "_acc_done"), ae=sig(tag + "_acc_out", 2),
                    po=sig(tag + "_acc_turned", 2), ph=sig(tag + "_added", 2),
                    z=sig(tag + "_activated", nt), u=sig(tag + "_times_up", nt), g=sig(tag + "_times_gate", nt),
                    zh=sig(tag + "_z_high", nt), zl=sig(tag + "_z_low", nt), dn=sig(tag + "_down_done", nt),
                    gb=sig(tag + "_gate_spread", nt))

    def down_pe(pe, S, c, t, nt, main_h, main_l, rem):
        zz = t % 2
        m, r = slice(128 * t, 128 * t + 128), slice(128 * t, 128 * t + 128)
        pe.wait_ge(S["zh"].sem, S["zh"].at(c, t + 1))
        pe.matmul(banks[:, 0, 0:NT], main_h[:, m], zh[:, zz], start=(t == 0), stop=False)
        pe.matmul(banks[:, 0, 0:NT], main_l[:, m], zh[:, zz], start=False, stop=False)
        pe.matmul(banks[:, 1, 0:NT], rem[:, r], zh[:, zz], start=(t == 0), stop=False)
        pe.wait_ge(S["zl"].sem, S["zl"].at(c, t + 1))
        pe.matmul(banks[:, 0, 0:NT], main_h[:, m], zl[:, zz], start=False, stop=(t == nt - 1))
        mm = pe.matmul(banks[:, 1, 0:NT], rem[:, r], zl[:, zz], start=False, stop=(t == nt - 1))
        mm.then_inc(S["dn"].sem, 1)
        return mm

    MISC, GB = 7, 6
    P2 = new_prep(1)
    M0 = new_mix("ffn0", T0, 20, 2)
    r1_done, r1_act = sig("router_hidden"), sig("router_gelu")
    fst, fmv, fve, frs, fx, fg = (sig("out_stats", NP), sig("out_meanvar", NP), sig("out_vareps"), sig("out_rstd"),
                                  sig("out_normed", NP), sig("out_gamma"))
    fbeta = sig("beta_added")
    fadd = sig("moe_added", 2)
    fh = sig("ffn0_residual")

    with nc.Block() as block:
        @block.sync
        def _(sp):
            start_at_one(sp)

        @block.gpsimd
        def _(pool):
            with pool.Fori(0, NC) as c:
                prep_pool(pool, P2, c)
                pool.wait_ge(P2["xn"].sem, P2["xn"].at(c, NP))
                pool.tensor_tensor(hc(c), hc(c), row["beta"].unsqueeze(1).to_broadcast([RT, NP, D]),
                                   ALU.add).then_inc(fbeta.sem, 1)
                pool.wait_ge(fve.sem, fve.at(c, 1))
                pool.tensor_tensor(rstd[:], rstd[:], mhalf[:], ALU.pow).then_inc(frs.sem, 1)

        @block.scalar
        def _(act):
            with act.Fori(0, NC) as c:
                prep_split_act(act, P2, c, 2, 3)
                act.wait_ge(r1_done.sem, r1_done.at(c, 1))
                act.activation(g1, banks[0:96, MISC, 0:NT], ACT.Gelu, bias=cols[0:96, 16:17]).then_inc(r1_act.sem, 1)
                gates_act(act, M0, c, True)
                for t in range(T0):
                    act.wait_ge(M0["hd"].sem, M0["hd"].at(c, t + 1))
                    act.wait_ge(M0["g"].sem, M0["g"].at(c, max(t - 1, 0)))
                    act.activation(zbuf[:, t % 2], banks[:, 2 + t % 3, 0:NT], ACT.Gelu,
                                   bias=cols[:, t:t + 1]).then_inc(M0["z"].sem, 1)
                post_act(act, M0, c)

        @block.vector
        def _(dve):
            with dve.Fori(0, NC) as c:
                prep_dve(dve, P2, c, None, None)
                prep_split_dve(dve, P2, c, 2, 3)
                gates_dve(dve, M0, c, MISC, True)
                gates_out(dve, M0, c, MISC)
                for t in range(T0):
                    zz = t % 2
                    dve.wait_ge(M0["z"].sem, M0["z"].at(c, t + 1))
                    dve.wait_ge(M0["gb"].sem, M0["gb"].at(c, t + 1))
                    dve.tensor_tensor(zg[:, zz], zbuf[:, zz], banks[:, GB, 0:NT], ALU.mult).then_inc(M0["g"].sem, 1)
                    dve.wait_ge(M0["g"].sem, M0["g"].at(c, t + 1))
                    dve.wait_ge(M0["dn"].sem, M0["dn"].at(c, max(t - 1, 0)))
                    dve.tensor_copy(zh[:, zz], zg[:, zz]).then_inc(M0["zh"].sem, 1)
                    dve.wait_ge(M0["zh"].sem, M0["zh"].at(c, t + 1))
                    dve.tensor_tensor(zl[:, zz], zg[:, zz], zh[:, zz].bitcast(F32), ALU.subtract).then_inc(M0["zl"].sem, 1)
                for q in range(2):
                    dve.wait_ge(M0["po"].sem, M0["po"].at(c, q + 1))
                    dve.tensor_tensor(y0[:, 2 * q:2 * q + 2, :], banks[0:RT, 2 + q, 0:2 * D].rearrange("q (p f) -> q p f", p=2),
                                      xn[:, 2 * q:2 * q + 2, 0:D], ALU.add).then_inc(fadd.sem, 1)
                for p in range(NP):
                    dve.wait_ge(fadd.sem, fadd.at(c, p // 2 + 1))
                    dve.bn_stats(stats[:, p, :], y0[:, p, :]).then_inc(fst.sem, 1)
                for p in range(NP):
                    dve.wait_ge(fst.sem, fst.at(c, p + 1))
                    plain(dve)
                    dve.bn_aggr(mv[:, p, :], stats[:, p, :]).then_inc(fmv.sem, 1)
                dve.wait_ge(fmv.sem, fmv.at(c, NP))
                dve.tensor_scalar(rstd[:], mv[:, :, 1], EPS, None, ALU.add).then_inc(fve.sem, 1)
                dve.wait_ge(frs.sem, frs.at(c, 1))
                for p in range(NP):
                    dve.tensor_scalar(y0[:, p, :], y0[:, p, :], mv[:, p, 0:1], rstd[:, p:p + 1],
                                      ALU.subtract, ALU.mult).then_inc(fx.sem, 1)
                dve.wait_ge(fx.sem, fx.at(c, NP))
                dve.tensor_tensor(y0, y0, row["gamma"].unsqueeze(1).to_broadcast([RT, NP, D]), ALU.mult).then_inc(fg.sem, 1)
                dve.wait_ge(fg.sem, fg.at(c, 1))
                dve.wait_ge(fbeta.sem, fbeta.at(c, 1))
                dve.tensor_tensor(hc(c), hc(c), y0, ALU.add).then_inc(fh.sem, 1)

        @block.tensor
        def _(pe):
            w1 = kparts(small, 0, SZ_W1)
            dn = kparts(big, 0, SZ_DN0)
            um, ul = big[:, up0_main:up0_main + T0 * 128], big[:, up0_main + T0 * 128:up0_main + 2 * T0 * 128]
            ur = big[:, up0_rem:up0_rem + T0 * 128]
            with pe.Fori(0, NC) as c:
                prep_pe(pe, P2, c, 2, 3)
                prep_wait(pe, P2, c)
                mov = (xh[:], xl[:], xr[:])
                weave(pe, banks[0:96, MISC, 0:NT], w1, slice(0, 96), mov, True, True).then_inc(r1_done.sem, 1)

                def hidden(t):
                    if t >= 3:
                        pe.wait_ge(M0["z"].sem, M0["z"].at(c, t - 2))
                    weave(pe, banks[:, 2 + t % 3, 0:NT], dn, slice(128 * t, 128 * t + 128), mov,
                          True, True).then_inc(M0["hd"].sem, 1)

                hidden(0)
                hidden(1)
                pe.wait_ge(r1_act.sem, r1_act.at(c, 1))
                for p in range(NP):
                    mm = pe.matmul(banks[0:RT, MISC, 10 * p:10 * p + 8], g1[:, RT * p:RT * p + RT], w2s[:],
                                   start=True, stop=True)
                mm.then_inc(M0["lg"].sem, 1)
                gates_pe(pe, M0, c, MISC)
                pe.wait_ge(M0["gl"].sem, M0["gl"].at(c, 1))

                def spread(t):
                    e = t // 2
                    if t:
                        pe.wait_ge(M0["g"].sem, M0["g"].at(c, t))
                    pe.matmul(banks[:, GB, 0:NT], selr[:, 128 * e:128 * e + 128], gT[:],
                              start=True, stop=True).then_inc(M0["gb"].sem, 1)

                spread(0)
                for t in range(T0):
                    if t + 2 < T0:
                        hidden(t + 2)
                    mm = down_pe(pe, M0, c, t, T0, um, ul, ur)
                    if t + 1 < T0:
                        spread(t + 1)
                pe.wait_ge(M0["dn"].sem, M0["dn"].at(c, T0))
                pe.sem_inc(M0["ac"].sem, 1)
                post_pe(pe, M0, c, 2)

    P3 = new_prep(2)
    S3 = new_mix("att1", QJ, 1, 1)
    ws = work[:, 0:QJ * NT].rearrange("q (j t) -> q j t", j=QJ)
    sq = work[:, QJ * NT:2 * QJ * NT].rearrange("q (j t) -> q j t", j=QJ)
    wn = work[:, 2 * QJ * NT:3 * QJ * NT].rearrange("q (j t) -> q j t", j=QJ)
    o1 = sq
    n2 = sb("n2", [128, QJ, IMG])
    dt_ = sb("dots", [128, QJ, IMG])
    pq = sb("pq", [NH, NT + IMG])
    hs = sb("hs", [NH, 3, IMG])
    w_done, w_cp, w_sq = sig("w_done", QJ), sig("w_copied", QJ), sig("w_squared", QJ)
    n_sum, n_max, n_rec, w_nrm = sig("norm_sum", QJ), sig("norm_guard"), sig("norm_recip"), sig("w_normed", QJ)
    l_done, l_t = sig("token_logits"), sig("token_logits_temp")
    hv, l_sub, l_exp = sig("head_steps", 7), sig("token_less_max"), sig("token_exp")
    pb_done = sig("pi_spread", QJ)
    o_w, o_e, d_sum, d_st, o_n = (sig("w_pi", QJ), sig("w2_pi", QJ), sig("dots_sum", QJ), sig("dots_steps", QJ + 2),
                                  sig("out_scaled", QJ))
    bo_done = sig("bout_added")
    att1_h = sig("att1_residual", 2)

    def img(v):
        return v.rearrange("q (i n) -> q i n", n=NTOK)

    n_lo0 = len(order[0])
    with nc.Block() as block:
        @block.sync
        def _(sp):
            start_at_one(sp)
            load_pieces(sp, att1_p, first[2])

        @block.gpsimd
        def _(pool):
            with pool.Fori(0, NC) as c:
                prep_pool(pool, P3, c)
                pool.wait_ge(P3["xn"].sem, P3["xn"].at(c, NP))
                pool.tensor_tensor(hc(c), hc(c), row["bout"].unsqueeze(1).to_broadcast([RT, NP, D]),
                                   ALU.add).then_inc(bo_done.sem, 1)

        @block.scalar
        def _(act):
            split_high(act, att1_p, first[2])
            with act.Fori(0, NC) as c:
                prep_split_act(act, P3, c, 2, 3)
                for j in range(QJ):
                    act.wait_ge(w_done.sem, w_done.at(c, j + 1))
                    act.wait_ge(o_n.sem, o_n.at(c, 0))
                    act.activation(ws[:, j], banks[:, 2 + j % 2, 0:NT], ACT.Copy).then_inc(w_cp.sem, 1)
                    act.activation(sq[:, j], banks[:, 2 + j % 2, 0:NT], ACT.Square).then_inc(w_sq.sem, 1)
                act.wait_ge(l_done.sem, l_done.at(c, 1))
                act.activation(pq[:, 0:NT], banks[0:NH, 4, 0:NT], ACT.Copy, scale=tempc[:, 0:1]).then_inc(l_t.sem, 1)
                act.wait_ge(l_sub.sem, l_sub.at(c, 1))
                act.activation(pq[:, 0:NT], pq[:, 0:NT], ACT.Exp).then_inc(l_exp.sem, 1)
                post_act(act, S3, c)

        @block.vector
        def _(dve):
            split_low(dve, att1_p, first[2])
            with dve.Fori(0, NC) as c:
                prep_dve(dve, P3, c, None, None)
                prep_split_dve(dve, P3, c, 2, 3)
                for j in range(QJ):
                    dve.wait_ge(w_sq.sem, w_sq.at(c, j + 1))
                    dve.tensor_reduce(n2[:, j, :], img(sq[:, j]), X, ALU.add).then_inc(n_sum.sem, 1)
                dve.wait_ge(n_sum.sem, n_sum.at(c, QJ))
                dve.tensor_scalar(n2[:], n2[:], 1e-24, None, ALU.max).then_inc(n_max.sem, 1)
                dve.wait_ge(n_max.sem, n_max.at(c, 1))
                dve.reciprocal(n2[:], n2[:]).then_inc(n_rec.sem, 1)
                dve.wait_ge(n_rec.sem, n_rec.at(c, 1))
                for j in range(QJ):
                    dve.tensor_tensor(img(wn[:, j]), img(sq[:, j]), n2[:, j, :].unsqueeze(2).to_broadcast([128, IMG, NTOK]),
                                      ALU.mult).then_inc(w_nrm.sem, 1)
                k = [0]

                def link(ins):
                    k[0] += 1
                    ins.then_inc(hv.sem, 1)
                    dve.wait_ge(hv.sem, hv.at(c, k[0]))

                def wide(v):
                    return v.unsqueeze(2).to_broadcast([NH, IMG, NTOK])
                dve.wait_ge(l_t.sem, l_t.at(c, 1))
                link(dve.tensor_reduce(hs[:, 0, :], img(pq[:, 0:NT]), X, ALU.max))
                dve.tensor_tensor(img(pq[:, 0:NT]), img(pq[:, 0:NT]), wide(hs[:, 0, :]), ALU.subtract).then_inc(l_sub.sem, 1)
                dve.wait_ge(l_exp.sem, l_exp.at(c, 1))
                link(dve.tensor_reduce(hs[:, 1, :], img(pq[:, 0:NT]), X, ALU.add))
                link(dve.reciprocal(hs[:, 2, :], hs[:, 1, :]))
                link(dve.tensor_tensor(img(pq[:, 0:NT]), img(pq[:, 0:NT]), wide(hs[:, 2, :]), ALU.mult))
                link(dve.tensor_reduce(hs[:, 1, :], img(pq[:, 0:NT]), X, ALU.add))
                link(dve.tensor_scalar(hs[:, 1, :], hs[:, 1, :], 1e-8, None, ALU.add))
                link(dve.reciprocal(pq[:, NT:NT + IMG], hs[:, 1, :]))
                for j in range(QJ):
                    dve.wait_ge(pb_done.sem, pb_done.at(c, j + 1))
                    dve.tensor_tensor(o1[:, j], ws[:, j], banks[:, 4 + j % 2, 0:NT], ALU.mult).then_inc(o_w.sem, 1)
                    dve.tensor_copy(dt_[:, j, :], banks[:, 4 + j % 2, NT:NT + IMG]).then_inc(d_st.sem, 1)
                    dve.wait_ge(o_w.sem, o_w.at(c, j + 1))
                    dve.tensor_tensor(wn[:, j], o1[:, j], ws[:, j], ALU.mult).then_inc(o_e.sem, 1)
                    dve.wait_ge(o_e.sem, o_e.at(c, j + 1))
                    dve.tensor_reduce(n2[:, j, :], img(wn[:, j]), X, ALU.add).then_inc(d_sum.sem, 1)
                dve.wait_ge(d_sum.sem, d_sum.at(c, QJ))
                dve.wait_ge(d_st.sem, d_st.at(c, QJ))
                dve.tensor_tensor(n2[:], n2[:], dt_[:], ALU.mult).then_inc(d_st.sem, 1)
                dve.wait_ge(d_st.sem, d_st.at(c, QJ + 1))
                dve.tensor_scalar(n2[:], n2[:], 1.0, -1.0, ALU.add, ALU.mult).then_inc(d_st.sem, 1)
                dve.wait_ge(d_st.sem, d_st.at(c, QJ + 2))
                dve.reciprocal(n2[:], n2[:]).then_inc(S3["gl"].sem, 1)
                dve.wait_ge(S3["gl"].sem, S3["gl"].at(c, 1))
                for j in range(QJ):
                    zz = j % 2
                    dve.tensor_tensor(img(zg[:, zz]), img(o1[:, j]), n2[:, j, :].unsqueeze(2).to_broadcast([128, IMG, NTOK]),
                                      ALU.mult).then_inc(o_n.sem, 1)
                    dve.wait_ge(o_n.sem, o_n.at(c, j + 1))
                    dve.wait_ge(S3["dn"].sem, S3["dn"].at(c, max(j - 1, 0)))
                    dve.tensor_copy(zh[:, zz], zg[:, zz]).then_inc(S3["zh"].sem, 1)
                    dve.wait_ge(S3["zh"].sem, S3["zh"].at(c, j + 1))
                    dve.tensor_tensor(zl[:, zz], zg[:, zz], zh[:, zz].bitcast(F32), ALU.subtract).then_inc(S3["zl"].sem, 1)
                dve.wait_ge(bo_done.sem, bo_done.at(c, 1))
                for q in range(2):
                    dve.wait_ge(S3["po"].sem, S3["po"].at(c, q + 1))
                    hq = h[:, bass.ds(c * NP + 2 * q, 2), :]
                    dve.tensor_tensor(hq, hq, banks[0:RT, 2 + q, 0:2 * D].rearrange("q (p f) -> q p f", p=2),
                                      ALU.add).then_inc(att1_h.sem, 1)

        @block.tensor
        def _(pe):
            qk = kparts(mid, 0, SZ_QKV)
            wm, wl = mid[:, wo_main:wo_main + QJ * 128], mid[:, wo_main + QJ * 128:wo_main + 2 * QJ * 128]
            wr = mid[:, wo_rem:wo_rem + QJ * 128]
            pe.wait_ge(lo_done, first[3])
            with pe.Fori(0, NC) as c:
                prep_pe(pe, P3, c, 2, 3)
                prep_wait(pe, P3, c)
                mov = (xh[:], xl[:], xr[:])
                for j in range(QJ):
                    if j >= 2:
                        pe.wait_ge(w_sq.sem, w_sq.at(c, j - 1))
                    weave(pe, banks[:, 2 + j % 2, 0:NT], qk, slice(128 * j, 128 * j + 128), mov,
                          True, True).then_inc(w_done.sem, 1)
                for j in range(QJ):
                    pe.wait_ge(w_nrm.sem, w_nrm.at(c, j + 1))
                    mm = pe.matmul(banks[0:NH, 4, 0:NT], const[:, C_B + NH * j:C_B + NH * (j + 1)], wn[:, j],
                                   start=(j == 0), stop=(j == QJ - 1))
                mm.then_inc(l_done.sem, 1)
                pe.wait_ge(hv.sem, hv.at(c, 7))
                for j in range(QJ):
                    if j >= 2:
                        pe.wait_ge(d_st.sem, d_st.at(c, j - 1))
                    pe.matmul(banks[:, 4 + j % 2, 0:NT + IMG], const[0:NH, C_SB + 128 * j:C_SB + 128 * (j + 1)],
                              pq[:], start=True, stop=True).then_inc(pb_done.sem, 1)
                for j in range(QJ):
                    down_pe(pe, S3, c, j, QJ, wm, wl, wr)
                pe.wait_ge(S3["dn"].sem, S3["dn"].at(c, QJ))
                pe.sem_inc(S3["ac"].sem, 1)
                post_pe(pe, S3, c, 2)

    P4 = new_prep(3)
    M1 = new_mix("ffn1", T1, 24, 4)
    out_done = sem("stored")

    with nc.Block() as block:
        @block.sync
        def _(sp):
            start_at_one(sp)
            load_pieces(sp, ffn1_p, first[3])
            for c in range(NC):
                sp.wait_ge(M1["ph"].sem, M1["ph"].at(c, 2))
                sp.dma_start(a["out"][c], h[:, c * NP:(c + 1) * NP, :]).then_inc(out_done, 16)
            sp.wait_ge(out_done, 16 * NC)

        @block.gpsimd
        def _(pool):
            with pool.Fori(0, NC) as c:
                prep_pool(pool, P4, c)

        @block.scalar
        def _(act):
            split_high(act, ffn1_p, first[3])
            with act.Fori(0, NC) as c:
                prep_split_act(act, P4, c, 2, 3)
                gates_act(act, M1, c, False)
                for t in range(T1):
                    act.wait_ge(M1["hd"].sem, M1["hd"].at(c, t + 1))
                    act.wait_ge(M1["u"].sem, M1["u"].at(c, max(t - 1, 0)))
                    act.activation(zbuf[:, t % 2], banks[:, 2 + t % 2, 0:NT], ACT.Silu).then_inc(M1["z"].sem, 1)
                post_act(act, M1, c)

        @block.vector
        def _(dve):
            split_low(dve, ffn1_p, first[3])
            with dve.Fori(0, NC) as c:
                prep_dve(dve, P4, c, None, None)
                prep_split_dve(dve, P4, c, 2, 3)
                gates_dve(dve, M1, c, MISC, False)
                gates_out(dve, M1, c, MISC)
                for t in range(T1):
                    zz = t % 2
                    dve.wait_ge(M1["z"].sem, M1["z"].at(c, t + 1))
                    dve.tensor_tensor(zg[:, zz], zbuf[:, zz], banks[:, 4 + zz, 0:NT], ALU.mult).then_inc(M1["u"].sem, 1)
                    dve.wait_ge(M1["u"].sem, M1["u"].at(c, t + 1))
                    dve.wait_ge(M1["gb"].sem, M1["gb"].at(c, t + 1))
                    dve.tensor_tensor(zg[:, zz], zg[:, zz], banks[:, GB, 0:NT], ALU.mult).then_inc(M1["g"].sem, 1)
                    dve.wait_ge(M1["g"].sem, M1["g"].at(c, t + 1))
                    dve.wait_ge(M1["dn"].sem, M1["dn"].at(c, max(t - 1, 0)))
                    dve.tensor_copy(zh[:, zz], zg[:, zz]).then_inc(M1["zh"].sem, 1)
                    dve.wait_ge(M1["zh"].sem, M1["zh"].at(c, t + 1))
                    dve.tensor_tensor(zl[:, zz], zg[:, zz], zh[:, zz].bitcast(F32), ALU.subtract).then_inc(M1["zl"].sem, 1)
                for q in range(2):
                    dve.wait_ge(M1["po"].sem, M1["po"].at(c, q + 1))
                    hq = h[:, bass.ds(c * NP + 2 * q, 2), :]
                    dve.tensor_tensor(hq, hq, banks[0:RT, 2 + q, 0:2 * D].rearrange("q (p f) -> q p f", p=2),
                                      ALU.add).then_inc(M1["ph"].sem, 1)

        @block.tensor
        def _(pe):
            gu = kparts(big, 0, SZ_GU)
            dm, dl = big[:, dn1_main:dn1_main + T1 * 128], big[:, dn1_main + T1 * 128:dn1_main + 2 * T1 * 128]
            dr = big[:, dn1_rem:dn1_rem + T1 * 128]
            rw = kparts(small, 4 * SZ_W1, SZ_RT)
            pe.wait_ge(lo_done, first[3] + len(ffn1_p))
            with pe.Fori(0, NC) as c:
                prep_pe(pe, P4, c, 2, 3)
                prep_wait(pe, P4, c)
                mov = (xh[:], xl[:], xr[:])
                for p in range(NP):
                    t = slice(RT * p, RT * p + RT)
                    H, L, RH, RL = rw
                    seq = [(xh, H), (xh, L), (xr, RH), (xr, RL), (xl, H)]
                    for k, (st, m) in enumerate(seq):
                        mm = pe.matmul(banks[0:RT, MISC, 10 * p:10 * p + 10], st[:, t], m, start=(k == 0), stop=(k == 4))
                mm.then_inc(M1["lg"].sem, 1)

                def hidden(t):
                    if t >= 2:
                        pe.wait_ge(M1["u"].sem, M1["u"].at(c, t - 1))
                    for i in range(2):
                        mm = weave(pe, banks[:, 2 + 2 * i + t % 2, 0:NT], gu,
                                   slice(256 * t + 128 * i, 256 * t + 128 * i + 128), mov, True, True)
                    mm.then_inc(M1["hd"].sem, 1)

                hidden(0)
                gates_pe(pe, M1, c, MISC)
                pe.wait_ge(M1["gl"].sem, M1["gl"].at(c, 1))

                def spread(t):
                    e = E0 + min(t, T1R)
                    if t:
                        pe.wait_ge(M1["g"].sem, M1["g"].at(c, t))
                    pe.matmul(banks[:, GB, 0:NT], selr[:, 128 * e:128 * e + 128], gT[:],
                              start=True, stop=True).then_inc(M1["gb"].sem, 1)

                spread(0)
                for t in range(T1):
                    if t + 1 < T1:
                        hidden(t + 1)
                    down_pe(pe, M1, c, t, T1, dm, dl, dr)
                    if t + 1 < T1:
                        spread(t + 1)
                pe.wait_ge(M1["dn"].sem, M1["dn"].at(c, T1))
                pe.sem_inc(M1["ac"].sem, 1)
                post_pe(pe, M1, c, 2)


def constants(np):
    c = np.zeros((128, C_ALL), np.float32)
    c[:, C_ID:C_ID + 128] = np.eye(128)
    c[:, C_II:C_II + DR] = np.tile(np.eye(DR), (2, 1))
    for j in range(QJ):
        for q in range(128):
            c[q, C_B + NH * j + 2 * j + q // 64] = 1
            c[2 * j + q // 64, C_SB + 128 * j + q] = 1
    for q in range(VR):
        c[q, C_VM + q // NTOK] = 1
    c[0:NTOK, C_MAB] = 1
    c[NTOK:RT, C_MAB + 1] = 1
    c[:, C_IOTA:C_IOTA + E0] = np.arange(E0)
    return c


def selectors(np):
    s = np.zeros((SELW, NSEL), np.float32)
    for n in range(NSEL):
        t, m = divmod(n, 128)
        e = t if t < E0 else ((128 * (t - E0) + m) // D if t - E0 < T1R else E0)
        s[e, n] = s[32 + e, n] = 1
    return s


def kernel(**inputs):
    import numpy as np
    import concourse.bacc as bacc
    from concourse.bass_utils import run_bass_kernel_spmd as run

    i = {k: np.asarray(v) for k, v in inputs.items()}
    cat = np.concatenate

    def twice(w):
        return cat([w, w], 0)

    x = i["x"].reshape(NI, 6, 16, 6, 16, 3).transpose(0, 1, 3, 2, 4, 5).reshape(NI, 36, 768)
    x = cat([np.zeros((NI, 1, 768), np.float32), x], 1)
    x = x.reshape(NC, IMG * NTOK, KP, 128).transpose(0, 3, 2, 1).reshape(NC * 128, KP * NT)

    def tiles(w):
        return w.reshape(-1, 128, w.shape[1]).transpose(1, 0, 2)

    basis = i["L0_attn_basis_w"].T
    z = np.zeros_like(basis)
    basis = cat([basis, z, z, basis], 1)
    val = i["L0_attn_value_w"].T
    dn0 = i["L0_ffn_down_w"].transpose(1, 0, 2).reshape(D, T0 * 128)
    up0 = tiles(i["L0_ffn_up_w"].reshape(T0 * 128, D))
    wo = tiles(i["L1_attn_w_out"])
    qkv = i["L1_attn_w_qkv"]
    gate = cat([i["L1_ffn_w_gate"].transpose(1, 0, 2).reshape(D, -1), i["L1_ffn_ws_gate"]], 1)
    up = cat([i["L1_ffn_w_up"].transpose(1, 0, 2).reshape(D, -1), i["L1_ffn_ws_up"]], 1)
    gu = np.stack([gate.reshape(D, T1, 128), up.reshape(D, T1, 128)], 2).reshape(D, SZ_GU)
    dn1 = tiles(cat([i["L1_ffn_w_down"].reshape(-1, D), i["L1_ffn_ws_down"]], 0))
    rt = cat([i["L1_ffn_router_w"], i["L1_ffn_sg_w"], np.zeros((D, 1), np.float32)], 1)
    cols = np.zeros((128, 32), np.float32)
    cols[:, 0:T0] = i["L0_ffn_down_b"].reshape(T0, 128).T
    cols[0:96, 16] = i["L0_ffn_b1"]
    arrays = {
        "const": constants(np), "sel": selectors(np), "patches": x, "w_tok": tiles(i["L0_tok_W_proj"]).reshape(128, -1),
        "w_att0_k": basis[0:128], "w_att0_r": twice(basis[128:]),
        "w_val_k": val[0:128], "w_val_r": twice(val[128:]),
        "w_dn0_k": dn0[0:128], "w_dn0_r": twice(dn0[128:]),
        "w_up0_m": up0[:, :, 0:128].reshape(128, -1), "w_up0_r": up0[:, :, 128:].reshape(128, -1),
        "w_w1_k": i["L0_ffn_w1"][0:128], "w_w1_r": twice(i["L0_ffn_w1"][128:]), "w_w2": i["L0_ffn_w2"],
        "w_qkv_k": qkv[0:128], "w_qkv_r": twice(qkv[128:]),
        "w_wo_m": wo[:, :, 0:128].reshape(128, -1), "w_wo_r": wo[:, :, 128:].reshape(128, -1),
        "w_gu_k": gu[0:128], "w_gu_r": twice(gu[128:]),
        "w_dn1_m": dn1[:, :, 0:128].reshape(128, -1), "w_dn1_r": dn1[:, :, 128:].reshape(128, -1),
        "w_rt_k": rt[0:128], "w_rt_r": twice(rt[128:]),
        "hrt": i["L0_attn_head_residual"].transpose(2, 0, 1), "coret": i["L0_attn_core"].T,
        "cols": cols, "temp": i["L1_attn_temp"], "pos": i["L0_tok_pos_embedding"],
        "cls": i["L0_tok_cls_token"].reshape(1, D), "bproj": i["L0_tok_b_proj"], "vb": i["L0_attn_value_b"],
        "gamma": i["L0_ffn_gamma"], "beta": i["L0_ffn_beta"], "bout": i["L1_attn_b_out"],
        "b2": i["L0_ffn_b2"], "sgb": i["L1_ffn_sg_b"],
    }
    nc = bacc.Bacc("TRN2", target_bir_lowering=False, num_devices=1)
    fed, a = {}, {}
    for name, v in arrays.items():
        v = np.ascontiguousarray(v)
        fed["in_" + name] = v
        a[name] = nc.dram_tensor("in_" + name, v.shape, F32, kind="ExternalInput").ap()
    a["out"] = nc.dram_tensor("out_0", (NC, RT, NP, D), F32, kind="ExternalOutput").ap()
    tower(nc, a)
    r = run(nc, [fed], core_ids=[0])
    got = r.results[0]["out_0"]
    return got.transpose(0, 2, 1, 3).reshape(NI, NTOK, D)
```

```python
from contextlib import ExitStack

import concourse.bass as bass
from concourse import mybir

F32 = mybir.dt.float32
F32R = mybir.dt.float32r
U32 = mybir.dt.uint32
ALU = mybir.AluOpType
ACT = mybir.ActivationFunctionType
X = mybir.AxisListType.X

D = 192
DR = D - 128
NI, NTOK = 32, 37
NC, NP = 4, 4
RT = 2 * NTOK
NT = NP * RT
IMG = 2 * NP
KP = 6
NH, HD, RK = 12, 16, 64
NG, GH = 4, 3
VR = GH * NTOK
E0, T0 = 8, 16
T1R, T1 = 12, 18
QJ = 6
EPS = 1e-5
SELW = 64

C_ID, C_II = 0, 128
C_B = C_II + DR
C_SB = C_B + QJ * NH
C_VM = C_SB + QJ * 128
C_MAB = C_VM + GH
C_IOTA = C_MAB + 2
C_ALL = C_IOTA + E0

NSEL = (E0 + T1R + 1) * 128

ROWS = ["pos", "bproj", "vb", "gamma", "beta", "bout"]
K_ROWS = 0
K_B2 = K_ROWS + len(ROWS) * D
K_SGB = K_B2 + E0
K_B1 = K_SGB + 1
K_DB = K_B1 + 1
K_W2 = K_DB + T0
K_TEMP = K_W2 + E0
K_ALL = K_TEMP + 1

SZ_TOK = KP * D
SZ_ATT0 = 2 * 256 + 2 * D
SZ_DN0 = T0 * 128
SZ_FFN0 = 3 * SZ_DN0
SZ_W1 = 96
SZ_QKV = QJ * 128
SZ_ATT1 = 3 * SZ_QKV
SZ_GU = 2 * T1 * 128
SZ_FFN1 = 2 * SZ_GU + T1 * 128
SZ_RT = 10
WST = 1024


STARTS_AT_ONE = {
    "att1_acc_out", "att1_down_done", "att1_residual", "att1_times_gate", "att1_z_low", "ctx_added",
    "ctx_done", "ffn0_acc_out", "ffn0_activated", "ffn0_down_done", "ffn0_residual",
    "ffn0_times_gate", "ffn0_z_low", "ffn1_acc_out", "ffn1_added", "ffn1_down_done",
    "ffn1_times_up", "ffn1_z_low", "moe_added", "norm_xl", "norm_xr_low", "probs_turned",
    "tok_done",
}


class Signal:

    def __init__(self, take, name, per=1, base=0):
        self.take, self.name, self.per, self.held, self.base = take, name, per, None, base

    @property
    def sem(self):
        if self.held is None:
            self.held = self.take(self.name)
        return self.held

    def at(self, c, k):
        assert self.base + k > 0, self.name
        return c * self.per + (self.base + k)


def tower(nc, a):
    with ExitStack() as ctx:
        body(nc, a, ctx)


def body(nc, a, ctx):
    first_half = ctx.enter_context(ExitStack())

    def sb(name, shape, dt=F32, where=ctx):
        return where.enter_context(nc.sbuf_tensor(name, shape, dt))

    def sem(name):
        return ctx.enter_context(nc.semaphore(name))

    def sig(name, per=1):
        s = Signal(sem, name, per, int(name in STARTS_AT_ONE))
        if s.base:
            ones.append(s)
        return s

    ones = []

    def start_at_one(sp):
        while ones:
            sp.sem_inc(ones.pop().sem, 1)

    banks = ctx.enter_context(nc.psum_tensor("banks", [128, 8, 512], F32))

    const = sb("const", [128, C_ALL])
    ident = const[:, C_ID:C_ID + 128]
    pack = sb("pack", [128, K_ALL])
    rows = pack[0:RT, K_ROWS:K_ROWS + 6 * D].rearrange("q (i f) -> q i f", i=6)
    row = {n: rows[:, i, :] for i, n in enumerate(ROWS)}
    h = sb("h", [RT, NC * NP, D])
    stats = sb("stats", [RT, NP, 6])
    mv = sb("mv", [RT, NP, 2])
    rstd = sb("rstd", [RT, NP])
    mhalf = sb("mhalf", [RT, NP])
    xh = sb("xh", [128, 2, NT], F32R)
    xl = sb("xl", [128, 2, NT], F32R)
    xr = sb("xr", [128, 2, NT], F32R)
    gT = sb("gT", [SELW, 2, NT], F32R)
    gx = sb("gx", [RT, NP, SELW])
    rt = sb("rt", [RT, 8, NP, 10])
    ri = sb("ri", [RT, NP, 8], U32)
    wstage = sb("wstage", [128, 2, WST])
    zbuf = sb("zbuf", [128, 2, NT])
    zg = sb("zg", [128, 3, NT])
    zh = sb("zh", [128, 3, NT], F32R)
    zl = sb("zl", [128, 3, NT], F32R)
    acc_sb = sb("acc_sb", [128, 2, NT])
    mid = sb("mid", [128, 2 * SZ_ATT1 + QJ * 128], F32R)

    xn = sb("xn", [RT, 2, NP, D + DR], where=first_half)
    sel0 = sb("sel0", [SELW, E0 * 128], F32R, first_half)
    wtok = sb("wtok", [128, 2 * SZ_TOK + 2 * SZ_ATT0], F32R, first_half)
    big0 = sb("big0", [128, 2 * SZ_FFN0 + T0 * 128], F32R, first_half)
    w1s = sb("w1s", [128, 4 * SZ_W1], F32R, first_half)
    xs = sb("xs", [128, KP * NT], where=first_half)
    xsh = sb("xsh", [128, KP * NT], F32R, first_half)
    xsl = sb("xsl", [128, KP * NT], F32R, first_half)
    xrep = mid[:, 0:3 * IMG * VR].rearrange("q (k i m) -> q k i m", k=3, i=IMG)
    uh = sb("uh", [128, NP, NH, NTOK], where=first_half)
    mbd = sb("mbd", [128, NH, 128], where=first_half)
    lat = sb("lat", [128, NP * NTOK], where=first_half)
    lbd = sb("lbd", [128, NP, RT], where=first_half)
    sx = sb("sx", [RT, 2, NH * NTOK], where=first_half)
    pts = sb("pts", [VR, 2, NG, RT], where=first_half)
    vbd = sb("vbd", [VR, 2, 2 * D], where=first_half)
    uc = sb("uc", [RT, D], where=first_half)
    sm = sb("sm", [RT, 2, 3, NH], where=first_half)
    hrt = uh[:].rearrange("q a b c -> q (a b c)")[:, 0:NH * RK].rearrange("q (h r) -> q h r", h=NH)
    hset = uh[:].rearrange("q a b c -> q (a b c)")[:, 800:800 + 3 * RK].rearrange("q (i r) -> q i r", i=3)
    g1 = xs[0:96, 0:NT]
    y0 = xs[0:RT, NT:NT + NP * D].rearrange("q (p f) -> q p f", p=NP)

    def split_pass(eng, out, parts, mov, start=True, stop=True):
        H, L, RH, RL = parts
        mh, ml, mr = mov
        seq = [(H, mh), (L, mh), (RH, mr), (RL, mr), (H, ml)]
        for i, (w, m) in enumerate(seq):
            ins = eng.matmul(out, w, m, start=start and i == 0, stop=stop and i == len(seq) - 1)
        return ins

    slot_loaded = [sem("stage0_loaded"), sem("stage1_loaded")]
    hi_done, lo_done = sem("weights_high_done"), sem("weights_low_done")

    class Piece:

        def __init__(self, first, src, high, low, n, step=0):
            self.first, self.src, self.high, self.low, self.n, self.step = first, src, high, low, n, step
            assert step % 2 == 0

        def number(self, i):
            return self.first + (self.step * i if self.step else 0)

        def stage(self):
            v = wstage[:, self.first % 2, 0:self.n]
            return v.rearrange("p (t f) -> p t f", f=DR) if len(self.high(0).shape) == 3 else v

    numbers = [0]

    def straight(src, high, low, n):
        out = []
        for o in range(0, n, WST):
            m = min(WST, n - o)
            out.append(Piece(numbers[0], lambda i, o=o, m=m: src[:, o:o + m], lambda i, o=o, m=m: high[:, o:o + m],
                             lambda i, o=o, m=m: low[:, o:o + m], m))
            numbers[0] += 1
        return out

    def side_by_side(src, nt, dst):
        v = dst.rearrange("p (t s f) -> p t s f", s=2, f=DR)
        out, m = [], WST // DR
        for o in range(0, nt, m):
            e = min(o + m, nt)
            out.append(Piece(numbers[0], lambda i, o=o, e=e: src[:, o * DR:e * DR],
                             lambda i, o=o, e=e: v[:, o:e, 0, :], lambda i, o=o, e=e: v[:, o:e, 1, :], (e - o) * DR))
            numbers[0] += 1
        return out

    def looped(src, high, low, n, loops, unroll):
        w = n // (loops * unroll)
        assert w * loops * unroll == n and w <= WST
        out = []
        for j in range(unroll):
            def at(t, j=j):
                return lambda i: t[:, bass.ds(w * j + w * unroll * i, w)]
            out.append(Piece(numbers[0] + j, at(src), at(high), at(low), w, unroll))
        numbers[0] += loops * unroll
        return out

    def load(sp, ps, i=0):
        for p in ps:
            if p.first >= 2:
                sp.wait_ge(hi_done, p.number(i) - 1)
                sp.wait_ge(lo_done, p.number(i) - 1)
            sp.dma_start(wstage[:, p.first % 2, 0:p.n], p.src(i)).then_inc(slot_loaded[p.first % 2], 16)

    def high(act, ps, i=0):
        for p in ps:
            turns = p.first // 2 + 1
            act.wait_ge(slot_loaded[p.first % 2], 16 * turns + (8 * p.step * i if p.step else 0))
            act.activation(p.high(i), p.stage(), ACT.Copy).then_inc(hi_done, 1)

    def low(eng, ps, i=0):
        for p in ps:
            eng.wait_ge(hi_done, p.number(i) + 1)
            eng.tensor_tensor(p.low(i), p.stage(), p.high(i).bitcast(F32), ALU.subtract).then_inc(lo_done, 1)

    big0_h, big0_l, up0_r = big0[:, 0:SZ_FFN0], big0[:, SZ_FFN0:2 * SZ_FFN0], big0[:, 2 * SZ_FFN0:]
    mid_h, mid_l, wo_r = mid[:, 0:SZ_ATT1], mid[:, SZ_ATT1:2 * SZ_ATT1], mid[:, 2 * SZ_ATT1:]
    tok_p = straight(a["w_tok"], wtok[:, 0:SZ_TOK], wtok[:, SZ_TOK:2 * SZ_TOK], SZ_TOK)
    att0_p = straight(a["w_att0"], wtok[:, 2 * SZ_TOK:2 * SZ_TOK + SZ_ATT0],
                      wtok[:, 2 * SZ_TOK + SZ_ATT0:], SZ_ATT0)
    ffn0_p = looped(a["w_ffn0"], big0_h, big0_l, SZ_FFN0, NC, 2)
    ffn0_q = straight(a["w_w1"], w1s[:, 0:2 * SZ_W1], w1s[:, 2 * SZ_W1:], 2 * SZ_W1) + \
        side_by_side(a["w_up0_r"], T0, up0_r)
    att1_q = side_by_side(a["w_wo_r"], QJ, wo_r)
    att1_p = looped(a["w_att1"], mid_h, mid_l, SZ_ATT1, 2, 2)

    wait_taken = sem("wait_taken")

    def plain(eng):
        eng.sem_inc(wait_taken, 1)

    PREP = dict(st=sig("norm_stats", NP), mv=sig("norm_meanvar", NP), ve=sig("norm_vareps"), rs=sig("norm_rstd"),
                xn=sig("norm_normed", NP), tw=sig("norm_normed_twice"), t0=sig("norm_turned"),
                t1=sig("norm_rest_turned"), xh=sig("norm_xh"), xl=sig("norm_xl"), rh=sig("norm_xr_high"),
                rl=sig("norm_xr_low"))

    def hc(tile, n=NP):
        return h[:, bass.ds(tile, n), :]

    def h1(tile):
        return h[:, tile, :] if isinstance(tile, int) else hc(tile, 1).rearrange("a b d -> a (b d)")

    def norm_dve(dve, n, tile):
        for p in range(NP):
            dve.bn_stats(stats[:, p, :], h1(tile + p)).then_inc(PREP["st"].sem, 1)
        for p in range(NP):
            dve.wait_ge(PREP["st"].sem, PREP["st"].at(n, p + 1))
            plain(dve)
            dve.bn_aggr(mv[:, p, :], stats[:, p, :]).then_inc(PREP["mv"].sem, 1)
        dve.wait_ge(PREP["mv"].sem, PREP["mv"].at(n, NP))
        dve.tensor_scalar(rstd[:], mv[:, :, 1], EPS, None, ALU.add).then_inc(PREP["ve"].sem, 1)

    def norm_dve2(dve, n, tile, xn_):
        dve.wait_ge(PREP["rs"].sem, PREP["rs"].at(n, 1))
        for p in range(NP):
            dve.tensor_scalar(xn_[:, p, 0:D], h1(tile + p), mv[:, p, 0:1], rstd[:, p:p + 1],
                              ALU.subtract, ALU.mult).then_inc(PREP["xn"].sem, 1)

    def norm_pool(pool, n):
        pool.wait_ge(PREP["ve"].sem, PREP["ve"].at(n, 1))
        pool.tensor_tensor(rstd[:], rstd[:], mhalf[:], ALU.pow).then_inc(PREP["rs"].sem, 1)

    def norm_act(act, n, xn_):
        act.wait_ge(PREP["xn"].sem, PREP["xn"].at(n, NP))
        act.activation(xn_[:, :, D:D + DR], xn_[:, :, 128:D], ACT.Copy).then_inc(PREP["tw"].sem, 1)

    def turn_pe(pe, n, xn_, bank):
        pe.wait_ge(PREP["xn"].sem, PREP["xn"].at(n, NP))
        for p in range(NP):
            mm = pe.transpose(banks[:, bank, p * RT:(p + 1) * RT], xn_[:, p, 0:128], ident[0:RT, 0:RT])
        mm.then_inc(PREP["t0"].sem, 1)

    def turn_rest_pe(pe, n, xn_, bank):
        pe.wait_ge(PREP["tw"].sem, PREP["tw"].at(n, 1))
        for p in range(NP):
            mm = pe.transpose(banks[:, bank, p * RT:(p + 1) * RT], xn_[:, p, 128:D + DR], ident[0:RT, 0:RT])
        mm.then_inc(PREP["t1"].sem, 1)

    def columns(by_half):
        if not by_half:
            return (lambda v: v), (lambda v: v)
        return (lambda v: v.rearrange("q (p s n) -> q s p n", p=NP, s=2),
                lambda v: v.rearrange("q (s p n) -> q s p n", p=NP, s=2))

    def turned_act(act, n, u, bank, by_half=False):
        f, g = columns(by_half)
        act.wait_ge(PREP["t0"].sem, PREP["t0"].at(n, 1))
        act.activation(g(xh[:, u]), f(banks[:, bank, 0:NT]), ACT.Copy).then_inc(PREP["xh"].sem, 1)

    def turned_dve(dve, n, u, bank, by_half=False):
        f, g = columns(by_half)
        dve.wait_ge(PREP["xh"].sem, PREP["xh"].at(n, 1))
        dve.tensor_tensor(g(xl[:, u]), f(banks[:, bank, 0:NT]), g(xh[:, u].bitcast(F32)),
                          ALU.subtract).then_inc(PREP["xl"].sem, 1)

    def rest_act(act, n, u, bank, by_half=False):
        f, g = columns(by_half)
        act.wait_ge(PREP["t1"].sem, PREP["t1"].at(n, 1))
        act.activation(g(xr[:, u]), f(banks[:, bank, 0:NT]), ACT.Copy).then_inc(PREP["rh"].sem, 1)

    def rest_dve(dve, n, u, bank, by_half=False):
        f, g = columns(by_half)
        dve.wait_ge(PREP["rh"].sem, PREP["rh"].at(n, 1))
        dve.tensor_tensor(g(xr[64:128, u]), f(banks[64:128, bank, 0:NT]), g(xr[64:128, u].bitcast(F32)),
                          ALU.subtract).then_inc(PREP["rl"].sem, 1)

    def turned_wait(pe, n):
        for k in ("xh", "xl", "rh", "rl"):
            pe.wait_ge(PREP[k].sem, PREP[k].at(n, 1))

    setup, const_in = sem("setup_vec"), sem("const_in")
    x_in, x_hi, x_lo = sem("patches_in"), sig("patches_high"), sig("patches_low")
    tok_done, h0_done = sig("tok_done", 2), sig("tok_added", 2)
    lat_done, lat_ev = sig("latent_done"), sig("latent_out", 3)
    u_done, u_ev = sig("u_done", 4), sig("u_out", 4)
    s_done, mx_done, sub_done = sig("scores_done", NP), sig("score_max", NP), sig("scores_less_max", NP)
    e_done, sum_done, rec_done = sig("exp_done", NP), sig("prob_sum", NP), sig("prob_recip", NP)
    pt_done, pt_ev = sig("probs_turned", NP), sig("probs_turned_out", NP)
    v_done, v_ev = sig("values_done", NP), sig("values_out", NP)
    c_done, c_a, c_b, c_n, c_h = (sig("ctx_done", NP), sig("ctx_first_image", NP), sig("ctx_both", NP),
                                  sig("ctx_normed", NP), sig("ctx_added", NP))
    vb_done = sig("value_bias_added")
    rep_done = [sig(n + "_repeated") for n in ("xh", "xl", "xr")]
    PH = NP * NTOK
    XU = 1
    wt_h, wt_l = wtok[:, 0:SZ_TOK], wtok[:, SZ_TOK:2 * SZ_TOK]
    w0h, w0l = wtok[:, 2 * SZ_TOK:2 * SZ_TOK + SZ_ATT0], wtok[:, 2 * SZ_TOK + SZ_ATT0:]
    N_CONST = 16 * 4

    with nc.Block() as block:
        @block.sync
        def _(sp):
            start_at_one(sp)
            sp.dma_start(xs[:], a["patches"][0:128, :]).then_inc(x_in, 16)
            load(sp, tok_p)
            sp.dma_start(pack[:], a["pack"]).then_inc(const_in, 16)
            sp.dma_start(hrt, a["hrt"][:, 0:NH * RK].rearrange("q (h r) -> q h r", h=NH)).then_inc(const_in, 16)
            sp.dma_start(hset[:, 0, :], a["hrt"][:, NH * RK:]).then_inc(const_in, 16)
            sp.dma_start(const[:], a["const"]).then_inc(const_in, 16)
            load(sp, att0_p)

            def more(c, last=False):
                if not last:
                    sp.wait_ge(x_hi.sem, x_hi.at(c, 1))
                    sp.wait_ge(x_lo.sem, x_lo.at(c, 1))
                    sp.dma_start(xs[:], a["patches"][bass.ds(c * 128 + 128, 128), :]).then_inc(x_in, 16)
                load(sp, ffn0_p, c)
            with sp.Fori(0, NC - 1) as c:
                more(c)
            more(NC - 1, True)
            load(sp, ffn0_q)

        @block.gpsimd
        def _(pool):
            def patches(n):
                pool.wait_ge(x_in, n * 16 + 16)
                pool.wait_ge(tok_done.sem, tok_done.at(n, 0))
                plain(pool)
                pool.tensor_scalar(xsh[:], xs[:], 1.0, 0.0, ALU.mult, ALU.add).then_inc(x_hi.sem, 1)
                pool.wait_ge(x_hi.sem, x_hi.at(n, 1))
                pool.tensor_tensor(xsl[:], xs[:], xsh[:].bitcast(F32), ALU.subtract).then_inc(x_lo.sem, 1)

            def chunk(c, last=False):
                if not last:
                    patches(c + 1)
                pool.wait_ge(PREP["xn"].sem, PREP["xn"].at(c, NP))
                pool.tensor_tensor(hc(c * NP), hc(c * NP), row["vb"].unsqueeze(1).to_broadcast([RT, NP, D]),
                                   ALU.add).then_inc(vb_done.sem, 1)
                low(pool, ffn0_p, c)
                norm_pool(pool, c + 1)

            norm_pool(pool, 0)
            with pool.Fori(0, NC - 1) as c:
                chunk(c)
            chunk(NC - 1, True)
            low(pool, ffn0_q)

        @block.scalar
        def _(act):
            act.wait_ge(x_in, 16)
            act.activation(xsh[:], xs[:], ACT.Copy).then_inc(x_hi.sem, 1)
            high(act, tok_p)
            high(act, att0_p)

            def finish(n, u, by_half):
                norm_act(act, n, xn[:, u])
                turned_act(act, n, u, 0, by_half)
                rest_act(act, n, u, 1, by_half)

            def repeat_x(n):
                v = xh[:, XU].bitcast(F32).rearrange("q (i n) -> q i n", i=IMG).unsqueeze(2).to_broadcast([128, IMG, GH, NTOK])
                act.wait_ge(PREP["xh"].sem, PREP["xh"].at(n, 1))
                act.wait_ge(c_done.sem, c_done.at(n, 0))
                act.activation(xrep[:, 0].rearrange("q i (r n) -> q i r n", r=GH), v, ACT.Copy).then_inc(rep_done[0].sem, 1)

            def chunk(c, last=False):
                act.wait_ge(lat_done.sem, lat_done.at(c, 1))
                act.wait_ge(c_done.sem, c_done.at(c, 0))
                act.activation(lat[:], banks[:, 2, 0:PH], ACT.Copy).then_inc(lat_ev.sem, 1)
                for i in range(2):
                    s = slice(64 * i, 64 * i + 64)
                    act.activation(lbd[s, :, NTOK * i:NTOK * (i + 1)],
                                   banks[s, 2, 0:PH].rearrange("q (p n) -> q p n", p=NP),
                                   ACT.Copy).then_inc(lat_ev.sem, 1)
                for k in range(4):
                    act.wait_ge(u_done.sem, u_done.at(c, k + 1))
                    act.activation(uh[:, :, GH * k:GH * (k + 1), :],
                                   banks[:, 4 + k, 0:GH * PH].rearrange("q (h p n) -> q p h n", h=GH, p=NP),
                                   ACT.Copy).then_inc(u_ev.sem, 1)
                high(act, ffn0_p[0:1], c)

                def exp(p):
                    act.wait_ge(sub_done.sem, sub_done.at(c, p + 1))
                    act.activation(sx[:, p % 2], sx[:, p % 2], ACT.Exp).then_inc(e_done.sem, 1)

                exp(0)
                for p in range(NP):
                    if p + 1 < NP:
                        exp(p + 1)
                    act.wait_ge(pt_done.sem, pt_done.at(c, p + 1))
                    act.activation(pts[:, p % 2], banks[0:VR, 6, 0:NT].rearrange("q (g t) -> q g t", g=NG),
                                   ACT.Copy).then_inc(pt_ev.sem, 1)
                    act.wait_ge(c_done.sem, c_done.at(c, p + 1))
                    act.wait_ge(c_h.sem, c_h.at(c, p))
                    act.activation(uc[:], banks[0:RT, 7, 0:D], ACT.Copy,
                                   scale=const[0:RT, C_MAB:C_MAB + 1]).then_inc(c_a.sem, 1)
                    if p == 1:
                        high(act, ffn0_p[1:2], c)
                if last:
                    finish(NC, 0, False)
                else:
                    finish(c + 1, XU, True)
                    repeat_x(c + 1)

            finish(0, XU, True)
            repeat_x(0)
            with act.Fori(0, NC - 1) as c:
                chunk(c)
            chunk(NC - 1, True)
            high(act, ffn0_q)

        @block.vector
        def _(dve):
            dve.memset(mbd[:], 0.0).then_inc(setup, 1)
            dve.memset(mhalf[:], -0.5).then_inc(setup, 1)
            dve.memset(gx[:], 0.0).then_inc(setup, 1)
            dve.memset(lbd[:], 0.0).then_inc(setup, 1)
            dve.wait_ge(x_hi.sem, x_hi.at(0, 1))
            dve.tensor_tensor(xsl[:], xs[:], xsh[:].bitcast(F32), ALU.subtract).then_inc(x_lo.sem, 1)
            low(dve, tok_p)
            dve.wait_ge(const_in, N_CONST)
            dve.tensor_tensor(row["pos"], row["pos"], row["bproj"], ALU.add).then_inc(setup, 1)
            dve.tensor_reduce(hset[:, 1, :], hrt.rearrange("p h r -> p r h"), X, ALU.add).then_inc(setup, 1)
            dve.wait_ge(setup, 6)
            dve.tensor_tensor(hset[:, 2, :], hset[:, 0, :], hset[:, 1, :], ALU.subtract).then_inc(setup, 1)
            dve.wait_ge(setup, 7)
            dve.tensor_scalar(hset[:, 1, :], hset[:, 2, :], 1.0 / NH, None, ALU.mult).then_inc(setup, 1)
            dve.wait_ge(setup, 8)
            dve.tensor_tensor(hrt, hrt, hset[:, 1, :].unsqueeze(1).to_broadcast([128, NH, RK]), ALU.add).then_inc(setup, 1)
            dve.wait_ge(setup, 9)
            for i in range(2):
                s = slice(64 * i, 64 * i + 64)
                dve.tensor_scalar(mbd[s, :, s], hrt[s], RK ** -0.5, None, ALU.mult).then_inc(setup, 1)
            low(dve, att0_p)

            def tok_add(n, i):
                dve.wait_ge(tok_done.sem, tok_done.at(n, i + 1))
                dve.tensor_tensor(hc(n * NP + 2 * i, 2), banks[0:RT, i, 0:2 * D].rearrange("q (p f) -> q p f", p=2),
                                  row["pos"].unsqueeze(1).to_broadcast([RT, 2, D]), ALU.add).then_inc(h0_done.sem, 1)

            def finish(n, u, by_half):
                turned_dve(dve, n, u, 0, by_half)
                rest_dve(dve, n, u, 1, by_half)

            def repeat_x(n):
                for k, (t, s) in enumerate(((xl, "xl"), (xr, "rl"))):
                    v = t[:, XU].bitcast(F32).rearrange("q (i n) -> q i n", i=IMG).unsqueeze(2).to_broadcast([128, IMG, GH, NTOK])
                    dve.wait_ge(PREP[s].sem, PREP[s].at(n, 1))
                    if k:
                        dve.wait_ge(PREP["rh"].sem, PREP["rh"].at(n, 1))
                    dve.wait_ge(c_done.sem, c_done.at(n, 0))
                    dve.tensor_copy(xrep[:, k + 1].rearrange("q i (r n) -> q i r n", r=GH), v).then_inc(rep_done[k + 1].sem, 1)

            def chunk(c, last=False):
                def less_max(p):
                    S = banks[0:RT, 4 + p % 2, 0:NH * NTOK].rearrange("q (h m) -> q h m", h=NH)
                    dve.wait_ge(s_done.sem, s_done.at(c, p + 1))
                    dve.tensor_reduce(sm[:, p % 2, 0], S, X, ALU.max).then_inc(mx_done.sem, 1)
                    dve.wait_ge(mx_done.sem, mx_done.at(c, p + 1))
                    dve.wait_ge(pt_done.sem, pt_done.at(c, max(p - 1, 0)))
                    dve.tensor_tensor(sx[:, p % 2].rearrange("q (h m) -> q h m", h=NH), S,
                                      sm[:, p % 2, 0].unsqueeze(2).to_broadcast([RT, NH, NTOK]),
                                      ALU.subtract).then_inc(sub_done.sem, 1)

                def values(p):
                    dve.wait_ge(v_done.sem, v_done.at(c, p + 1))
                    dve.wait_ge(c_done.sem, c_done.at(c, max(p - 1, 0)))
                    dve.tensor_tensor(vbd[:, p % 2].rearrange("q (g h d) -> q g h d", h=GH, d=HD),
                                      banks[0:VR, 3, 0:2 * D].rearrange("q (g h d) -> q g h d", h=GH, d=HD),
                                      const[0:VR, C_VM:C_VM + GH].unsqueeze(1).unsqueeze(3).to_broadcast([VR, 2 * NG, GH, HD]),
                                      ALU.mult).then_inc(v_ev.sem, 1)

                less_max(0)
                values(0)
                for p in range(NP):
                    if p + 1 < NP:
                        less_max(p + 1)
                    dve.wait_ge(e_done.sem, e_done.at(c, p + 1))
                    dve.tensor_reduce(sm[:, p % 2, 1], sx[:, p % 2].rearrange("q (h m) -> q h m", h=NH),
                                      X, ALU.add).then_inc(sum_done.sem, 1)
                    dve.wait_ge(sum_done.sem, sum_done.at(c, p + 1))
                    dve.reciprocal(sm[:, p % 2, 2], sm[:, p % 2, 1]).then_inc(rec_done.sem, 1)
                    if p + 1 < NP:
                        values(p + 1)
                    if not last and p in (1, 2):
                        tok_add(c + 1, p - 1)
                    if not last and p == 3:
                        dve.wait_ge(h0_done.sem, h0_done.at(c + 1, 2))
                        plain(dve)
                        norm_dve(dve, c + 1, c * NP + NP)
                    dve.wait_ge(c_a.sem, c_a.at(c, p + 1))
                    dve.scalar_tensor_tensor(uc[:], banks[0:RT, 7, D:2 * D], const[0:RT, C_MAB + 1:C_MAB + 2],
                                             uc[:], ALU.mult, ALU.add).then_inc(c_b.sem, 1)
                    dve.wait_ge(c_b.sem, c_b.at(c, p + 1))
                    dve.wait_ge(rec_done.sem, rec_done.at(c, p + 1))
                    u3 = uc[:].rearrange("q (h d) -> q h d", h=NH)
                    dve.tensor_tensor(u3, u3, sm[:, p % 2, 2].unsqueeze(2).to_broadcast([RT, NH, HD]),
                                      ALU.mult).then_inc(c_n.sem, 1)
                    dve.wait_ge(c_n.sem, c_n.at(c, p + 1))
                    dve.wait_ge(vb_done.sem, vb_done.at(c, 1))
                    dve.tensor_tensor(h1(c * NP + p), h1(c * NP + p), uc[:], ALU.add).then_inc(c_h.sem, 1)
                if last:
                    dve.wait_ge(c_h.sem, c_h.at(c, NP))
                    norm_dve(dve, NC, 0)
                    norm_dve2(dve, NC, 0, xn[:, 0])
                    finish(NC, 0, False)
                else:
                    norm_dve2(dve, c + 1, c * NP + NP, xn[:, XU])
                    finish(c + 1, XU, True)
                    repeat_x(c + 1)

            for i in range(2):
                tok_add(0, i)
            dve.wait_ge(h0_done.sem, h0_done.at(0, 2))
            norm_dve(dve, 0, 0)
            norm_dve2(dve, 0, 0, xn[:, XU])
            finish(0, XU, True)
            repeat_x(0)
            with dve.Fori(0, NC - 1) as c:
                chunk(c)
            chunk(NC - 1, True)

        @block.tensor
        def _(pe):
            def tok(n, tiles):
                for p in tiles:
                    out = banks[0:RT, p // 2, D * (p % 2):D * (p % 2) + D]
                    if p == 0:
                        pe.wait_ge(x_hi.sem, x_hi.at(n, 1))
                        pe.wait_ge(x_lo.sem, x_lo.at(n, 1))
                        pe.wait_ge(PREP["xl"].sem, PREP["xl"].at(n, 0))
                        pe.wait_ge(PREP["rl"].sem, PREP["rl"].at(n, 0))
                    for k in range(KP):
                        s = slice(k * NT + p * RT, k * NT + (p + 1) * RT)
                        w = slice(k * D, (k + 1) * D)
                        pe.matmul(out, xsh[:, s], wt_h[:, w], start=(k == 0), stop=False)
                        pe.matmul(out, xsh[:, s], wt_l[:, w], start=False, stop=False)
                        mm = pe.matmul(out, xsl[:, s], wt_h[:, w], start=False, stop=(k == KP - 1))
                    if p % 2:
                        mm.then_inc(tok_done.sem, 1)

            def finish(n, u):
                turn_pe(pe, n, xn[:, u], 0)
                turn_rest_pe(pe, n, xn[:, u], 1)

            def chunk(c, last=False):
                turned_wait(pe, c)
                for i in range(2):
                    t = slice(PH * i, PH * (i + 1))
                    b = [w[:, o + 128 * i:o + 128 * i + 128] for o in (0, 256) for w in (w0h, w0l)]
                    mm = split_pass(pe, banks[:, 2, 0:PH], b, (xh[:, XU, t], xl[:, XU, t], xr[:, XU, t]), i == 0, i == 1)
                mm.then_inc(lat_done.sem, 1)
                pe.wait_ge(lat_ev.sem, lat_ev.at(c, 3))
                pe.wait_ge(c_h.sem, c_h.at(c, 0))
                for hd in range(NH):
                    mm = pe.matmul(banks[:, 4 + hd // GH, PH * (hd % GH):PH * (hd % GH) + PH],
                                   mbd[:, hd, :], lat[:], start=True, stop=True)
                    if hd % GH == GH - 1:
                        mm.then_inc(u_done.sem, 1)

                def scores(p):
                    if p >= 2:
                        pe.wait_ge(sub_done.sem, sub_done.at(c, p - 1))
                    pe.matmul(banks[0:RT, 4 + p % 2, 0:NH * NTOK], lbd[:, p, :], uh[:, p],
                              start=True, stop=True).then_inc(s_done.sem, 1)

                def values(p):
                    if p:
                        pe.wait_ge(v_ev.sem, v_ev.at(c, p))
                    for i in range(2):
                        x0, x1, x2 = (xrep[:, k, NP * i + p, :] for k in range(3))
                        H, L, RH, RL = (w[:, o:o + D] for o in (512, 512 + D) for w in (w0h, w0l))
                        seq = [(x0, H), (x0, L), (x2, RH), (x2, RL), (x1, H)]
                        for k, (st, m) in enumerate(seq):
                            mm = pe.matmul(banks[0:VR, 3, D * i:D * i + D], st, m, start=(k == 0), stop=(k == 4))
                    mm.then_inc(v_done.sem, 1)

                pe.wait_ge(u_ev.sem, u_ev.at(c, 4))
                scores(0)
                for r in rep_done:
                    pe.wait_ge(r.sem, r.at(c, 1))
                values(0)
                for p in range(NP):
                    if p + 1 < NP:
                        scores(p + 1)
                        values(p + 1)
                    if not last and p in (1, 2):
                        tok(c + 1, (2 * p - 2, 2 * p - 1))
                    pe.wait_ge(e_done.sem, e_done.at(c, p + 1))
                    if p:
                        pe.wait_ge(pt_ev.sem, pt_ev.at(c, p))
                    for g in range(NG):
                        mm = pe.transpose(banks[0:VR, 6, RT * g:RT * g + RT],
                                          sx[:, p % 2, VR * g:VR * (g + 1)], ident[0:RT, 0:RT])
                    mm.then_inc(pt_done.sem, 1)
                    pe.wait_ge(pt_ev.sem, pt_ev.at(c, p + 1))
                    pe.wait_ge(v_ev.sem, v_ev.at(c, p + 1))
                    if p:
                        pe.wait_ge(c_b.sem, c_b.at(c, p))
                    out = banks[0:RT, 7, 0:2 * D].rearrange("q (i g f) -> q i g f", i=2, g=NG)
                    vv = vbd[:, p % 2].rearrange("q (i g f) -> q i g f", i=2, g=NG)
                    for g in range(NG):
                        mm = pe.matmul(out[:, :, g, :], pts[:, p % 2, g, :], vv[:, :, g, :], start=True, stop=True)
                    mm.then_inc(c_done.sem, 1)
                if last:
                    finish(NC, 0)
                else:
                    finish(c + 1, XU)

            pe.wait_ge(lo_done, len(tok_p))
            tok(0, range(NP))
            pe.wait_ge(const_in, N_CONST)
            finish(0, XU)
            pe.wait_ge(setup, 11)
            pe.wait_ge(lo_done, len(tok_p) + len(att0_p))
            with pe.Fori(0, NC - 1) as c:
                chunk(c)
            chunk(NC - 1, True)

    MISC, GB = 7, 6

    def gates_dve(dve, S, c, part, first_layer):
        lg, ex, pr, tp = (rt[:, i, :, 0:8] for i in range(4))
        m0, m1 = rt[:, 4, :, 0:8], rt[:, 5, :, 0:8]
        idf = rt[:, 6, :, 0:2]
        one = [rt[:, 7, :, i:i + 1] for i in range(6)]
        count = S["count"]

        def step(ins, wait=True):
            count[0] += 1
            ins.then_inc(S["gv"].sem, 1)
            if wait:
                dve.wait_ge(S["gv"].sem, S["gv"].at(c, count[0]))

        def w8(v):
            return v.to_broadcast([RT, NP, 8])

        if part == 0:
            count[0] = 0
            lp = banks[0:RT, MISC, 0:NP * 10].rearrange("q (p e) -> q p e", p=NP)
            dve.wait_ge(S["lg"].sem, S["lg"].at(c, 1))
            if first_layer:
                b2 = pack[0:RT, K_B2:K_B2 + E0].unsqueeze(1).to_broadcast([RT, NP, 8])
                step(dve.tensor_tensor(lg, lp[:, :, 0:8], b2, ALU.add))
            else:
                step(dve.tensor_scalar(one[4], lp[:, :, 8:9], pack[0:RT, K_SGB:K_SGB + 1], -1.0, ALU.add, ALU.mult), False)
                step(dve.tensor_copy(lg, lp[:, :, 0:8]))
            plain(dve)
            for p in range(NP):
                step(dve.max(tp[:, p, :], lg[:, p, :]), False)
            dve.wait_ge(S["gv"].sem, S["gv"].at(c, count[0]))
            dve.tensor_tensor(ex, lg, w8(tp[:, :, 0:1]), ALU.subtract).then_inc(S["gs"].sem, 1)
            for p in range(NP):
                step(dve.max_index(ri[:, p, :], tp[:, p, :], lg[:, p, :]), False)
        if part == 1:
            io = const[0:RT, C_IOTA:C_IOTA + 8].unsqueeze(1).to_broadcast([RT, NP, 8])
            dve.wait_ge(S["gv"].sem, S["gv"].at(c, count[0]))
            step(dve.tensor_copy(idf, ri[:, :, 0:2]))
            step(dve.tensor_tensor(m0, io, w8(idf[:, :, 0:1]), ALU.is_equal), False)
            step(dve.tensor_tensor(m1, io, w8(idf[:, :, 1:2]), ALU.is_equal))
            step(dve.tensor_tensor(m0, m0, m1, ALU.add))
        if part == 2:
            dve.wait_ge(S["ge"].sem, S["ge"].at(c, 1))
            step(dve.tensor_reduce(one[0], ex, X, ALU.add))
            step(dve.reciprocal(one[1], one[0]))
            step(dve.tensor_tensor(pr, ex, w8(one[1]), ALU.mult))
            step(dve.tensor_tensor(pr, pr, m0, ALU.mult))
            step(dve.tensor_reduce(one[2], pr, X, ALU.add))
            if first_layer:
                step(dve.tensor_scalar(one[2], one[2], 1e-8, None, ALU.add))
            step(dve.reciprocal(one[3], one[2]))
            if not first_layer:
                step(dve.tensor_scalar(one[4], one[4], 1.0, None, ALU.add))
                step(dve.reciprocal(one[5], one[4]))
                step(dve.tensor_scalar(one[4], one[5], -1.0, 1.0, ALU.mult, ALU.add))
                step(dve.tensor_tensor(one[3], one[3], one[4], ALU.mult))
            for i in range(2):
                dve.tensor_tensor(gx[:, :, 32 * i:32 * i + 8], pr, w8(one[3]), ALU.mult).then_inc(S["gx"].sem, 1)
                if not first_layer:
                    dve.tensor_copy(gx[:, :, 32 * i + 8:32 * i + 9], one[5]).then_inc(S["gx"].sem, 1)
            assert count[0] == S["gv"].per, count[0]

    def gates_act(act, S, c, first_layer):
        act.wait_ge(S["gs"].sem, S["gs"].at(c, 1))
        if not first_layer:
            act.activation(rt[:, 7, :, 4:5], rt[:, 7, :, 4:5], ACT.Exp).then_inc(S["ga"].sem, 1)
            act.wait_ge(S["ga"].sem, S["ga"].at(c, 1))
        act.activation(rt[:, 1, :, 0:8], rt[:, 1, :, 0:8], ACT.Exp).then_inc(S["ge"].sem, 1)

    def gates_pe(pe, S, c):
        pe.wait_ge(S["gx"].sem, S["gx"].at(c, S["gx"].per))
        plain(pe)
        for p in range(NP):
            mm = pe.transpose(banks[0:SELW, MISC, RT * p:RT * p + RT], gx[:, p, :], ident[0:RT, 0:RT])
        mm.then_inc(S["gt"].sem, 1)

    def gates_out(dve, S, c, u):
        dve.wait_ge(S["gt"].sem, S["gt"].at(c, 1))
        dve.tensor_copy(gT[:, u], banks[0:SELW, MISC, 0:NT]).then_inc(S["gh"].sem, 1)
        dve.wait_ge(S["gh"].sem, S["gh"].at(c, 1))
        dve.tensor_tensor(gT[32:64, u], banks[32:64, MISC, 0:NT], gT[32:64, u].bitcast(F32),
                          ALU.subtract).then_inc(S["gl"].sem, 1)

    def post_act(act, S, c):
        act.wait_ge(S["dn"].sem, S["dn"].at(c, S["dn"].per))
        for i in range(2):
            act.activation(acc_sb[:, i, :], banks[:, i, 0:NT], ACT.Copy).then_inc(S["ae"].sem, 1)

    POST = (MISC, GB)

    def post_pe(pe, S, c):
        pe.wait_ge(S["ae"].sem, S["ae"].at(c, 2))
        for q in range(2):
            for p in (2 * q, 2 * q + 1):
                t = slice(RT * p, RT * p + RT)
                o = D * (p % 2)
                pe.transpose(banks[0:RT, POST[q], o:o + 128], acc_sb[:, 0, t], ident)
                mm = pe.matmul(banks[0:RT, POST[q], o + 128:o + D], acc_sb[:, 1, t],
                               const[:, C_II:C_II + DR], start=True, stop=True)
            mm.then_inc(S["po"].sem, 1)

    def turned_back(q):
        return banks[0:RT, POST[q], 0:2 * D].rearrange("q (p f) -> q p f", p=2)

    def new_mix(tag, nt, gv, gxn):
        return dict(count=[0], lg=sig(tag + "_logits"), gv=sig(tag + "_gate_steps", gv), gs=sig(tag + "_logits_less_max"),
                    ge=sig(tag + "_gate_exp"), ga=sig(tag + "_alpha_exp"), gx=sig(tag + "_gates", gxn),
                    gt=sig(tag + "_gates_turned"), gh=sig(tag + "_gates_high"), gl=sig(tag + "_gates_low"),
                    hd=sig(tag + "_hidden", nt), ae=sig(tag + "_acc_out", 2),
                    po=sig(tag + "_acc_turned", 2), ph=sig(tag + "_added", 2),
                    z=sig(tag + "_activated", nt), u=sig(tag + "_times_up", nt), g=sig(tag + "_times_gate", nt),
                    zh=sig(tag + "_z_high", nt), zl=sig(tag + "_z_low", nt), dn=sig(tag + "_down_done", nt),
                    gb=sig(tag + "_gate_spread", nt))

    def down_pe(pe, S, c, t, nt, main_h, main_l, rem):
        zz, m = t % 3, slice(128 * t, 128 * t + 128)
        pe.wait_ge(S["zh"].sem, S["zh"].at(c, t + 1))
        if t == 0:
            pe.wait_ge(S["ae"].sem, S["ae"].at(c, 0))
        pe.matmul(banks[:, 0, 0:NT], main_h[:, m], zh[:, zz], start=(t == 0), stop=False)
        pe.matmul(banks[:, 0, 0:NT], main_l[:, m], zh[:, zz], start=False, stop=False)
        pe.matmul(banks[:, 1, 0:NT], rem[:, m], zh[:, zz], start=(t == 0), stop=False)
        pe.wait_ge(S["zl"].sem, S["zl"].at(c, t + 1))
        pe.matmul(banks[:, 0, 0:NT], main_h[:, m], zl[:, zz], start=False, stop=(t == nt - 1))
        pe.matmul(banks[:, 1, 0:NT], rem[:, m], zl[:, zz], start=False, stop=(t == nt - 1)).then_inc(S["dn"].sem, 1)

    def z_high(act, S, c, t):
        act.wait_ge(S["g"].sem, S["g"].at(c, t + 1))
        act.wait_ge(S["dn"].sem, S["dn"].at(c, max(t - 2, 0)))
        act.activation(zh[:, t % 3], zg[:, t % 3], ACT.Copy).then_inc(S["zh"].sem, 1)

    def z_low(pool, S, c, t):
        pool.wait_ge(S["zh"].sem, S["zh"].at(c, t + 1))
        pool.wait_ge(S["dn"].sem, S["dn"].at(c, max(t - 2, 0)))
        pool.tensor_tensor(zl[:, t % 3], zg[:, t % 3], zh[:, t % 3].bitcast(F32), ALU.subtract).then_inc(S["zl"].sem, 1)

    M0 = new_mix("ffn0", T0, 20, 2)
    M0["gb"] = sig("ffn0_gate_spread", E0)
    r1_done, r1_act = sig("router_hidden"), sig("router_gelu")
    fst, fmv, fve, frs, fx, fg = (sig("out_stats", NP), sig("out_meanvar", NP), sig("out_vareps"), sig("out_rstd"),
                                  sig("out_normed", NP), sig("out_gamma"))
    fbeta, fadd, fh = sig("beta_added"), sig("moe_added", 2), sig("ffn0_residual")
    w1 = [w1s[:, i * SZ_W1:(i + 1) * SZ_W1] for i in (0, 2, 1, 3)]
    dn0 = [w[:, o:o + SZ_DN0] for o in (0, SZ_DN0) for w in (big0_h, big0_l)]
    up_h, up_l = big0_h[:, 2 * SZ_DN0:], big0_l[:, 2 * SZ_DN0:]

    sel0_in, sel0_done = sem("early_selectors_in"), sem("early_selectors_rounded")
    sel_stage = uh[0:SELW].rearrange("q a b c -> q (a b c)")[:, 0:E0 * 128]

    def plan(**at):
        return at

    A0 = plan(norm=0, norm2=1, turn=2, turned=3, rest=4, rested=5, router=6, router_act=7, logits=8,
              gates0=9, gexp=10, gates1=10, gates2=11, gturn=12, gout=13)

    with nc.Block() as block:
        @block.sync
        def _(sp):
            start_at_one(sp)
            sp.dma_start(sel_stage, a["sel"][:, 0:E0 * 128]).then_inc(sel0_in, 16)
            load(sp, att1_q)
            with sp.Fori(0, 2) as i:
                load(sp, att1_p, i)

        def ahead(i, u):
            return 2 * i + (u + 1), 2 * NP * i + NP if u == 0 else i * (-2 * NP) + 2 * NP

        @block.gpsimd
        def _(pool):
            low(pool, att1_q)

            def chunk(i, u):
                c = 2 * i + u
                nxt, _ = ahead(i, u)
                for t in range(T0):
                    z_low(pool, M0, c, t)
                    if t == 0:
                        pool.wait_ge(PREP["xn"].sem, PREP["xn"].at(NC + c, NP))
                        pool.tensor_tensor(hc(c * NP), hc(c * NP), row["beta"].unsqueeze(1).to_broadcast([RT, NP, D]),
                                           ALU.add).then_inc(fbeta.sem, 1)
                    if t == A0["norm"]:
                        norm_pool(pool, NC + nxt)
                    if t == 8:
                        low(pool, att1_p[u:u + 1], i)
                pool.wait_ge(fve.sem, fve.at(c, 1))
                pool.tensor_tensor(rstd[:], rstd[:], mhalf[:], ALU.pow).then_inc(frs.sem, 1)

            with pool.Fori(0, 2) as i:
                for u in range(2):
                    chunk(i, u)

        @block.scalar
        def _(act):
            high(act, att1_q)

            def router(n):
                act.wait_ge(r1_done.sem, r1_done.at(n, 1))
                act.activation(g1, banks[0:96, MISC, 0:NT], ACT.Gelu, bias=pack[0:96, K_B1:K_B1 + 1]).then_inc(r1_act.sem, 1)

            def chunk(i, u):
                c = 2 * i + u
                nxt, _ = ahead(i, u)

                def gelu(t):
                    act.wait_ge(M0["hd"].sem, M0["hd"].at(c, t + 1))
                    act.wait_ge(M0["g"].sem, M0["g"].at(c, max(t - 1, 0)))
                    act.activation(zbuf[:, t % 2], banks[:, 2 + t % 3, 0:NT], ACT.Gelu,
                                   bias=pack[:, K_DB + t:K_DB + t + 1]).then_inc(M0["z"].sem, 1)

                gelu(0)
                for t in range(T0):
                    if t + 1 < T0:
                        gelu(t + 1)
                    z_high(act, M0, c, t)
                    if t == A0["norm2"]:
                        norm_act(act, NC + nxt, xn[:, (u + 1) % 2])
                    if t == A0["turned"]:
                        turned_act(act, NC + nxt, (u + 1) % 2, MISC)
                    if t == A0["rested"]:
                        rest_act(act, NC + nxt, (u + 1) % 2, MISC)
                    if t == A0["router_act"]:
                        router(nxt)
                    if t == A0["gexp"]:
                        gates_act(act, M0, nxt, True)
                    if t == 4:
                        high(act, att1_p[u:u + 1], i)
                post_act(act, M0, c)

            router(0)
            gates_act(act, M0, 0, True)
            with act.Fori(0, 2) as i:
                for u in range(2):
                    chunk(i, u)

        @block.vector
        def _(dve):
            dve.wait_ge(sel0_in, 16)
            dve.tensor_copy(sel0[:], sel_stage).then_inc(sel0_done, 1)

            def chunk(i, u):
                c = 2 * i + u
                nxt, tile = ahead(i, u)
                for t in range(T0):
                    dve.wait_ge(M0["z"].sem, M0["z"].at(c, t + 1))
                    dve.wait_ge(M0["gb"].sem, M0["gb"].at(c, t // 2 + 1))
                    dve.wait_ge(M0["zl"].sem, M0["zl"].at(c, max(t - 2, 0)))
                    dve.tensor_tensor(zg[:, t % 3], zbuf[:, t % 2], banks[:, 5 + t // 2 % 2, 0:NT],
                                      ALU.mult).then_inc(M0["g"].sem, 1)
                    if t == A0["norm"]:
                        dve.wait_ge(fh.sem, fh.at(c, 0))
                        plain(dve)
                        norm_dve(dve, NC + nxt, tile)
                    if t == A0["norm2"]:
                        norm_dve2(dve, NC + nxt, tile, xn[:, (u + 1) % 2])
                    if t == A0["turned"]:
                        turned_dve(dve, NC + nxt, (u + 1) % 2, MISC)
                    if t == A0["rested"]:
                        rest_dve(dve, NC + nxt, (u + 1) % 2, MISC)
                    for k in range(3):
                        if t == A0["gates%d" % k]:
                            gates_dve(dve, M0, nxt, k, True)
                    if t == A0["gout"]:
                        gates_out(dve, M0, nxt, (u + 1) % 2)
                for q in range(2):
                    dve.wait_ge(M0["po"].sem, M0["po"].at(c, q + 1))
                    dve.tensor_tensor(y0[:, 2 * q:2 * q + 2, :], turned_back(q),
                                      xn[:, u, 2 * q:2 * q + 2, 0:D], ALU.add).then_inc(fadd.sem, 1)
                for p in range(NP):
                    dve.wait_ge(fadd.sem, fadd.at(c, p // 2 + 1))
                    dve.bn_stats(stats[:, p, :], y0[:, p, :]).then_inc(fst.sem, 1)
                for p in range(NP):
                    dve.wait_ge(fst.sem, fst.at(c, p + 1))
                    plain(dve)
                    dve.bn_aggr(mv[:, p, :], stats[:, p, :]).then_inc(fmv.sem, 1)
                dve.wait_ge(fmv.sem, fmv.at(c, NP))
                dve.tensor_scalar(rstd[:], mv[:, :, 1], EPS, None, ALU.add).then_inc(fve.sem, 1)
                dve.wait_ge(frs.sem, frs.at(c, 1))
                for p in range(NP):
                    dve.tensor_scalar(y0[:, p, :], y0[:, p, :], mv[:, p, 0:1], rstd[:, p:p + 1],
                                      ALU.subtract, ALU.mult).then_inc(fx.sem, 1)
                dve.wait_ge(fx.sem, fx.at(c, NP))
                dve.tensor_tensor(y0, y0, row["gamma"].unsqueeze(1).to_broadcast([RT, NP, D]), ALU.mult).then_inc(fg.sem, 1)
                dve.wait_ge(fg.sem, fg.at(c, 1))
                dve.wait_ge(fbeta.sem, fbeta.at(c, 1))
                dve.tensor_tensor(hc(c * NP), hc(c * NP), y0, ALU.add).then_inc(fh.sem, 1)

            for k in range(3):
                gates_dve(dve, M0, 0, k, True)
            gates_out(dve, M0, 0, 0)
            with dve.Fori(0, 2) as i:
                for u in range(2):
                    chunk(i, u)

        @block.tensor
        def _(pe):
            def router(n, u):
                turned_wait(pe, NC + n)
                split_pass(pe, banks[0:96, MISC, 0:NT], w1, (xh[:, u], xl[:, u], xr[:, u])).then_inc(r1_done.sem, 1)

            def logits(n):
                pe.wait_ge(r1_act.sem, r1_act.at(n, 1))
                for p in range(NP):
                    mm = pe.matmul(banks[0:RT, MISC, 10 * p:10 * p + 8], g1[:, RT * p:RT * p + RT],
                                   pack[0:96, K_W2:K_W2 + E0], start=True, stop=True)
                mm.then_inc(M0["lg"].sem, 1)

            def chunk(i, u):
                c = 2 * i + u
                nxt, _ = ahead(i, u)
                mov = (xh[:, u], xl[:, u], xr[:, u])

                def hidden(t):
                    pe.wait_ge(M0["z"].sem, M0["z"].at(c, max(t - 2, 0)))
                    split_pass(pe, banks[:, 2 + t % 3, 0:NT], [w[:, 128 * t:128 * t + 128] for w in dn0], mov
                               ).then_inc(M0["hd"].sem, 1)

                def spread(e):
                    pe.wait_ge(M0["g"].sem, M0["g"].at(c, max(2 * e - 2, 0)))
                    if e < 2:
                        pe.wait_ge(fadd.sem, fadd.at(c, 0))
                    pe.matmul(banks[:, 5 + e % 2, 0:NT], sel0[:, 128 * e:128 * e + 128], gT[:, u],
                              start=True, stop=True).then_inc(M0["gb"].sem, 1)

                pe.wait_ge(M0["gl"].sem, M0["gl"].at(c, 1))
                hidden(0)
                spread(0)
                hidden(1)
                for t in range(T0 + 1):
                    if t + 2 < T0:
                        hidden(t + 2)
                    if t % 2 == 0 and t // 2 + 1 < E0:
                        spread(t // 2 + 1)
                    if t:
                        down_pe(pe, M0, c, t - 1, T0, up_h, up_l, up0_r)
                    if t == A0["turn"]:
                        pe.wait_ge(fadd.sem, fadd.at(c, 0))
                        turn_pe(pe, NC + nxt, xn[:, (u + 1) % 2], MISC)
                    if t == A0["rest"]:
                        pe.wait_ge(PREP["xl"].sem, PREP["xl"].at(NC + nxt, 1))
                        pe.wait_ge(PREP["xh"].sem, PREP["xh"].at(NC + nxt, 1))
                        turn_rest_pe(pe, NC + nxt, xn[:, (u + 1) % 2], MISC)
                    if t == A0["router"]:
                        router(nxt, (u + 1) % 2)
                    if t == A0["logits"]:
                        logits(nxt)
                    if t == A0["gturn"]:
                        gates_pe(pe, M0, nxt)
                pe.wait_ge(M0["gl"].sem, M0["gl"].at(nxt, 1))
                post_pe(pe, M0, c)

            pe.wait_ge(sel0_done, 1)
            router(0, 0)
            logits(0)
            gates_pe(pe, M0, 0)
            with pe.Fori(0, 2) as i:
                for u in range(2):
                    chunk(i, u)

    first_half.close()

    xn = sb("xn1", [RT, NP, D + DR])
    big1 = sb("big1", [128, 2 * SZ_FFN1 + T1 * 128], F32R)
    rws = sb("rws", [128, 4 * SZ_RT], F32R)
    sel1 = sb("sel1", [SELW, (T1R + 1) * 128], F32R)
    ws = sb("w", [128, QJ, NT])
    sq = sb("w2", [128, QJ, NT])
    wn = sb("wn", [128, QJ, NT])
    o1 = sq
    n2 = sb("n2", [128, QJ, IMG])
    dots = sb("dots", [128, QJ, IMG])
    pq = zbuf[0:NH].rearrange("q a t -> q (a t)")[:, 0:NT + IMG]
    hs = sb("hs", [NH, 3, IMG])

    big1_h, big1_l, dn1_r = big1[:, 0:SZ_FFN1], big1[:, SZ_FFN1:2 * SZ_FFN1], big1[:, 2 * SZ_FFN1:]
    ffn1_q = straight(a["w_rt"], rws[:, 0:2 * SZ_RT], rws[:, 2 * SZ_RT:], 2 * SZ_RT) + \
        side_by_side(a["w_dn1_r"], T1, dn1_r)
    ffn1_p = looped(a["w_ffn1"], big1_h, big1_l, SZ_FFN1, 2, 6)

    S3 = new_mix("att1", QJ, 1, 1)
    w_done, w_cp, w_sq = sig("w_done", QJ), sig("w_copied", QJ), sig("w_squared", QJ)
    n_sum, n_max, n_rec, w_nrm = sig("norm_sum", QJ), sig("norm_guard"), sig("norm_recip"), sig("w_normed", QJ)
    l_done, l_t = sig("token_logits"), sig("token_logits_temp")
    hv, l_sub, l_exp = sig("head_steps", 7), sig("token_less_max"), sig("token_exp")
    pb_done = sig("pi_spread", QJ)
    o_w, o_e, d_sum, d_st = sig("w_pi", QJ), sig("w2_pi", QJ), sig("dots_sum", QJ), sig("dots_steps", QJ + 2)
    d_rec = sig("dots_recip")
    bo_done, att1_h = sig("bout_added"), sig("att1_residual", 2)
    sel_in, sel1_done = sem("selectors_in"), sem("late_selectors_rounded")
    qk = [w[:, o:o + SZ_QKV] for o in (0, SZ_QKV) for w in (mid_h, mid_l)]
    wo_h, wo_l = mid_h[:, 2 * SZ_QKV:], mid_l[:, 2 * SZ_QKV:]
    sel_stage = wn[0:SELW].rearrange("q j t -> q (j t)")[:, 0:(T1R + 1) * 128]

    def img(v):
        return v.rearrange("q (i n) -> q i n", n=NTOK)

    with nc.Block() as block:
        @block.sync
        def _(sp):
            start_at_one(sp)
            sp.dma_start(sel_stage, a["sel"][:, E0 * 128:]).then_inc(sel_in, 16)
            load(sp, ffn1_q)
            with sp.Fori(0, 2) as i:
                load(sp, ffn1_p, i)

        @block.gpsimd
        def _(pool):
            def chunk(i, u):
                c = 2 * i + u
                nxt, _ = ahead(i, u)
                pool.tensor_tensor(hc(c * NP), hc(c * NP), row["bout"].unsqueeze(1).to_broadcast([RT, NP, D]),
                                   ALU.add).then_inc(bo_done.sem, 1)
                norm_pool(pool, 2 * NC + nxt)
                low(pool, ffn1_p[3 * u:3 * u + 1], i)
                for j in range(QJ):
                    pool.wait_ge(o_w.sem, o_w.at(c, j + 1))
                    pool.tensor_tensor(wn[:, j], o1[:, j], ws[:, j], ALU.mult).then_inc(o_e.sem, 1)
                for j in range(QJ):
                    z_low(pool, S3, c, j)
                low(pool, ffn1_p[3 * u + 1:3 * u + 3], i)

            low(pool, ffn1_q)
            with pool.Fori(0, 2) as i:
                for u in range(2):
                    chunk(i, u)

        @block.scalar
        def _(act):
            high(act, ffn1_q)

            def chunk(i, u):
                c = 2 * i + u
                nxt, _ = ahead(i, u)
                for j in range(QJ):
                    act.wait_ge(w_done.sem, w_done.at(c, j + 1))
                    act.wait_ge(S3["g"].sem, S3["g"].at(c, 0))
                    act.activation(ws[:, j], banks[:, 2 + j % 3, 0:NT], ACT.Copy).then_inc(w_cp.sem, 1)
                    act.activation(sq[:, j], banks[:, 2 + j % 3, 0:NT], ACT.Square).then_inc(w_sq.sem, 1)
                high(act, ffn1_p[3 * u:3 * u + 1], i)
                act.wait_ge(l_done.sem, l_done.at(c, 1))
                act.activation(pq[:, 0:NT], banks[0:NH, 4, 0:NT], ACT.Copy, scale=pack[0:NH, K_TEMP:K_TEMP + 1]).then_inc(l_t.sem, 1)
                act.wait_ge(l_sub.sem, l_sub.at(c, 1))
                act.activation(pq[:, 0:NT], pq[:, 0:NT], ACT.Exp).then_inc(l_exp.sem, 1)
                norm_act(act, 2 * NC + nxt, xn)
                turned_act(act, 2 * NC + nxt, (u + 1) % 2, MISC)
                high(act, ffn1_p[3 * u + 1:3 * u + 2], i)
                rest_act(act, 2 * NC + nxt, (u + 1) % 2, MISC)
                for j in range(QJ):
                    z_high(act, S3, c, j)
                post_act(act, S3, c)
                high(act, ffn1_p[3 * u + 2:3 * u + 3], i)

            with act.Fori(0, 2) as i:
                for u in range(2):
                    chunk(i, u)

        @block.vector
        def _(dve):
            dve.wait_ge(sel_in, 16)
            dve.tensor_copy(sel1[:], sel_stage).then_inc(sel1_done, 1)
            dve.wait_ge(sel1_done, 1)

            def chunk(i, u):
                c = 2 * i + u
                nxt, tile = ahead(i, u)
                for j in range(QJ):
                    dve.wait_ge(w_sq.sem, w_sq.at(c, j + 1))
                    dve.tensor_reduce(n2[:, j, :], img(sq[:, j]), X, ALU.add).then_inc(n_sum.sem, 1)
                dve.wait_ge(n_sum.sem, n_sum.at(c, QJ))
                dve.tensor_scalar(n2[:], n2[:], 1e-24, None, ALU.max).then_inc(n_max.sem, 1)
                dve.wait_ge(n_max.sem, n_max.at(c, 1))
                dve.reciprocal(n2[:], n2[:]).then_inc(n_rec.sem, 1)
                dve.wait_ge(n_rec.sem, n_rec.at(c, 1))
                for j in range(QJ):
                    dve.tensor_tensor(img(wn[:, j]), img(sq[:, j]), n2[:, j, :].unsqueeze(2).to_broadcast([128, IMG, NTOK]),
                                      ALU.mult).then_inc(w_nrm.sem, 1)
                dve.wait_ge(att1_h.sem, att1_h.at(c, 0))
                plain(dve)
                norm_dve(dve, 2 * NC + nxt, tile)
                k = [0]

                def link(ins):
                    k[0] += 1
                    ins.then_inc(hv.sem, 1)
                    dve.wait_ge(hv.sem, hv.at(c, k[0]))

                def wide(v):
                    return v.unsqueeze(2).to_broadcast([NH, IMG, NTOK])
                dve.wait_ge(l_t.sem, l_t.at(c, 1))
                link(dve.tensor_reduce(hs[:, 0, :], img(pq[:, 0:NT]), X, ALU.max))
                dve.tensor_tensor(img(pq[:, 0:NT]), img(pq[:, 0:NT]), wide(hs[:, 0, :]), ALU.subtract).then_inc(l_sub.sem, 1)
                norm_dve2(dve, 2 * NC + nxt, tile, xn)
                dve.wait_ge(l_exp.sem, l_exp.at(c, 1))
                link(dve.tensor_reduce(hs[:, 1, :], img(pq[:, 0:NT]), X, ALU.add))
                link(dve.reciprocal(hs[:, 2, :], hs[:, 1, :]))
                link(dve.tensor_tensor(img(pq[:, 0:NT]), img(pq[:, 0:NT]), wide(hs[:, 2, :]), ALU.mult))
                link(dve.tensor_reduce(hs[:, 1, :], img(pq[:, 0:NT]), X, ALU.add))
                link(dve.tensor_scalar(hs[:, 1, :], hs[:, 1, :], 1e-8, None, ALU.add))
                link(dve.reciprocal(pq[:, NT:NT + IMG], hs[:, 1, :]))

                def dot(j):
                    dve.wait_ge(o_e.sem, o_e.at(c, j + 1))
                    dve.tensor_reduce(n2[:, j, :], img(wn[:, j]), X, ALU.add).then_inc(d_sum.sem, 1)

                for j in range(QJ):
                    dve.wait_ge(pb_done.sem, pb_done.at(c, j + 1))
                    dve.tensor_tensor(o1[:, j], ws[:, j], banks[:, 4 + j % 2, 0:NT], ALU.mult).then_inc(o_w.sem, 1)
                    dve.tensor_copy(dots[:, j, :], banks[:, 4 + j % 2, NT:NT + IMG]).then_inc(d_st.sem, 1)
                    if j == 2:
                        turned_dve(dve, 2 * NC + nxt, (u + 1) % 2, MISC)
                    if j >= 2:
                        dot(j - 2)
                rest_dve(dve, 2 * NC + nxt, (u + 1) % 2, MISC)
                dot(QJ - 2)
                dot(QJ - 1)
                dve.wait_ge(d_sum.sem, d_sum.at(c, QJ))
                dve.wait_ge(d_st.sem, d_st.at(c, QJ))
                dve.tensor_tensor(n2[:], n2[:], dots[:], ALU.mult).then_inc(d_st.sem, 1)
                dve.wait_ge(d_st.sem, d_st.at(c, QJ + 1))
                dve.tensor_scalar(n2[:], n2[:], 1.0, -1.0, ALU.add, ALU.mult).then_inc(d_st.sem, 1)
                dve.wait_ge(d_st.sem, d_st.at(c, QJ + 2))
                dve.reciprocal(n2[:], n2[:]).then_inc(d_rec.sem, 1)
                dve.wait_ge(d_rec.sem, d_rec.at(c, 1))
                for j in range(QJ):
                    dve.wait_ge(S3["zl"].sem, S3["zl"].at(c, max(j - 2, 0)))
                    dve.tensor_tensor(img(zg[:, j % 3]), img(o1[:, j]), n2[:, j, :].unsqueeze(2).to_broadcast([128, IMG, NTOK]),
                                      ALU.mult).then_inc(S3["g"].sem, 1)
                dve.wait_ge(bo_done.sem, bo_done.at(c, 1))
                for q in range(2):
                    dve.wait_ge(S3["po"].sem, S3["po"].at(c, q + 1))
                    dve.tensor_tensor(hc(c * NP + 2 * q, 2), hc(c * NP + 2 * q, 2), turned_back(q), ALU.add).then_inc(att1_h.sem, 1)

            with dve.Fori(0, 2) as i:
                for u in range(2):
                    chunk(i, u)

        @block.tensor
        def _(pe):
            def chunk(i, u):
                c = 2 * i + u
                nxt, _ = ahead(i, u)
                mov = (xh[:, u], xl[:, u], xr[:, u])
                turned_wait(pe, 2 * NC + c)
                for j in range(QJ):
                    if j >= 3:
                        pe.wait_ge(w_sq.sem, w_sq.at(c, j - 2))
                    split_pass(pe, banks[:, 2 + j % 3, 0:NT], [w[:, 128 * j:128 * j + 128] for w in qk], mov
                               ).then_inc(w_done.sem, 1)
                pe.wait_ge(w_sq.sem, w_sq.at(c, QJ))
                for j in range(QJ):
                    pe.wait_ge(w_nrm.sem, w_nrm.at(c, j + 1))
                    mm = pe.matmul(banks[0:NH, 4, 0:NT], const[:, C_B + NH * j:C_B + NH * (j + 1)], wn[:, j],
                                   start=(j == 0), stop=(j == QJ - 1))
                mm.then_inc(l_done.sem, 1)
                pe.wait_ge(att1_h.sem, att1_h.at(c, 0))
                turn_pe(pe, 2 * NC + nxt, xn, MISC)
                pe.wait_ge(hv.sem, hv.at(c, 7))
                for j in range(QJ):
                    if j >= 2:
                        pe.wait_ge(d_st.sem, d_st.at(c, j - 1))
                    pe.matmul(banks[:, 4 + j % 2, 0:NT + IMG], const[0:NH, C_SB + 128 * j:C_SB + 128 * (j + 1)],
                              pq, start=True, stop=True).then_inc(pb_done.sem, 1)
                pe.wait_ge(PREP["xl"].sem, PREP["xl"].at(2 * NC + nxt, 1))
                turn_rest_pe(pe, 2 * NC + nxt, xn, MISC)
                for j in range(QJ):
                    down_pe(pe, S3, c, j, QJ, wo_h, wo_l, wo_r)
                pe.wait_ge(PREP["rl"].sem, PREP["rl"].at(2 * NC + nxt, 1))
                post_pe(pe, S3, c)

            with pe.Fori(0, 2) as i:
                for u in range(2):
                    chunk(i, u)

    M1 = new_mix("ffn1", T1, 24, 4)
    out_done = sem("stored")
    rw = [rws[:, i * SZ_RT:(i + 1) * SZ_RT] for i in (0, 2, 1, 3)]
    gu = [w[:, o:o + SZ_GU] for o in (0, SZ_GU) for w in (big1_h, big1_l)]
    dn_h, dn_l = big1_h[:, 2 * SZ_GU:], big1_l[:, 2 * SZ_GU:]
    A1 = plan(norm=0, norm2=1, turn=2, turned=3, rest=4, rested=5, logits=6, gates0=8, gexp=9, gates1=10,
              gates2=11, gturn=12, gout=13)

    with nc.Block() as block:
        @block.sync
        def _(sp):
            start_at_one(sp)
            for c in range(NC):
                sp.wait_ge(M1["ph"].sem, M1["ph"].at(c, 2))
                sp.dma_start(a["out"][c], h[:, c * NP:(c + 1) * NP, :]).then_inc(out_done, 16)
            sp.wait_ge(out_done, 16 * NC)

        @block.gpsimd
        def _(pool):
            def chunk(i, u):
                for t in range(T1):
                    z_low(pool, M1, 2 * i + u, t)
                    if t == A1["norm"]:
                        norm_pool(pool, 3 * NC + ahead(i, u)[0])

            with pool.Fori(0, 2) as i:
                for u in range(2):
                    chunk(i, u)

        @block.scalar
        def _(act):
            def chunk(i, u):
                c = 2 * i + u
                nxt, _ = ahead(i, u)

                def silu(t):
                    act.wait_ge(M1["hd"].sem, M1["hd"].at(c, t + 1))
                    act.wait_ge(M1["u"].sem, M1["u"].at(c, max(t - 1, 0)))
                    act.activation(zbuf[:, t % 2], banks[:, 2 + t % 2, 0:NT], ACT.Silu).then_inc(M1["z"].sem, 1)

                silu(0)
                for t in range(T1):
                    if t + 1 < T1:
                        silu(t + 1)
                    z_high(act, M1, c, t)
                    if t == A1["norm2"]:
                        norm_act(act, 3 * NC + nxt, xn)
                    if t == A1["turned"]:
                        turned_act(act, 3 * NC + nxt, (u + 1) % 2, MISC)
                    if t == A1["rested"]:
                        rest_act(act, 3 * NC + nxt, (u + 1) % 2, MISC)
                    if t == A1["gexp"]:
                        gates_act(act, M1, nxt, False)
                post_act(act, M1, c)

            gates_act(act, M1, 0, False)
            with act.Fori(0, 2) as i:
                for u in range(2):
                    chunk(i, u)

        @block.vector
        def _(dve):
            def chunk(i, u):
                c = 2 * i + u
                nxt, tile = ahead(i, u)
                for t in range(T1):
                    zz = t % 3
                    dve.wait_ge(M1["z"].sem, M1["z"].at(c, t + 1))
                    dve.wait_ge(M1["zl"].sem, M1["zl"].at(c, max(t - 2, 0)))
                    dve.tensor_tensor(zg[:, zz], zbuf[:, t % 2], banks[:, 4 + t % 2, 0:NT], ALU.mult).then_inc(M1["u"].sem, 1)
                    dve.wait_ge(M1["u"].sem, M1["u"].at(c, t + 1))
                    dve.wait_ge(M1["gb"].sem, M1["gb"].at(c, t + 1))
                    dve.tensor_tensor(zg[:, zz], zg[:, zz], banks[:, GB, 0:NT], ALU.mult).then_inc(M1["g"].sem, 1)
                    if t == A1["norm"]:
                        dve.wait_ge(M1["ph"].sem, M1["ph"].at(c, 0))
                        plain(dve)
                        norm_dve(dve, 3 * NC + nxt, tile)
                    if t == A1["norm2"]:
                        norm_dve2(dve, 3 * NC + nxt, tile, xn)
                    if t == A1["turned"]:
                        turned_dve(dve, 3 * NC + nxt, (u + 1) % 2, MISC)
                    if t == A1["rested"]:
                        rest_dve(dve, 3 * NC + nxt, (u + 1) % 2, MISC)
                    for k in range(3):
                        if t == A1["gates%d" % k]:
                            gates_dve(dve, M1, nxt, k, False)
                    if t == A1["gout"]:
                        gates_out(dve, M1, nxt, (u + 1) % 2)
                for q in range(2):
                    dve.wait_ge(M1["po"].sem, M1["po"].at(c, q + 1))
                    dve.tensor_tensor(hc(c * NP + 2 * q, 2), hc(c * NP + 2 * q, 2), turned_back(q), ALU.add).then_inc(M1["ph"].sem, 1)

            for k in range(3):
                gates_dve(dve, M1, 0, k, False)
            gates_out(dve, M1, 0, 0)
            with dve.Fori(0, 2) as i:
                for u in range(2):
                    chunk(i, u)

        @block.tensor
        def _(pe):
            def logits(n, u):
                turned_wait(pe, 3 * NC + n)
                H, L, RH, RL = rw
                for p in range(NP):
                    t = slice(RT * p, RT * p + RT)
                    seq = [(xh, H), (xh, L), (xr, RH), (xr, RL), (xl, H)]
                    for k, (st, m) in enumerate(seq):
                        mm = pe.matmul(banks[0:RT, MISC, 10 * p:10 * p + 10], st[:, u, t], m, start=(k == 0), stop=(k == 4))
                mm.then_inc(M1["lg"].sem, 1)

            def chunk(i, u):
                c = 2 * i + u
                nxt, _ = ahead(i, u)
                mov = (xh[:, u], xl[:, u], xr[:, u])

                def hidden(t):
                    pe.wait_ge(M1["u"].sem, M1["u"].at(c, max(t - 1, 0)))
                    for k in range(2):
                        mm = split_pass(pe, banks[:, 2 + 2 * k + t % 2, 0:NT],
                                        [w[:, 256 * t + 128 * k:256 * t + 128 * k + 128] for w in gu], mov)
                    mm.then_inc(M1["hd"].sem, 1)

                def spread(t):
                    e = min(t, T1R)
                    if t:
                        pe.wait_ge(M1["g"].sem, M1["g"].at(c, t))
                    else:
                        pe.wait_ge(M1["ph"].sem, M1["ph"].at(c, 0))
                    pe.matmul(banks[:, GB, 0:NT], sel1[:, 128 * e:128 * e + 128], gT[:, u],
                              start=True, stop=True).then_inc(M1["gb"].sem, 1)

                pe.wait_ge(M1["gl"].sem, M1["gl"].at(c, 1))
                hidden(0)
                spread(0)
                for t in range(T1 + 1):
                    if t + 1 < T1:
                        hidden(t + 1)
                        spread(t + 1)
                    if t:
                        down_pe(pe, M1, c, t - 1, T1, dn_h, dn_l, dn1_r)
                    if t == A1["turn"]:
                        turn_pe(pe, 3 * NC + nxt, xn, MISC)
                    if t == A1["rest"]:
                        pe.wait_ge(PREP["xl"].sem, PREP["xl"].at(3 * NC + nxt, 1))
                        turn_rest_pe(pe, 3 * NC + nxt, xn, MISC)
                    if t == A1["logits"]:
                        logits(nxt, (u + 1) % 2)
                    if t == A1["gturn"]:
                        gates_pe(pe, M1, nxt)
                pe.wait_ge(M1["gl"].sem, M1["gl"].at(nxt, 1))
                post_pe(pe, M1, c)

            logits(0, 0)
            gates_pe(pe, M1, 0)
            with pe.Fori(0, 2) as i:
                for u in range(2):
                    chunk(i, u)


def constants(np):
    c = np.zeros((128, C_ALL), np.float32)
    c[:, C_ID:C_ID + 128] = np.eye(128)
    c[:, C_II:C_II + DR] = np.tile(np.eye(DR), (2, 1))
    for j in range(QJ):
        for q in range(128):
            c[q, C_B + NH * j + 2 * j + q // 64] = 1
            c[2 * j + q // 64, C_SB + 128 * j + q] = 1
    for q in range(VR):
        c[q, C_VM + q // NTOK] = 1
    c[0:NTOK, C_MAB] = 1
    c[NTOK:RT, C_MAB + 1] = 1
    c[:, C_IOTA:C_IOTA + E0] = np.arange(E0)
    return c


def selectors(np):
    s = np.zeros((SELW, NSEL), np.float32)
    for n in range(NSEL):
        t, m = divmod(n, 128)
        e = t if t < E0 else ((128 * (t - E0) + m) // D if t - E0 < T1R else E0)
        s[e, n] = s[32 + e, n] = 1
    return s


def kernel(**inputs):
    import numpy as np
    import concourse.bacc as bacc
    from concourse.bass_utils import run_bass_kernel_spmd as run

    i = {k: np.asarray(v) for k, v in inputs.items()}
    cat = np.concatenate

    def twice(w):
        return cat([w, w], 0)

    x = i["x"].reshape(NI, 6, 16, 6, 16, 3).transpose(0, 1, 3, 2, 4, 5).reshape(NI, 36, 768)
    x = cat([np.zeros((NI, 1, 768), np.float32), x], 1)
    x = x.reshape(NC, IMG * NTOK, KP, 128).transpose(0, 3, 2, 1).reshape(NC * 128, KP * NT)

    def tiles(w):
        return w.reshape(-1, 128, w.shape[1]).transpose(1, 0, 2)

    basis = i["L0_attn_basis_w"].T
    z = np.zeros_like(basis)
    basis = cat([basis, z, z, basis], 1)
    val = i["L0_attn_value_w"].T
    dn0 = i["L0_ffn_down_w"].transpose(1, 0, 2).reshape(D, T0 * 128)
    up0 = tiles(i["L0_ffn_up_w"].reshape(T0 * 128, D))
    wo = tiles(i["L1_attn_w_out"])
    qkv = i["L1_attn_w_qkv"]
    gate = cat([i["L1_ffn_w_gate"].transpose(1, 0, 2).reshape(D, -1), i["L1_ffn_ws_gate"]], 1)
    up = cat([i["L1_ffn_w_up"].transpose(1, 0, 2).reshape(D, -1), i["L1_ffn_ws_up"]], 1)
    gu = np.stack([gate.reshape(D, T1, 128), up.reshape(D, T1, 128)], 2).reshape(D, SZ_GU)
    dn1 = tiles(cat([i["L1_ffn_w_down"].reshape(-1, D), i["L1_ffn_ws_down"]], 0))
    rt = cat([i["L1_ffn_router_w"], i["L1_ffn_sg_w"], np.zeros((D, 1), np.float32)], 1)
    pack = np.zeros((128, K_ALL), np.float32)
    pack[0:RT, K_ROWS:K_ROWS + D] = np.tile(i["L0_tok_pos_embedding"].reshape(NTOK, D), (2, 1))
    proj = np.tile(i["L0_tok_b_proj"], (NTOK, 1))
    proj[0] = i["L0_tok_cls_token"].reshape(D)
    for k, v in enumerate([np.tile(proj, (2, 1)), i["L0_attn_value_b"], i["L0_ffn_gamma"], i["L0_ffn_beta"],
                           i["L1_attn_b_out"]], 1):
        pack[0:RT, K_ROWS + D * k:K_ROWS + D * (k + 1)] = v
    pack[0:RT, K_B2:K_B2 + E0] = i["L0_ffn_b2"]
    pack[0:RT, K_SGB] = i["L1_ffn_sg_b"][0]
    pack[0:96, K_B1] = i["L0_ffn_b1"]
    pack[:, K_DB:K_DB + T0] = i["L0_ffn_down_b"].reshape(T0, 128).T
    pack[0:96, K_W2:K_W2 + E0] = i["L0_ffn_w2"]
    pack[0:NH, K_TEMP:K_TEMP + 1] = i["L1_attn_temp"].reshape(NH, 1)

    def k192(w):
        return cat([w[0:128], twice(w[128:])], 1)

    def main(w):
        return w[:, :, 0:128].reshape(128, -1)

    def rest(w):
        return w[:, :, 128:].reshape(128, -1)

    arrays = {
        "const": constants(np), "sel": selectors(np), "pack": pack, "patches": x,
        "w_tok": tiles(i["L0_tok_W_proj"]).reshape(128, -1),
        "w_att0": cat([k192(basis), k192(val)], 1),
        "w_ffn0": cat([k192(dn0), main(up0)], 1), "w_up0_r": rest(up0), "w_w1": k192(i["L0_ffn_w1"]),
        "w_att1": cat([k192(qkv), main(wo)], 1), "w_wo_r": rest(wo),
        "w_ffn1": cat([k192(gu), main(dn1)], 1), "w_dn1_r": rest(dn1), "w_rt": k192(rt),
        "hrt": twice(cat([i["L0_attn_head_residual"].transpose(2, 0, 1).reshape(RK, NH * RK), i["L0_attn_core"].T], 1)),
    }
    nc = bacc.Bacc("TRN2", target_bir_lowering=False, num_devices=1)
    fed, a = {}, {}
    for name, v in arrays.items():
        v = np.ascontiguousarray(v)
        fed["in_" + name] = v
        a[name] = nc.dram_tensor("in_" + name, v.shape, F32, kind="ExternalInput").ap()
    a["out"] = nc.dram_tensor("out_0", (NC, RT, NP, D), F32, kind="ExternalOutput").ap()
    tower(nc, a)
    r = run(nc, [fed], core_ids=[0])
    got = r.results[0]["out_0"]
    return got.transpose(0, 2, 1, 3).reshape(NI, NTOK, D)
```

```python
from contextlib import ExitStack

import concourse.bass as bass
from concourse import mybir

F32 = mybir.dt.float32
F32R = mybir.dt.float32r
U32 = mybir.dt.uint32
ALU = mybir.AluOpType
ACT = mybir.ActivationFunctionType
X = mybir.AxisListType.X

D = 192
DR = D - 128
NI, NTOK = 32, 37
NC, NP = 4, 4
RT = 2 * NTOK
NT = NP * RT
IMG = 2 * NP
KP = 6
NH, HD, RK = 12, 16, 64
NG, GH = 4, 3
VR = GH * NTOK
E0, T0 = 8, 16
T1R, T1 = 12, 18
QJ = 6
EPS = 1e-5
RING0, RING1 = 4, 3
SELW = 64

C_ID, C_II = 0, 128
C_B = C_II + DR
C_SB = C_B + QJ * NH
C_VM = C_SB + QJ * 128
C_MAB = C_VM + GH
C_IOTA = C_MAB + 2
C_ALL = C_IOTA + E0

NSEL = (E0 + T1R + 1) * 128

ROWS = ["pos", "bproj", "vb", "gamma", "beta", "bout"]
K_ROWS = 0
K_B2 = K_ROWS + len(ROWS) * D
K_SGB = K_B2 + E0
K_B1 = K_SGB + 1
K_DB = K_B1 + 1
K_W2 = K_DB + T0
K_TEMP = K_W2 + E0
K_ALL = K_TEMP + 1

SZ_TOK = KP * D
SZ_ATT0 = 2 * 128 + 2 * D
SZ_DN0 = T0 * 128
SZ_FFN0 = 3 * SZ_DN0
SZ_W1 = 96
SZ_QKV = QJ * 128
SZ_ATT1 = 3 * SZ_QKV
SZ_GU = 2 * T1 * 128
SZ_FFN1 = 2 * SZ_GU + T1 * 128
SZ_RT = 10
WST = 1024


STARTS_AT_ONE = {
    "att1_acc_out", "beta_added", "att1_down_done", "att1_residual", "att1_times_gate", "att1_z_low", "ctx_added",
    "ctx_done", "ffn0_acc_out", "ffn0_activated", "ffn0_down_done", "ffn0_residual",
    "ffn0_times_gate", "ffn0_z_low", "ffn1_acc_out", "ffn1_added", "ffn1_down_done",
    "ffn1_times_up", "ffn1_z_low", "moe_added", "norm_xl", "norm_xr_low", "probs_turned",
    "tok_done",
}


class Signal:

    def __init__(self, take, name, per=1, base=0):
        self.take, self.name, self.per, self.held, self.base = take, name, per, None, base

    @property
    def sem(self):
        if self.held is None:
            self.held = self.take(self.name)
        return self.held

    def at(self, c, k):
        assert self.base + k > 0, self.name
        return c * self.per + (self.base + k)


def tower(nc, a):
    with ExitStack() as ctx:
        body(nc, a, ctx)


def body(nc, a, ctx):
    first_half = ctx.enter_context(ExitStack())

    def sb(name, shape, dt=F32, where=ctx):
        return where.enter_context(nc.sbuf_tensor(name, shape, dt))

    def sem(name):
        return ctx.enter_context(nc.semaphore(name))

    def sig(name, per=1):
        s = Signal(sem, name, per, int(name in STARTS_AT_ONE))
        if s.base:
            ones.append(s)
        return s

    ones = []

    def start_at_one(sp):
        while ones:
            sp.sem_inc(ones.pop().sem, 1)

    banks = ctx.enter_context(nc.psum_tensor("banks", [128, 8, 512], F32))

    const = sb("const", [128, C_ALL])
    ident = const[:, C_ID:C_ID + 128]
    pack = sb("pack", [128, K_ALL])
    rows = pack[0:RT, K_ROWS:K_ROWS + 6 * D].rearrange("q (i f) -> q i f", i=6)
    row = {n: rows[:, i, :] for i, n in enumerate(ROWS)}
    h = sb("h", [RT, NC * NP, D])
    stats = sb("stats", [RT, NP, 6])
    mv = sb("mv", [RT, NP, 2])
    rstd = sb("rstd", [RT, NP])
    mhalf = sb("mhalf", [RT, NP])
    xh = sb("xh", [128, 2, NT], F32R)
    xl = sb("xl", [128, 2, NT], F32R)
    xr = sb("xr", [128, 2, NT], F32R)
    gT = sb("gT", [SELW, 2, NT], F32R)
    gx = sb("gx", [RT, NP, SELW])
    rt = sb("rt", [RT, 8, NP, 10])
    ri = sb("ri", [RT, NP, 8], U32)
    wstage = sb("wstage", [128, 2, WST])
    zbuf = sb("zbuf", [128, 2, NT])
    acc_sb = sb("acc_sb", [128, 2, NT])
    mid = sb("mid", [128, 2 * SZ_ATT1 + QJ * 128], F32R)

    zh = sb("zh0", [128, RING0, NT], F32R, first_half)
    zl = sb("zl0", [128, RING0, NT], F32R, first_half)
    xn = sb("xn", [RT, 2, NP, D + DR], where=first_half)
    sel0 = sb("sel0", [SELW, E0 * 128], F32R, first_half)
    wtok = sb("wtok", [128, 2 * SZ_TOK + 2 * SZ_ATT0], F32R, first_half)
    big0 = sb("big0", [128, 2 * SZ_FFN0 + T0 * 128], F32R, first_half)
    w1s = sb("w1s", [128, 4 * SZ_W1], F32R, first_half)
    xs = sb("xs", [128, KP * NT], where=first_half)
    xsh = sb("xsh", [128, KP * NT], F32R, first_half)
    xsl = sb("xsl", [128, KP * NT], F32R, first_half)
    xrep = mid[:, 0:3 * IMG * VR].rearrange("q (k i m) -> q k i m", k=3, i=IMG)
    uh = sb("uh", [128, NP, NH, NTOK], where=first_half)
    mh = sb("mh", [128, NH * RK], F32R, first_half)
    ml = sb("ml", [128, NH * RK], F32R, first_half)
    ls = sb("latents", [128, NT], F32R, first_half)
    lbd = sb("lbd", [128, NP, RT], where=first_half)
    sx = sb("sx", [RT, 2, NH * NTOK], where=first_half)
    pts = sb("pts", [VR, 2, NG, RT], where=first_half)
    vbd = sb("vbd", [VR, 2, 2 * D], where=first_half)
    uc = sb("uc", [RT, D], where=first_half)
    sm = sb("sm", [RT, 2, 3, NH], where=first_half)
    ystats = sb("out_stats_buf", [RT, NP, 6], where=first_half)
    ymv = sb("out_mv", [RT, NP, 2], where=first_half)
    yrstd = sb("out_rstd_buf", [RT, NP], where=first_half)
    zg = uh[:].rearrange("q a b c -> q (a b c)")[:, 0:RING0 * NT].rearrange("q (r t) -> q r t", r=RING0)
    g1 = xs[0:96, 0:NT]
    y0 = xs[0:RT, NT:NT + NP * D].rearrange("q (p f) -> q p f", p=NP)
    hrt = uh[:].rearrange("q a b c -> q (a b c)")[:, 0:NH * RK].rearrange("q (h r) -> q h r", h=NH)
    hset = uh[:].rearrange("q a b c -> q (a b c)")[:, 800:800 + 3 * RK].rearrange("q (i r) -> q i r", i=3)

    def split_pass(eng, out, parts, mov, start=True, stop=True):
        H, L, RH, RL = parts
        mh, ml, mr = mov
        seq = [(H, mh), (L, mh), (RH, mr), (RL, mr), (H, ml)]
        for i, (w, m) in enumerate(seq):
            ins = eng.matmul(out, w, m, start=start and i == 0, stop=stop and i == len(seq) - 1)
        return ins

    slot_loaded = [sem("stage0_loaded"), sem("stage1_loaded")]
    hi_done, lo_done = sem("weights_high_done"), sem("weights_low_done")

    class Piece:

        def __init__(self, first, src, high, low, n, step=0):
            self.first, self.src, self.high, self.low, self.n, self.step = first, src, high, low, n, step
            assert step % 2 == 0

        def number(self, i):
            return self.first + (self.step * i if self.step else 0)

        def stage(self):
            v = wstage[:, self.first % 2, 0:self.n]
            return v.rearrange("p (t f) -> p t f", f=DR) if len(self.high(0).shape) == 3 else v

    numbers = [0]

    def straight(src, high, low, n):
        out = []
        for o in range(0, n, WST):
            m = min(WST, n - o)
            out.append(Piece(numbers[0], lambda i, o=o, m=m: src[:, o:o + m], lambda i, o=o, m=m: high[:, o:o + m],
                             lambda i, o=o, m=m: low[:, o:o + m], m))
            numbers[0] += 1
        return out

    def side_by_side(src, nt, dst):
        v = dst.rearrange("p (t s f) -> p t s f", s=2, f=DR)
        out, m = [], WST // DR
        for o in range(0, nt, m):
            e = min(o + m, nt)
            out.append(Piece(numbers[0], lambda i, o=o, e=e: src[:, o * DR:e * DR],
                             lambda i, o=o, e=e: v[:, o:e, 0, :], lambda i, o=o, e=e: v[:, o:e, 1, :], (e - o) * DR))
            numbers[0] += 1
        return out

    def looped(src, high, low, n, loops, unroll):
        w = n // (loops * unroll)
        assert w * loops * unroll == n and w <= WST
        out = []
        for j in range(unroll):
            def at(t, j=j):
                return lambda i: t[:, bass.ds(w * j + w * unroll * i, w)]
            out.append(Piece(numbers[0] + j, at(src), at(high), at(low), w, unroll))
        numbers[0] += loops * unroll
        return out

    def load(sp, ps, i=0):
        for p in ps:
            if p.first >= 2:
                sp.wait_ge(hi_done, p.number(i) - 1)
                sp.wait_ge(lo_done, p.number(i) - 1)
            sp.dma_start(wstage[:, p.first % 2, 0:p.n], p.src(i)).then_inc(slot_loaded[p.first % 2], 16)

    def high(act, ps, i=0):
        for p in ps:
            turns = p.first // 2 + 1
            act.wait_ge(slot_loaded[p.first % 2], 16 * turns + (8 * p.step * i if p.step else 0))
            act.activation(p.high(i), p.stage(), ACT.Copy).then_inc(hi_done, 1)

    def low(eng, ps, i=0):
        for p in ps:
            eng.wait_ge(hi_done, p.number(i) + 1)
            eng.tensor_tensor(p.low(i), p.stage(), p.high(i).bitcast(F32), ALU.subtract).then_inc(lo_done, 1)

    big0_h, big0_l, up0_r = big0[:, 0:SZ_FFN0], big0[:, SZ_FFN0:2 * SZ_FFN0], big0[:, 2 * SZ_FFN0:]
    mid_h, mid_l, wo_r = mid[:, 0:SZ_ATT1], mid[:, SZ_ATT1:2 * SZ_ATT1], mid[:, 2 * SZ_ATT1:]
    tok_p = straight(a["w_tok"], wtok[:, 0:SZ_TOK], wtok[:, SZ_TOK:2 * SZ_TOK], SZ_TOK)
    att0_p = straight(a["w_att0"], wtok[:, 2 * SZ_TOK:2 * SZ_TOK + SZ_ATT0],
                      wtok[:, 2 * SZ_TOK + SZ_ATT0:], SZ_ATT0)
    ffn0_p = looped(a["w_ffn0"], big0_h, big0_l, SZ_FFN0, NC, 2)
    ffn0_q = straight(a["w_w1"], w1s[:, 0:2 * SZ_W1], w1s[:, 2 * SZ_W1:], 2 * SZ_W1) + \
        side_by_side(a["w_up0_r"], T0, up0_r)
    att1_q = side_by_side(a["w_wo_r"], QJ, wo_r)
    att1_p = looped(a["w_att1"], mid_h, mid_l, SZ_ATT1, 2, 2)

    wait_taken = sem("wait_taken")

    def plain(eng):
        eng.sem_inc(wait_taken, 1)

    PREP = dict(st=sig("norm_stats", NP), mv=sig("norm_meanvar", NP), ve=sig("norm_vareps"), rs=sig("norm_rstd"),
                xn=sig("norm_normed", NP), tw=sig("norm_normed_twice"), t0=sig("norm_turned"),
                t1=sig("norm_rest_turned"), xh=sig("norm_xh"), xl=sig("norm_xl"), rh=sig("norm_xr_high"),
                rl=sig("norm_xr_low"))

    def hc(tile, n=NP):
        return h[:, bass.ds(tile, n), :]

    def h1(tile):
        return h[:, tile, :] if isinstance(tile, int) else hc(tile, 1).rearrange("a b d -> a (b d)")

    def norm_dve(dve, n, tile):
        norm_stats(dve, n, tile, range(NP))
        norm_moments(dve, n)

    def norm_stats(dve, n, tile, ps):
        for p in ps:
            dve.bn_stats(stats[:, p, :], h1(tile + p)).then_inc(PREP["st"].sem, 1)

    def norm_moments(dve, n):
        for p in range(NP):
            dve.wait_ge(PREP["st"].sem, PREP["st"].at(n, p + 1))
            plain(dve)
            dve.bn_aggr(mv[:, p, :], stats[:, p, :]).then_inc(PREP["mv"].sem, 1)
        dve.wait_ge(PREP["mv"].sem, PREP["mv"].at(n, NP))
        dve.tensor_scalar(rstd[:], mv[:, :, 1], EPS, None, ALU.add).then_inc(PREP["ve"].sem, 1)

    def norm_dve2(dve, n, tile, xn_, ps=range(NP)):
        dve.wait_ge(PREP["rs"].sem, PREP["rs"].at(n, 1))
        for p in ps:
            dve.tensor_scalar(xn_[:, p, 0:D], h1(tile + p), mv[:, p, 0:1], rstd[:, p:p + 1],
                              ALU.subtract, ALU.mult).then_inc(PREP["xn"].sem, 1)

    def norm_pool(pool, n):
        pool.wait_ge(PREP["ve"].sem, PREP["ve"].at(n, 1))
        pool.tensor_tensor(rstd[:], rstd[:], mhalf[:], ALU.pow).then_inc(PREP["rs"].sem, 1)

    def norm_act(act, n, xn_):
        act.wait_ge(PREP["xn"].sem, PREP["xn"].at(n, NP))
        act.activation(xn_[:, :, D:D + DR], xn_[:, :, 128:D], ACT.Copy).then_inc(PREP["tw"].sem, 1)

    def turn_pe(pe, n, xn_, bank):
        pe.wait_ge(PREP["xn"].sem, PREP["xn"].at(n, NP))
        for p in range(NP):
            mm = pe.transpose(banks[:, bank, p * RT:(p + 1) * RT], xn_[:, p, 0:128], ident[0:RT, 0:RT])
        mm.then_inc(PREP["t0"].sem, 1)

    def turn_rest_pe(pe, n, xn_, bank):
        pe.wait_ge(PREP["tw"].sem, PREP["tw"].at(n, 1))
        for p in range(NP):
            mm = pe.transpose(banks[:, bank, p * RT:(p + 1) * RT], xn_[:, p, 128:D + DR], ident[0:RT, 0:RT])
        mm.then_inc(PREP["t1"].sem, 1)

    def columns(by_half):
        if not by_half:
            return (lambda v: v), (lambda v: v)
        return (lambda v: v.rearrange("q (p s n) -> q s p n", p=NP, s=2),
                lambda v: v.rearrange("q (s p n) -> q s p n", p=NP, s=2))

    def turned_act(act, n, u, bank, by_half=False):
        f, g = columns(by_half)
        act.wait_ge(PREP["t0"].sem, PREP["t0"].at(n, 1))
        act.activation(g(xh[:, u]), f(banks[:, bank, 0:NT]), ACT.Copy).then_inc(PREP["xh"].sem, 1)

    def turned_dve(dve, n, u, bank, by_half=False):
        f, g = columns(by_half)
        dve.wait_ge(PREP["xh"].sem, PREP["xh"].at(n, 1))
        dve.tensor_tensor(g(xl[:, u]), f(banks[:, bank, 0:NT]), g(xh[:, u].bitcast(F32)),
                          ALU.subtract).then_inc(PREP["xl"].sem, 1)

    def rest_act(act, n, u, bank, by_half=False):
        f, g = columns(by_half)
        act.wait_ge(PREP["t1"].sem, PREP["t1"].at(n, 1))
        act.activation(g(xr[:, u]), f(banks[:, bank, 0:NT]), ACT.Copy).then_inc(PREP["rh"].sem, 1)

    def rest_dve(dve, n, u, bank, by_half=False):
        f, g = columns(by_half)
        dve.wait_ge(PREP["rh"].sem, PREP["rh"].at(n, 1))
        dve.tensor_tensor(g(xr[64:128, u]), f(banks[64:128, bank, 0:NT]), g(xr[64:128, u].bitcast(F32)),
                          ALU.subtract).then_inc(PREP["rl"].sem, 1)

    def turned_wait(pe, n):
        for k in ("xh", "xl", "rh", "rl"):
            pe.wait_ge(PREP[k].sem, PREP[k].at(n, 1))

    setup, const_in = sem("setup_vec"), sem("const_in")
    x_in, x_hi, x_lo = sem("patches_in"), sig("patches_high"), sig("patches_low")
    tok_done, h0_done = sig("tok_done", 2), sig("tok_added", 2)
    lat_done, lat_ev = sig("latent_done"), sig("latent_out", 3)
    lat_low = sig("latent_low")
    u_done, u_ev, u_ev2 = sig("u_done", NH // 2), sig("u_out", NH), sig("u_out_crossed", NH)
    U_BANK = (4, 5, 6, 7, 3, 2)
    s_done, mx_done, sub_done = sig("scores_done", NP), sig("score_max", NP), sig("scores_less_max", NP)
    e_done, sum_done, rec_done = sig("exp_done", NP), sig("prob_sum", NP), sig("prob_recip", NP)
    pt_done, pt_ev = sig("probs_turned", NP), sig("probs_turned_out", NP)
    v_done, v_ev = sig("values_done", NP), sig("values_out", NP)
    c_done, c_a, c_b, c_n, c_h = (sig("ctx_done", NP), sig("ctx_first_image", NP), sig("ctx_both", NP),
                                  sig("ctx_normed", NP), sig("ctx_added", NP))
    vb_done = sig("value_bias_added")
    rep_done = [sig(n + "_repeated") for n in ("xh", "xl", "xr")]
    sel0_in, sel0_done = sem("early_selectors_in"), sem("early_selectors_rounded")
    sel0_stage = xs[0:SELW, 0:E0 * 128]
    PH = NP * NTOK
    XU = 1
    wt_h, wt_l = wtok[:, 0:SZ_TOK], wtok[:, SZ_TOK:2 * SZ_TOK]
    w0h, w0l = wtok[:, 2 * SZ_TOK:2 * SZ_TOK + SZ_ATT0], wtok[:, 2 * SZ_TOK + SZ_ATT0:]
    N_CONST = 16 * 4

    def u_part(j, second, odd):
        return banks[64 * second:64 * second + 64, U_BANK[j], PH * odd:PH * odd + PH].rearrange("q (p n) -> q p n", p=NP)


    with nc.Block() as block:
        @block.sync
        def _(sp):
            start_at_one(sp)
            sp.dma_start(xs[:], a["patches"][0:128, :]).then_inc(x_in, 16)
            load(sp, tok_p)
            sp.dma_start(pack[:], a["pack"]).then_inc(const_in, 16)
            sp.dma_start(hrt, a["hrt"][:, 0:NH * RK].rearrange("q (h r) -> q h r", h=NH)).then_inc(const_in, 16)
            sp.dma_start(hset[:, 0, :], a["hrt"][:, NH * RK:]).then_inc(const_in, 16)
            sp.dma_start(const[:], a["const"]).then_inc(const_in, 16)
            load(sp, att0_p)

            def more(c, last=False):
                if not last:
                    sp.wait_ge(x_hi.sem, x_hi.at(c, 1))
                    sp.wait_ge(x_lo.sem, x_lo.at(c, 1))
                    sp.dma_start(xs[:], a["patches"][bass.ds(c * 128 + 128, 128), :]).then_inc(x_in, 16)
                load(sp, ffn0_p, c)
            with sp.Fori(0, NC - 1) as c:
                more(c)
            more(NC - 1, True)
            sp.wait_ge(x_hi.sem, x_hi.at(NC - 1, 1))
            sp.wait_ge(x_lo.sem, x_lo.at(NC - 1, 1))
            sp.dma_start(sel0_stage, a["sel"][0:SELW, 0:E0 * 128]).then_inc(sel0_in, 16)
            load(sp, ffn0_q)

        @block.gpsimd
        def _(pool):
            def patches(n):
                pool.wait_ge(x_in, n * 16 + 16)
                pool.wait_ge(tok_done.sem, tok_done.at(n, 0))
                plain(pool)
                pool.tensor_scalar(xsh[:], xs[:], 1.0, 0.0, ALU.mult, ALU.add).then_inc(x_hi.sem, 1)
                pool.wait_ge(x_hi.sem, x_hi.at(n, 1))
                pool.tensor_tensor(xsl[:], xs[:], xsh[:].bitcast(F32), ALU.subtract).then_inc(x_lo.sem, 1)

            def chunk(c, last=False):
                if not last:
                    patches(c + 1)
                pool.wait_ge(PREP["xn"].sem, PREP["xn"].at(c, NP))
                pool.tensor_tensor(hc(c * NP), hc(c * NP), row["vb"].unsqueeze(1).to_broadcast([RT, NP, D]),
                                   ALU.add).then_inc(vb_done.sem, 1)
                low(pool, ffn0_p[0:1], c)
                if not last:
                    norm_pool(pool, c + 1)
                low(pool, ffn0_p[1:2], c)
                if last:
                    low(pool, ffn0_q)
                    norm_pool(pool, c + 1)

            norm_pool(pool, 0)
            with pool.Fori(0, NC - 1) as c:
                chunk(c)
            chunk(NC - 1, True)

        @block.scalar
        def _(act):
            act.wait_ge(x_in, 16)
            act.activation(xsh[:], xs[:], ACT.Copy).then_inc(x_hi.sem, 1)
            high(act, tok_p)
            high(act, att0_p)

            def finish(n, u, by_half):
                norm_act(act, n, xn[:, u])
                turned_act(act, n, u, 0, by_half)
                rest_act(act, n, u, 1, by_half)

            def repeat_x(n):
                v = xh[:, XU].bitcast(F32).rearrange("q (i n) -> q i n", i=IMG).unsqueeze(2).to_broadcast([128, IMG, GH, NTOK])
                act.wait_ge(PREP["xh"].sem, PREP["xh"].at(n, 1))
                act.wait_ge(c_done.sem, c_done.at(n, 0))
                act.activation(xrep[:, 0].rearrange("q i (r n) -> q i r n", r=GH), v, ACT.Copy).then_inc(rep_done[0].sem, 1)

            def chunk(c, last=False):
                act.wait_ge(lat_done.sem, lat_done.at(c, 1))
                act.wait_ge(c_done.sem, c_done.at(c, 0))
                act.activation(ls[:], banks[:, 2, 0:NT], ACT.Copy).then_inc(lat_ev.sem, 1)
                act.wait_ge(lat_low.sem, lat_low.at(c, 1))
                for i in range(2):
                    s = slice(64 * i, 64 * i + 64)
                    act.activation(lbd[s, :, NTOK * i:NTOK * (i + 1)],
                                   banks[s, 2, PH * i:PH * i + PH].rearrange("q (p n) -> q p n", p=NP),
                                   ACT.Copy).then_inc(lat_ev.sem, 1)
                for j in range(NH // 2):
                    act.wait_ge(u_done.sem, u_done.at(c, j + 1))
                    for r in range(2):
                        act.activation(uh[64 * r:64 * r + 64, :, 2 * j + r, :], u_part(j, r, r), ACT.Copy).then_inc(u_ev.sem, 1)
                repeat_x(c)
                high(act, ffn0_p[0:1], c)

                def exp(p):
                    act.wait_ge(sub_done.sem, sub_done.at(c, p + 1))
                    act.activation(sx[:, p % 2], sx[:, p % 2], ACT.Exp).then_inc(e_done.sem, 1)

                exp(0)
                for p in range(NP):
                    if p + 1 < NP:
                        exp(p + 1)
                    act.wait_ge(pt_done.sem, pt_done.at(c, p + 1))
                    act.activation(pts[:, p % 2], banks[0:VR, 6, 0:NT].rearrange("q (g t) -> q g t", g=NG),
                                   ACT.Copy).then_inc(pt_ev.sem, 1)
                    if p == 3 and not last:
                        rest_act(act, c + 1, XU, 1, True)
                    if p == 3 and last:
                        high(act, ffn0_q)
                    act.wait_ge(c_done.sem, c_done.at(c, p + 1))
                    act.wait_ge(c_h.sem, c_h.at(c, p))
                    act.activation(uc[:], banks[0:RT, 7, 0:D], ACT.Copy,
                                   scale=const[0:RT, C_MAB:C_MAB + 1]).then_inc(c_a.sem, 1)
                    if p == 1:
                        high(act, ffn0_p[1:2], c)
                    if p == 2 and not last:
                        norm_act(act, c + 1, xn[:, XU])
                        turned_act(act, c + 1, XU, 0, True)
                if last:
                    finish(NC, 0, False)

            finish(0, XU, True)
            with act.Fori(0, NC - 1) as c:
                chunk(c)
            chunk(NC - 1, True)

        @block.vector
        def _(dve):
            dve.memset(mhalf[:], -0.5).then_inc(setup, 1)
            dve.memset(gx[:], 0.0).then_inc(setup, 1)
            dve.memset(lbd[:], 0.0).then_inc(setup, 1)
            dve.wait_ge(x_hi.sem, x_hi.at(0, 1))
            dve.tensor_tensor(xsl[:], xs[:], xsh[:].bitcast(F32), ALU.subtract).then_inc(x_lo.sem, 1)
            low(dve, tok_p)
            dve.wait_ge(const_in, N_CONST)
            dve.tensor_tensor(row["pos"], row["pos"], row["bproj"], ALU.add).then_inc(setup, 1)
            dve.tensor_reduce(hset[:, 1, :], hrt.rearrange("p h r -> p r h"), X, ALU.add).then_inc(setup, 1)
            dve.wait_ge(setup, 5)
            dve.tensor_tensor(hset[:, 2, :], hset[:, 0, :], hset[:, 1, :], ALU.subtract).then_inc(setup, 1)
            dve.wait_ge(setup, 6)
            dve.tensor_scalar(hset[:, 1, :], hset[:, 2, :], 1.0 / NH, None, ALU.mult).then_inc(setup, 1)
            dve.wait_ge(setup, 7)
            dve.tensor_tensor(hrt, hrt, hset[:, 1, :].unsqueeze(1).to_broadcast([128, NH, RK]), ALU.add).then_inc(setup, 1)
            dve.wait_ge(setup, 8)
            dve.tensor_scalar(hrt, hrt, RK ** -0.5, None, ALU.mult).then_inc(setup, 1)
            dve.wait_ge(setup, 9)
            flat = hrt.rearrange("q h r -> q (h r)")
            dve.tensor_copy(mh[:], flat).then_inc(setup, 1)
            dve.wait_ge(setup, 10)
            dve.tensor_tensor(ml[:], flat, mh[:].bitcast(F32), ALU.subtract).then_inc(setup, 1)
            low(dve, att0_p)

            def tok_add(n, i):
                dve.wait_ge(tok_done.sem, tok_done.at(n, i + 1))
                dve.tensor_tensor(hc(n * NP + 2 * i, 2), banks[0:RT, i, 0:2 * D].rearrange("q (p f) -> q p f", p=2),
                                  row["pos"].unsqueeze(1).to_broadcast([RT, 2, D]), ALU.add).then_inc(h0_done.sem, 1)

            def finish(n, u, by_half):
                turned_dve(dve, n, u, 0, by_half)
                rest_dve(dve, n, u, 1, by_half)

            def repeat_x(n):
                for k, (t, s) in enumerate(((xl, "xl"), (xr, "rl"))):
                    v = t[:, XU].bitcast(F32).rearrange("q (i n) -> q i n", i=IMG).unsqueeze(2).to_broadcast([128, IMG, GH, NTOK])
                    dve.wait_ge(PREP[s].sem, PREP[s].at(n, 1))
                    if k:
                        dve.wait_ge(PREP["rh"].sem, PREP["rh"].at(n, 1))
                    dve.wait_ge(c_done.sem, c_done.at(n, 0))
                    dve.tensor_copy(xrep[:, k + 1].rearrange("q i (r n) -> q i r n", r=GH), v).then_inc(rep_done[k + 1].sem, 1)

            def chunk(c, last=False):
                def less_max(p):
                    S = banks[0:RT, 4 + p % 2, 0:NH * NTOK].rearrange("q (h m) -> q h m", h=NH)
                    dve.wait_ge(s_done.sem, s_done.at(c, p + 1))
                    dve.tensor_reduce(sm[:, p % 2, 0], S, X, ALU.max).then_inc(mx_done.sem, 1)
                    dve.wait_ge(mx_done.sem, mx_done.at(c, p + 1))
                    dve.wait_ge(pt_done.sem, pt_done.at(c, max(p - 1, 0)))
                    dve.tensor_tensor(sx[:, p % 2].rearrange("q (h m) -> q h m", h=NH), S,
                                      sm[:, p % 2, 0].unsqueeze(2).to_broadcast([RT, NH, NTOK]),
                                      ALU.subtract).then_inc(sub_done.sem, 1)

                def values(p):
                    dve.wait_ge(v_done.sem, v_done.at(c, p + 1))
                    dve.wait_ge(c_done.sem, c_done.at(c, max(p - 1, 0)))
                    dve.tensor_tensor(vbd[:, p % 2].rearrange("q (g h d) -> q g h d", h=GH, d=HD),
                                      banks[0:VR, 3, 0:2 * D].rearrange("q (g h d) -> q g h d", h=GH, d=HD),
                                      const[0:VR, C_VM:C_VM + GH].unsqueeze(1).unsqueeze(3).to_broadcast([VR, 2 * NG, GH, HD]),
                                      ALU.mult).then_inc(v_ev.sem, 1)

                dve.wait_ge(lat_ev.sem, lat_ev.at(c, 1))
                dve.tensor_tensor(ls[64:128], banks[64:128, 2, 0:NT], ls[64:128].bitcast(F32), ALU.subtract).then_inc(lat_low.sem, 1)
                for j in range(NH // 2):
                    dve.wait_ge(u_ev.sem, u_ev.at(c, 2 * j + 2))
                    for hd, q, r in ((2 * j, 0, 1), (2 * j + 1, 1, 0)):
                        dve.tensor_copy(uh[64 * r:64 * r + 64, :, hd, :],
                                        u_part(j, q, r)).then_inc(u_ev2.sem, 1)
                repeat_x(c)
                if last:
                    dve.wait_ge(sel0_in, 16)
                    dve.tensor_copy(sel0[:], sel0_stage).then_inc(sel0_done, 1)
                less_max(0)
                values(0)
                for p in range(NP):
                    if p + 1 < NP:
                        less_max(p + 1)
                    dve.wait_ge(e_done.sem, e_done.at(c, p + 1))
                    dve.tensor_reduce(sm[:, p % 2, 1], sx[:, p % 2].rearrange("q (h m) -> q h m", h=NH),
                                      X, ALU.add).then_inc(sum_done.sem, 1)
                    dve.wait_ge(sum_done.sem, sum_done.at(c, p + 1))
                    dve.reciprocal(sm[:, p % 2, 2], sm[:, p % 2, 1]).then_inc(rec_done.sem, 1)
                    if p + 1 < NP:
                        values(p + 1)
                    if not last and p < 2:
                        tok_add(c + 1, p)
                    if not last and p == 1:
                        dve.wait_ge(h0_done.sem, h0_done.at(c + 1, 2))
                        plain(dve)
                        norm_dve(dve, c + 1, c * NP + NP)
                    if not last and p == 2:
                        norm_dve2(dve, c + 1, c * NP + NP, xn[:, XU])
                    if not last and p == 3:
                        finish(c + 1, XU, True)
                    dve.wait_ge(c_a.sem, c_a.at(c, p + 1))
                    dve.scalar_tensor_tensor(uc[:], banks[0:RT, 7, D:2 * D], const[0:RT, C_MAB + 1:C_MAB + 2],
                                             uc[:], ALU.mult, ALU.add).then_inc(c_b.sem, 1)
                    dve.wait_ge(c_b.sem, c_b.at(c, p + 1))
                    dve.wait_ge(rec_done.sem, rec_done.at(c, p + 1))
                    u3 = uc[:].rearrange("q (h d) -> q h d", h=NH)
                    dve.tensor_tensor(u3, u3, sm[:, p % 2, 2].unsqueeze(2).to_broadcast([RT, NH, HD]),
                                      ALU.mult).then_inc(c_n.sem, 1)
                    dve.wait_ge(c_n.sem, c_n.at(c, p + 1))
                    dve.wait_ge(vb_done.sem, vb_done.at(c, 1))
                    dve.tensor_tensor(h1(c * NP + p), h1(c * NP + p), uc[:], ALU.add).then_inc(c_h.sem, 1)
                if last:
                    dve.wait_ge(c_h.sem, c_h.at(c, NP))
                    norm_dve(dve, NC, 0)
                    norm_dve2(dve, NC, 0, xn[:, 0])
                    finish(NC, 0, False)

            for i in range(2):
                tok_add(0, i)
            dve.wait_ge(h0_done.sem, h0_done.at(0, 2))
            norm_dve(dve, 0, 0)
            norm_dve2(dve, 0, 0, xn[:, XU])
            finish(0, XU, True)
            with dve.Fori(0, NC - 1) as c:
                chunk(c)
            chunk(NC - 1, True)

        @block.tensor
        def _(pe):
            def tok(n, tiles):
                for p in tiles:
                    out = banks[0:RT, p // 2, D * (p % 2):D * (p % 2) + D]
                    if p == 0:
                        pe.wait_ge(x_hi.sem, x_hi.at(n, 1))
                        pe.wait_ge(x_lo.sem, x_lo.at(n, 1))
                        pe.wait_ge(PREP["xl"].sem, PREP["xl"].at(n, 0))
                        pe.wait_ge(PREP["rl"].sem, PREP["rl"].at(n, 0))
                    for k in range(KP):
                        s = slice(k * NT + p * RT, k * NT + (p + 1) * RT)
                        w = slice(k * D, (k + 1) * D)
                        pe.matmul(out, xsh[:, s], wt_h[:, w], start=(k == 0), stop=False)
                        pe.matmul(out, xsh[:, s], wt_l[:, w], start=False, stop=False)
                        mm = pe.matmul(out, xsl[:, s], wt_h[:, w], start=False, stop=(k == KP - 1))
                    if p % 2:
                        mm.then_inc(tok_done.sem, 1)

            def finish(n, u):
                turn_pe(pe, n, xn[:, u], 0)
                turn_rest_pe(pe, n, xn[:, u], 1)

            def chunk(c, last=False):
                turned_wait(pe, c)
                b = [w[:, o:o + 128] for o in (0, 128) for w in (w0h, w0l)]
                split_pass(pe, banks[:, 2, 0:NT], b, (xh[:, XU], xl[:, XU], xr[:, XU])).then_inc(lat_done.sem, 1)
                pe.wait_ge(c_h.sem, c_h.at(c, 0))
                pe.wait_ge(lat_low.sem, lat_low.at(c, 1))
                for j in range(NH // 2):
                    m = slice(128 * j, 128 * j + 128)
                    if U_BANK[j] == 2:
                        pe.wait_ge(lat_ev.sem, lat_ev.at(c, 3))
                    pe.matmul(banks[:, U_BANK[j], 0:NT], mh[:, m], ls[:], start=True, stop=False)
                    pe.matmul(banks[:, U_BANK[j], 0:NT], ml[:, m], ls[:], start=False, stop=True).then_inc(u_done.sem, 1)

                def scores(p):
                    if p >= 2:
                        pe.wait_ge(sub_done.sem, sub_done.at(c, p - 1))
                    pe.matmul(banks[0:RT, 4 + p % 2, 0:NH * NTOK], lbd[:, p, :], uh[:, p],
                              start=True, stop=True).then_inc(s_done.sem, 1)

                def values(p):
                    if p:
                        pe.wait_ge(v_ev.sem, v_ev.at(c, p))
                    for i in range(2):
                        x0, x1, x2 = (xrep[:, k, NP * i + p, :] for k in range(3))
                        H, L, RH, RL = (w[:, o:o + D] for o in (256, 256 + D) for w in (w0h, w0l))
                        seq = [(x0, H), (x0, L), (x2, RH), (x2, RL), (x1, H)]
                        for k, (st, m) in enumerate(seq):
                            mm = pe.matmul(banks[0:VR, 3, D * i:D * i + D], st, m, start=(k == 0), stop=(k == 4))
                    mm.then_inc(v_done.sem, 1)

                pe.wait_ge(u_ev.sem, u_ev.at(c, NH))
                pe.wait_ge(u_ev2.sem, u_ev2.at(c, NH))
                scores(0)
                for r in rep_done:
                    pe.wait_ge(r.sem, r.at(c, 1))
                values(0)
                for p in range(NP):
                    if p + 1 < NP:
                        scores(p + 1)
                        values(p + 1)
                    pe.wait_ge(e_done.sem, e_done.at(c, p + 1))
                    if p:
                        pe.wait_ge(pt_ev.sem, pt_ev.at(c, p))
                    for g in range(NG):
                        mm = pe.transpose(banks[0:VR, 6, RT * g:RT * g + RT],
                                          sx[:, p % 2, VR * g:VR * (g + 1)], ident[0:RT, 0:RT])
                    mm.then_inc(pt_done.sem, 1)
                    if not last and p < 2:
                        tok(c + 1, (2 * p, 2 * p + 1))
                    if not last and p == 3:
                        turn_rest_pe(pe, c + 1, xn[:, XU], 1)
                    pe.wait_ge(pt_ev.sem, pt_ev.at(c, p + 1))
                    pe.wait_ge(v_ev.sem, v_ev.at(c, p + 1))
                    if p:
                        pe.wait_ge(c_b.sem, c_b.at(c, p))
                    out = banks[0:RT, 7, 0:2 * D].rearrange("q (i g f) -> q i g f", i=2, g=NG)
                    vv = vbd[:, p % 2].rearrange("q (i g f) -> q i g f", i=2, g=NG)
                    for g in range(NG):
                        mm = pe.matmul(out[:, :, g, :], pts[:, p % 2, g, :], vv[:, :, g, :], start=True, stop=True)
                    mm.then_inc(c_done.sem, 1)
                    if not last and p == 2:
                        turn_pe(pe, c + 1, xn[:, XU], 0)
                if last:
                    finish(NC, 0)

            pe.wait_ge(lo_done, len(tok_p))
            tok(0, range(NP))
            pe.wait_ge(const_in, N_CONST)
            finish(0, XU)
            pe.wait_ge(setup, 11)
            pe.wait_ge(lo_done, len(tok_p) + len(att0_p))
            with pe.Fori(0, NC - 1) as c:
                chunk(c)
            chunk(NC - 1, True)

    MISC, GB = 7, 6

    def gates_dve(dve, S, c, part, first_layer):
        lg, ex, pr, tp = (rt[:, i, :, 0:8] for i in range(4))
        m0, m1 = rt[:, 4, :, 0:8], rt[:, 5, :, 0:8]
        idf = rt[:, 6, :, 0:2]
        one = [rt[:, 7, :, i:i + 1] for i in range(6)]
        count = S["count"]

        def step(ins, wait=True):
            count[0] += 1
            ins.then_inc(S["gv"].sem, 1)
            if wait:
                dve.wait_ge(S["gv"].sem, S["gv"].at(c, count[0]))

        def w8(v):
            return v.to_broadcast([RT, NP, 8])

        if part == 0:
            count[0] = 0
            lp = banks[0:RT, MISC, 0:NP * 10].rearrange("q (p e) -> q p e", p=NP)
            dve.wait_ge(S["lg"].sem, S["lg"].at(c, 1))
            if first_layer:
                b2 = pack[0:RT, K_B2:K_B2 + E0].unsqueeze(1).to_broadcast([RT, NP, 8])
                step(dve.tensor_tensor(lg, lp[:, :, 0:8], b2, ALU.add))
            else:
                step(dve.tensor_scalar(one[4], lp[:, :, 8:9], pack[0:RT, K_SGB:K_SGB + 1], -1.0, ALU.add, ALU.mult), False)
                step(dve.tensor_copy(lg, lp[:, :, 0:8]))
            plain(dve)
            for p in range(NP):
                step(dve.max(tp[:, p, :], lg[:, p, :]), False)
            dve.wait_ge(S["gv"].sem, S["gv"].at(c, count[0]))
            dve.tensor_tensor(ex, lg, w8(tp[:, :, 0:1]), ALU.subtract).then_inc(S["gs"].sem, 1)
            for p in range(NP):
                step(dve.max_index(ri[:, p, :], tp[:, p, :], lg[:, p, :]), False)
        if part == 1:
            io = const[0:RT, C_IOTA:C_IOTA + 8].unsqueeze(1).to_broadcast([RT, NP, 8])
            dve.wait_ge(S["gv"].sem, S["gv"].at(c, count[0]))
            step(dve.tensor_copy(idf, ri[:, :, 0:2]))
            step(dve.tensor_tensor(m0, io, w8(idf[:, :, 0:1]), ALU.is_equal), False)
            step(dve.tensor_tensor(m1, io, w8(idf[:, :, 1:2]), ALU.is_equal))
            step(dve.tensor_tensor(m0, m0, m1, ALU.add))
        if part == 2:
            dve.wait_ge(S["ge"].sem, S["ge"].at(c, 1))
            step(dve.tensor_reduce(one[0], ex, X, ALU.add))
            step(dve.reciprocal(one[1], one[0]))
            step(dve.tensor_tensor(pr, ex, w8(one[1]), ALU.mult))
            step(dve.tensor_tensor(pr, pr, m0, ALU.mult))
            step(dve.tensor_reduce(one[2], pr, X, ALU.add))
            if first_layer:
                step(dve.tensor_scalar(one[2], one[2], 1e-8, None, ALU.add))
            step(dve.reciprocal(one[3], one[2]))
            if not first_layer:
                step(dve.tensor_scalar(one[4], one[4], 1.0, None, ALU.add))
                step(dve.reciprocal(one[5], one[4]))
                step(dve.tensor_scalar(one[4], one[5], -1.0, 1.0, ALU.mult, ALU.add))
                step(dve.tensor_tensor(one[3], one[3], one[4], ALU.mult))
            for i in range(2):
                dve.tensor_tensor(gx[:, :, 32 * i:32 * i + 8], pr, w8(one[3]), ALU.mult).then_inc(S["gx"].sem, 1)
                if not first_layer:
                    dve.tensor_copy(gx[:, :, 32 * i + 8:32 * i + 9], one[5]).then_inc(S["gx"].sem, 1)
            assert count[0] == S["gv"].per, count[0]

    def gates_act(act, S, c, first_layer):
        act.wait_ge(S["gs"].sem, S["gs"].at(c, 1))
        if not first_layer:
            act.activation(rt[:, 7, :, 4:5], rt[:, 7, :, 4:5], ACT.Exp).then_inc(S["ga"].sem, 1)
            act.wait_ge(S["ga"].sem, S["ga"].at(c, 1))
        act.activation(rt[:, 1, :, 0:8], rt[:, 1, :, 0:8], ACT.Exp).then_inc(S["ge"].sem, 1)

    def gates_pe(pe, S, c):
        pe.wait_ge(S["gx"].sem, S["gx"].at(c, S["gx"].per))
        plain(pe)
        for p in range(NP):
            mm = pe.transpose(banks[0:SELW, MISC, RT * p:RT * p + RT], gx[:, p, :], ident[0:RT, 0:RT])
        mm.then_inc(S["gt"].sem, 1)

    def gates_out(dve, S, c, u):
        dve.wait_ge(S["gt"].sem, S["gt"].at(c, 1))
        dve.tensor_copy(gT[:, u], banks[0:SELW, MISC, 0:NT]).then_inc(S["gh"].sem, 1)
        dve.wait_ge(S["gh"].sem, S["gh"].at(c, 1))
        dve.tensor_tensor(gT[32:64, u], banks[32:64, MISC, 0:NT], gT[32:64, u].bitcast(F32),
                          ALU.subtract).then_inc(S["gl"].sem, 1)

    def post_act(act, S, c):
        act.wait_ge(S["dn"].sem, S["dn"].at(c, S["dn"].per))
        for i in range(2):
            act.activation(acc_sb[:, i, :], banks[:, i, 0:NT], ACT.Copy).then_inc(S["ae"].sem, 1)

    POST = (MISC, GB)

    def post_pe(pe, S, c):
        pe.wait_ge(S["ae"].sem, S["ae"].at(c, 2))
        for q in range(2):
            for p in (2 * q, 2 * q + 1):
                t = slice(RT * p, RT * p + RT)
                o = D * (p % 2)
                pe.transpose(banks[0:RT, POST[q], o:o + 128], acc_sb[:, 0, t], ident)
                mm = pe.matmul(banks[0:RT, POST[q], o + 128:o + D], acc_sb[:, 1, t],
                               const[:, C_II:C_II + DR], start=True, stop=True)
            mm.then_inc(S["po"].sem, 1)

    def turned_back(q):
        return banks[0:RT, POST[q], 0:2 * D].rearrange("q (p f) -> q p f", p=2)

    def new_mix(tag, nt, gv, gxn, ring):
        return dict(count=[0], ring=ring, lg=sig(tag + "_logits"), gv=sig(tag + "_gate_steps", gv), gs=sig(tag + "_logits_less_max"),
                    ge=sig(tag + "_gate_exp"), ga=sig(tag + "_alpha_exp"), gx=sig(tag + "_gates", gxn),
                    gt=sig(tag + "_gates_turned"), gh=sig(tag + "_gates_high"), gl=sig(tag + "_gates_low"),
                    hd=sig(tag + "_hidden", nt), ae=sig(tag + "_acc_out", 2),
                    po=sig(tag + "_acc_turned", 2), ph=sig(tag + "_added", 2),
                    z=sig(tag + "_activated", nt), u=sig(tag + "_times_up", nt), g=sig(tag + "_times_gate", nt),
                    zh=sig(tag + "_z_high", nt), zl=sig(tag + "_z_low", nt), dn=sig(tag + "_down_done", nt),
                    gb=sig(tag + "_gate_spread", nt))

    def down_pe(pe, S, c, t, nt, main_h, main_l, rem):
        zz, m = t % S["ring"], slice(128 * t, 128 * t + 128)
        pe.wait_ge(S["zh"].sem, S["zh"].at(c, t + 1))
        if t == 0:
            pe.wait_ge(S["ae"].sem, S["ae"].at(c, 0))
        pe.matmul(banks[:, 0, 0:NT], main_h[:, m], zh[:, zz], start=(t == 0), stop=False)
        pe.matmul(banks[:, 0, 0:NT], main_l[:, m], zh[:, zz], start=False, stop=False)
        pe.matmul(banks[:, 1, 0:NT], rem[:, m], zh[:, zz], start=(t == 0), stop=False)
        pe.wait_ge(S["zl"].sem, S["zl"].at(c, t + 1))
        pe.matmul(banks[:, 0, 0:NT], main_h[:, m], zl[:, zz], start=False, stop=(t == nt - 1))
        pe.matmul(banks[:, 1, 0:NT], rem[:, m], zl[:, zz], start=False, stop=(t == nt - 1)).then_inc(S["dn"].sem, 1)

    def z_high(act, S, c, t):
        act.wait_ge(S["g"].sem, S["g"].at(c, t + 1))
        act.wait_ge(S["dn"].sem, S["dn"].at(c, max(t + 1 - S["ring"], 0)))
        act.activation(zh[:, t % S["ring"]], zg[:, t % S["ring"]], ACT.Copy).then_inc(S["zh"].sem, 1)

    def z_low(pool, S, c, t):
        pool.wait_ge(S["zh"].sem, S["zh"].at(c, t + 1))
        pool.wait_ge(S["dn"].sem, S["dn"].at(c, max(t + 1 - S["ring"], 0)))
        pool.tensor_tensor(zl[:, t % S["ring"]], zg[:, t % S["ring"]], zh[:, t % S["ring"]].bitcast(F32), ALU.subtract).then_inc(S["zl"].sem, 1)

    M0 = new_mix("ffn0", T0, 20, 2, RING0)
    M0["gb"] = sig("ffn0_gate_spread", E0)
    r1_done, r1_act = sig("router_hidden"), sig("router_gelu")
    y_zero = sem("out_zero")
    fst, fmv, fve, frs, fx = (sig("out_stats", NP), sig("out_meanvar", NP), sig("out_vareps"), sig("out_rstd"),
                              sig("out_centred", NP))
    fbeta, fadd, fh = sig("beta_added", NP), sig("moe_added", 2), sig("ffn0_residual", NP)
    w1 = [w1s[:, i * SZ_W1:(i + 1) * SZ_W1] for i in (0, 2, 1, 3)]
    dn0 = [w[:, o:o + SZ_DN0] for o in (0, SZ_DN0) for w in (big0_h, big0_l)]
    up_h, up_l = big0_h[:, 2 * SZ_DN0:], big0_l[:, 2 * SZ_DN0:]

    def plan(**at):
        return at

    A0 = plan(stats=(0, 1), moments=2, norm=(3, 4), turn=5, turned=6, rest=7, rested=8, router=9, router_act=9,
              logits=10, gates0=11, gexp=12, gates1=12, gates2=13, gturn=14, gout=15)
    Y0 = plan(stats=(5, 5, 6, 7), moments=7, centred=(9, 9, 10, 10), added=(12, 14, 14, 15))

    with nc.Block() as block:
        @block.sync
        def _(sp):
            start_at_one(sp)
            load(sp, att1_q)
            with sp.Fori(0, 2) as i:
                load(sp, att1_p, i)

        def ahead(i, u):
            return 2 * i + (u + 1), 2 * NP * i + NP if u == 0 else i * (-2 * NP) + 2 * NP

        @block.gpsimd
        def _(pool):
            def out_rstd(pool, n):
                pool.wait_ge(fve.sem, fve.at(n, 1))
                pool.tensor_tensor(yrstd[:], yrstd[:], mhalf[:], ALU.pow).then_inc(frs.sem, 1)

            low(pool, att1_q)

            def chunk(i, u):
                c = 2 * i + u
                nxt, _ = ahead(i, u)
                for t in range(T0):
                    z_low(pool, M0, c, t)
                    if 9 <= t < 9 + NP:
                        pool.wait_ge(PREP["xn"].sem, PREP["xn"].at(NC + c, NP))
                        pool.tensor_tensor(h1(c * NP + t - 9), h1(c * NP + t - 9), row["beta"], ALU.add).then_inc(fbeta.sem, 1)
                    if t == A0["moments"]:
                        norm_pool(pool, NC + nxt)
                    if t == Y0["moments"]:
                        out_rstd(pool, c)
                    if t == 8:
                        low(pool, att1_p[u:u + 1], i)

            with pool.Fori(0, 2) as i:
                for u in range(2):
                    chunk(i, u)
            out_rstd(pool, NC)

        @block.scalar
        def _(act):
            high(act, att1_q)

            def router(n):
                act.wait_ge(r1_done.sem, r1_done.at(n, 1))
                act.activation(g1, banks[0:96, MISC, 0:NT], ACT.Gelu, bias=pack[0:96, K_B1:K_B1 + 1]).then_inc(r1_act.sem, 1)

            def chunk(i, u):
                c = 2 * i + u
                nxt, _ = ahead(i, u)

                def gelu(t):
                    act.wait_ge(M0["hd"].sem, M0["hd"].at(c, t + 1))
                    act.wait_ge(M0["g"].sem, M0["g"].at(c, max(t - 1, 0)))
                    act.activation(zbuf[:, t % 2], banks[:, 2 + t % 3, 0:NT], ACT.Gelu,
                                   bias=pack[:, K_DB + t:K_DB + t + 1]).then_inc(M0["z"].sem, 1)

                gelu(0)
                for t in range(T0):
                    if t + 1 < T0:
                        gelu(t + 1)
                    z_high(act, M0, c, t)
                    if t == A0["norm"][1]:
                        norm_act(act, NC + nxt, xn[:, (u + 1) % 2])
                    if t == A0["turned"]:
                        turned_act(act, NC + nxt, (u + 1) % 2, MISC)
                    if t == A0["rested"]:
                        rest_act(act, NC + nxt, (u + 1) % 2, MISC)
                    if t == A0["router_act"]:
                        router(nxt)
                    if t == A0["gexp"]:
                        gates_act(act, M0, nxt, True)
                    if t == 4:
                        high(act, att1_p[u:u + 1], i)
                post_act(act, M0, c)

            router(0)
            gates_act(act, M0, 0, True)
            with act.Fori(0, 2) as i:
                for u in range(2):
                    chunk(i, u)

        @block.vector
        def _(dve):

            def chunk(i, u):
                c = 2 * i + u
                nxt, tile = ahead(i, u)
                before = 2 * NP * i if u else i * (-2 * NP) + 3 * NP
                for t in range(T0):
                    dve.wait_ge(M0["z"].sem, M0["z"].at(c, t + 1))
                    dve.wait_ge(M0["gb"].sem, M0["gb"].at(c, t // 2 + 1))
                    dve.wait_ge(M0["zl"].sem, M0["zl"].at(c, max(t + 1 - RING0, 0)))
                    dve.tensor_tensor(zg[:, t % RING0], zbuf[:, t % 2], banks[:, 5 + t // 2 % 2, 0:NT],
                                      ALU.mult).then_inc(M0["g"].sem, 1)
                    if t in A0["stats"]:
                        dve.wait_ge(fh.sem, fh.at(c, 0))
                        plain(dve)
                        norm_stats(dve, NC + nxt, tile, (2 * t, 2 * t + 1))
                    if t == A0["moments"]:
                        norm_moments(dve, NC + nxt)
                    if t in A0["norm"]:
                        k = 2 * A0["norm"].index(t)
                        norm_dve2(dve, NC + nxt, tile, xn[:, (u + 1) % 2], (k, k + 1))
                    if t == A0["turned"]:
                        turned_dve(dve, NC + nxt, (u + 1) % 2, MISC)
                    if t == A0["rested"]:
                        rest_dve(dve, NC + nxt, (u + 1) % 2, MISC)
                    for k in range(3):
                        if t == A0["gates%d" % k]:
                            gates_dve(dve, M0, nxt, k, True)
                    if t == A0["gout"]:
                        gates_out(dve, M0, nxt, (u + 1) % 2)
                    for p in range(NP):
                        if t == Y0["stats"][p]:
                            out_stats(c, p)
                    if t == Y0["moments"]:
                        out_moments(c)
                    for p in range(NP):
                        if t == Y0["centred"][p]:
                            out_centred(c, p)
                        if t == Y0["added"][p]:
                            out_added(c, p, before)
                dve.wait_ge(fh.sem, fh.at(c, NP))
                plain(dve)
                for q in range(2):
                    dve.wait_ge(M0["po"].sem, M0["po"].at(c, q + 1))
                    dve.tensor_tensor(y0[:, 2 * q:2 * q + 2, :], turned_back(q),
                                      xn[:, u, 2 * q:2 * q + 2, 0:D], ALU.add).then_inc(fadd.sem, 1)

            def out_stats(n, p):
                dve.wait_ge(fadd.sem, fadd.at(n, 0))
                plain(dve)
                dve.bn_stats(ystats[:, p, :], y0[:, p, :]).then_inc(fst.sem, 1)

            def out_moments(n):
                for p in range(NP):
                    dve.wait_ge(fst.sem, fst.at(n, p + 1))
                    plain(dve)
                    dve.bn_aggr(ymv[:, p, :], ystats[:, p, :]).then_inc(fmv.sem, 1)
                dve.wait_ge(fmv.sem, fmv.at(n, NP))
                dve.tensor_scalar(yrstd[:], ymv[:, :, 1], EPS, None, ALU.add).then_inc(fve.sem, 1)

            def out_centred(n, p):
                dve.scalar_tensor_tensor(y0[:, p, :], y0[:, p, :], ymv[:, p, 0:1], row["gamma"],
                                         ALU.subtract, ALU.mult).then_inc(fx.sem, 1)

            def out_added(n, p, tile):
                dve.wait_ge(frs.sem, frs.at(n, 1))
                dve.wait_ge(fbeta.sem, fbeta.at(n, 0))
                dve.wait_ge(fx.sem, fx.at(n, p + 1))
                dve.scalar_tensor_tensor(h1(tile + p), y0[:, p, :], yrstd[:, p:p + 1], h1(tile + p),
                                         ALU.mult, ALU.add).then_inc(fh.sem, 1)

            dve.memset(y0, 0.0).then_inc(y_zero, 1)
            dve.wait_ge(y_zero, 1)
            for k in range(3):
                gates_dve(dve, M0, 0, k, True)
            gates_out(dve, M0, 0, 0)
            with dve.Fori(0, 2) as i:
                for u in range(2):
                    chunk(i, u)
            for p in range(NP):
                out_stats(NC, p)
            out_moments(NC)
            for p in range(NP):
                out_centred(NC, p)
            for p in range(NP):
                out_added(NC, p, (NC - 1) * NP)

        @block.tensor
        def _(pe):
            def router(n, u):
                turned_wait(pe, NC + n)
                split_pass(pe, banks[0:96, MISC, 0:NT], w1, (xh[:, u], xl[:, u], xr[:, u])).then_inc(r1_done.sem, 1)

            def logits(n):
                pe.wait_ge(r1_act.sem, r1_act.at(n, 1))
                for p in range(NP):
                    mm = pe.matmul(banks[0:RT, MISC, 10 * p:10 * p + 8], g1[:, RT * p:RT * p + RT],
                                   pack[0:96, K_W2:K_W2 + E0], start=True, stop=True)
                mm.then_inc(M0["lg"].sem, 1)

            def hidden(c, u, t):
                pe.wait_ge(M0["z"].sem, M0["z"].at(c, max(t - 2, 0)))
                split_pass(pe, banks[:, 2 + t % 3, 0:NT], [w[:, 128 * t:128 * t + 128] for w in dn0],
                           (xh[:, u], xl[:, u], xr[:, u])).then_inc(M0["hd"].sem, 1)

            def chunk(i, u):
                c = 2 * i + u
                nxt, _ = ahead(i, u)

                def spread(e):
                    pe.wait_ge(M0["g"].sem, M0["g"].at(c, max(2 * e - 2, 0)))
                    if e < 2:
                        pe.wait_ge(fadd.sem, fadd.at(c, 0))
                    pe.matmul(banks[:, 5 + e % 2, 0:NT], sel0[:, 128 * e:128 * e + 128], gT[:, u],
                              start=True, stop=True).then_inc(M0["gb"].sem, 1)

                pe.wait_ge(M0["gl"].sem, M0["gl"].at(c, 1))
                spread(0)
                for t in range(T0 + 2):
                    if t + 2 < T0:
                        hidden(c, u, t + 2)
                    if t % 2 == 0 and t // 2 + 1 < E0:
                        spread(t // 2 + 1)
                    if t >= 2:
                        down_pe(pe, M0, c, t - 2, T0, up_h, up_l, up0_r)
                    if t == A0["turn"]:
                        pe.wait_ge(fadd.sem, fadd.at(c, 0))
                        turn_pe(pe, NC + nxt, xn[:, (u + 1) % 2], MISC)
                    if t == A0["rest"]:
                        pe.wait_ge(PREP["xl"].sem, PREP["xl"].at(NC + nxt, 1))
                        pe.wait_ge(PREP["xh"].sem, PREP["xh"].at(NC + nxt, 1))
                        turn_rest_pe(pe, NC + nxt, xn[:, (u + 1) % 2], MISC)
                    if t == A0["router"]:
                        router(nxt, (u + 1) % 2)
                    if t == A0["logits"]:
                        logits(nxt)
                    if t == A0["gturn"]:
                        gates_pe(pe, M0, nxt)
                hidden(nxt, (u + 1) % 2, 0)
                hidden(nxt, (u + 1) % 2, 1)
                pe.wait_ge(M0["gl"].sem, M0["gl"].at(nxt, 1))
                post_pe(pe, M0, c)

            router(0, 0)
            hidden(0, 0, 0)
            hidden(0, 0, 1)
            logits(0)
            gates_pe(pe, M0, 0)
            with pe.Fori(0, 2) as i:
                for u in range(2):
                    chunk(i, u)

    first_half.close()

    zg = sb("zg1", [128, RING1, NT])
    zh = sb("zh1", [128, RING1, NT], F32R)
    zl = sb("zl1", [128, RING1, NT], F32R)
    xn = sb("xn1", [RT, NP, D + DR])
    big1 = sb("big1", [128, 2 * SZ_FFN1 + T1 * 128], F32R)
    rws = sb("rws", [128, 4 * SZ_RT], F32R)
    sel1 = sb("sel1", [SELW, (T1R + 1) * 128], F32R)
    ws = sb("w", [128, QJ, NT])
    sq = sb("w2", [128, QJ, NT])
    wn = sb("wn", [128, QJ, NT])
    o1 = [sq[:, j] for j in range(QJ)]
    n2 = sb("n2", [128, QJ, IMG])
    w2n = sb("w2_norms", [128, QJ, IMG])
    dots = sb("dots", [128, QJ, IMG])
    pq = zbuf[0:NH].rearrange("q a t -> q (a t)")[:, 0:NT + IMG]
    hs = sb("hs", [NH, 3, IMG])
    pq_h = zh[0:NH].rearrange("q a t -> q (a t)")[:, 0:NT + IMG]
    pq_l = zl[0:NH].rearrange("q a t -> q (a t)")[:, 0:NT + IMG]

    def heads(j):
        return (xh, xl, xr)[j // 2][0:NH, 1, 128 * (j % 2):128 * (j % 2) + 128]


    big1_h, big1_l, dn1_r = big1[:, 0:SZ_FFN1], big1[:, SZ_FFN1:2 * SZ_FFN1], big1[:, 2 * SZ_FFN1:]
    ffn1_q = straight(a["w_rt"], rws[:, 0:2 * SZ_RT], rws[:, 2 * SZ_RT:], 2 * SZ_RT) + \
        side_by_side(a["w_dn1_r"], T1, dn1_r)
    ffn1_p = looped(a["w_ffn1"], big1_h, big1_l, SZ_FFN1, NC, 4)

    S3 = new_mix("att1", QJ, 1, 1, RING1)
    M1 = new_mix("ffn1", T1, 24, 4, RING1)
    M1["gb"] = sig("ffn1_gate_spread", T1R + 1)
    rw = [rws[:, i * SZ_RT:(i + 1) * SZ_RT] for i in (0, 2, 1, 3)]
    w_done, w_cp, w_sq = sig("w_done", QJ), sig("w_copied", QJ), sig("w_squared", QJ)
    n_sum, n_max, n_rec, w_nrm = sig("norm_sum", QJ), sig("norm_guard"), sig("norm_recip"), sig("w_normed", QJ)
    l_done, l_t = sig("token_logits"), sig("token_logits_temp")
    hv, l_sub, l_exp = sig("head_steps", 7), sig("token_less_max"), sig("token_exp")
    pb_done, pq_split = sig("pi_spread", QJ), sig("pi_split", 2)
    heads_done = sem("head_selectors_rounded")
    o_w, o_e, d_sum, d_st = sig("w_pi", QJ), sig("w2_pi", QJ), sig("dots_sum", QJ), sig("dots_steps", QJ + 2)
    d_rec = sig("dots_recip")
    bo_done, att1_h = sig("bout_added"), sig("att1_residual", 2)
    sel1_in, sel1_done = sem("late_selectors_in"), sem("late_selectors_rounded")
    qk = [w[:, o:o + SZ_QKV] for o in (0, SZ_QKV) for w in (mid_h, mid_l)]
    wo_h, wo_l = mid_h[:, 2 * SZ_QKV:], mid_l[:, 2 * SZ_QKV:]
    sel1_stage = ws[0:SELW].rearrange("q j t -> q (j t)")[:, 0:(T1R + 1) * 128]
    W_BANK = (2, 3, 6)

    def logits(pe, n, u):
        turned_wait(pe, 3 * NC + n)
        H, L, RH, RL = rw
        for p in range(NP):
            t = slice(RT * p, RT * p + RT)
            seq = [(xh, H), (xh, L), (xr, RH), (xr, RL), (xl, H)]
            for k, (st, m) in enumerate(seq):
                mm = pe.matmul(banks[0:RT, MISC, 10 * p:10 * p + 10], st[:, u, t], m, start=(k == 0), stop=(k == 4))
        mm.then_inc(M1["lg"].sem, 1)

    def img(v):
        return v.rearrange("q (i n) -> q i n", n=NTOK)

    with nc.Block() as block:
        @block.sync
        def _(sp):
            start_at_one(sp)
            load(sp, ffn1_q)
            with sp.Fori(0, NC) as c:
                load(sp, ffn1_p, c)
            sp.wait_ge(o_e.sem, o_e.at(NC - 1, QJ))
            sp.dma_start(sel1_stage, a["sel"][0:SELW, E0 * 128:]).then_inc(sel1_in, 16)

        @block.gpsimd
        def _(pool):
            low(pool, ffn1_q)
            with pool.Fori(0, NC) as c:
                norm_pool(pool, 2 * NC + 1 + c)
                pool.wait_ge(PREP["xn"].sem, PREP["xn"].at(2 * NC + c, NP))
                pool.tensor_tensor(hc(c * NP), hc(c * NP), row["bout"].unsqueeze(1).to_broadcast([RT, NP, D]),
                                   ALU.add).then_inc(bo_done.sem, 1)
                low(pool, ffn1_p[0:2], c)
                for j in range(QJ):
                    pool.wait_ge(o_w.sem, o_w.at(c, j + 1))
                    pool.tensor_tensor(wn[:, j], o1[j], ws[:, j], ALU.mult).then_inc(o_e.sem, 1)
                for j in range(QJ):
                    z_low(pool, S3, c, j)
                low(pool, ffn1_p[2:4], c)

        @block.scalar
        def _(act):
            def copied(n, j):
                act.wait_ge(w_done.sem, w_done.at(n, j + 1))
                act.activation(ws[:, j], banks[:, W_BANK[j % 3], 0:NT], ACT.Copy).then_inc(w_cp.sem, 1)

            def squared(n, j):
                act.activation(sq[:, j], banks[:, W_BANK[j % 3], 0:NT], ACT.Square).then_inc(w_sq.sem, 1)

            def chunk(c, last=False):
                act.wait_ge(l_done.sem, l_done.at(c, 1))
                act.activation(pq[:, 0:NT], banks[0:NH, 4, 0:NT], ACT.Copy, scale=pack[0:NH, K_TEMP:K_TEMP + 1]).then_inc(l_t.sem, 1)
                act.wait_ge(l_sub.sem, l_sub.at(c, 1))
                act.activation(pq[:, 0:NT], pq[:, 0:NT], ACT.Exp).then_inc(l_exp.sem, 1)
                high(act, ffn1_p[0:1], c)
                norm_act(act, 2 * NC + 1 + c, xn)
                high(act, ffn1_p[1:2], c)
                turned_act(act, 2 * NC + 1 + c, 0, MISC)
                rest_act(act, 2 * NC + 1 + c, 0, MISC)
                if last:
                    high(act, ffn1_p[2:4], c)
                for j in range(QJ):
                    if not last and j == 0:
                        for k in range(3):
                            act.wait_ge(o_e.sem, o_e.at(c, k + 1))
                            copied(c + 1, k)
                    z_high(act, S3, c, j)
                    if j == 3 and last:
                        gates_act(act, M1, 0, False)
                    if not last:
                        act.wait_ge(S3["g"].sem, S3["g"].at(c, j + 1))
                        squared(c + 1, j)
                        if 1 <= j <= 3:
                            act.wait_ge(o_e.sem, o_e.at(c, j + 3))
                            copied(c + 1, j + 2)
                post_act(act, S3, c)
                if not last:
                    high(act, ffn1_p[2:4], c)

            high(act, ffn1_q)
            for j in range(QJ):
                copied(0, j)
                squared(0, j)
            with act.Fori(0, NC - 1) as c:
                chunk(c)
            chunk(NC - 1, True)
            act.wait_ge(sel1_in, 16)
            act.activation(sel1[:], sel1_stage, ACT.Copy).then_inc(sel1_done, 1)

        @block.vector
        def _(dve):
            def norm_of(n, j):
                dve.wait_ge(w_sq.sem, w_sq.at(n, j + 1))
                dve.tensor_reduce(w2n[:, j, :], img(sq[:, j]), X, ALU.add).then_inc(n_sum.sem, 1)

            def normed(n):
                dve.wait_ge(n_sum.sem, n_sum.at(n, QJ))
                dve.tensor_scalar(w2n[:], w2n[:], 1e-24, None, ALU.max).then_inc(n_max.sem, 1)
                dve.wait_ge(n_max.sem, n_max.at(n, 1))
                dve.reciprocal(w2n[:], w2n[:]).then_inc(n_rec.sem, 1)
                dve.wait_ge(n_rec.sem, n_rec.at(n, 1))
                for j in range(QJ):
                    dve.tensor_tensor(img(wn[:, j]), img(sq[:, j]), w2n[:, j, :].unsqueeze(2).to_broadcast([128, IMG, NTOK]),
                                      ALU.mult).then_inc(w_nrm.sem, 1)

            def chunk(c, last=False):
                following = 2 * NC + 1 + c
                tile = 0 if last else c * NP + NP
                dve.wait_ge(att1_h.sem, att1_h.at(c, 0))
                plain(dve)
                norm_dve(dve, following, tile)
                k = [0]

                def link(ins):
                    k[0] += 1
                    ins.then_inc(hv.sem, 1)
                    dve.wait_ge(hv.sem, hv.at(c, k[0]))

                def wide(v):
                    return v.unsqueeze(2).to_broadcast([NH, IMG, NTOK])
                dve.wait_ge(l_t.sem, l_t.at(c, 1))
                link(dve.tensor_reduce(hs[:, 0, :], img(pq[:, 0:NT]), X, ALU.max))
                dve.tensor_tensor(img(pq[:, 0:NT]), img(pq[:, 0:NT]), wide(hs[:, 0, :]), ALU.subtract).then_inc(l_sub.sem, 1)
                norm_dve2(dve, following, tile, xn)
                dve.wait_ge(l_exp.sem, l_exp.at(c, 1))
                link(dve.tensor_reduce(hs[:, 1, :], img(pq[:, 0:NT]), X, ALU.add))
                link(dve.reciprocal(hs[:, 2, :], hs[:, 1, :]))
                link(dve.tensor_tensor(img(pq[:, 0:NT]), img(pq[:, 0:NT]), wide(hs[:, 2, :]), ALU.mult))
                link(dve.tensor_reduce(hs[:, 1, :], img(pq[:, 0:NT]), X, ALU.add))
                link(dve.tensor_scalar(hs[:, 1, :], hs[:, 1, :], 1e-8, None, ALU.add))
                link(dve.reciprocal(pq[:, NT:NT + IMG], hs[:, 1, :]))
                dve.tensor_copy(pq_h, pq).then_inc(pq_split.sem, 1)
                dve.wait_ge(pq_split.sem, pq_split.at(c, 1))
                dve.tensor_tensor(pq_l, pq, pq_h.bitcast(F32), ALU.subtract).then_inc(pq_split.sem, 1)

                def dot(j):
                    dve.wait_ge(o_e.sem, o_e.at(c, j + 1))
                    dve.tensor_reduce(n2[:, j, :], img(wn[:, j]), X, ALU.add).then_inc(d_sum.sem, 1)

                for j in range(QJ):
                    dve.wait_ge(pb_done.sem, pb_done.at(c, j + 1))
                    dve.tensor_tensor(o1[j], ws[:, j], banks[:, 4 + j % 2, 0:NT], ALU.mult).then_inc(o_w.sem, 1)
                    dve.tensor_copy(dots[:, j, :], banks[:, 4 + j % 2, NT:NT + IMG]).then_inc(d_st.sem, 1)
                    if j == 0:
                        turned_dve(dve, following, 0, MISC)
                    if j == 3:
                        rest_dve(dve, following, 0, MISC)
                    if j >= 2:
                        dot(j - 2)
                dot(QJ - 2)
                dot(QJ - 1)
                dve.wait_ge(d_sum.sem, d_sum.at(c, QJ))
                dve.wait_ge(d_st.sem, d_st.at(c, QJ))
                dve.tensor_tensor(n2[:], n2[:], dots[:], ALU.mult).then_inc(d_st.sem, 1)
                dve.wait_ge(d_st.sem, d_st.at(c, QJ + 1))
                dve.tensor_scalar(n2[:], n2[:], 1.0, -1.0, ALU.add, ALU.mult).then_inc(d_st.sem, 1)
                dve.wait_ge(d_st.sem, d_st.at(c, QJ + 2))
                dve.reciprocal(n2[:], n2[:]).then_inc(d_rec.sem, 1)
                dve.wait_ge(d_rec.sem, d_rec.at(c, 1))
                for j in range(QJ):
                    dve.wait_ge(S3["zl"].sem, S3["zl"].at(c, max(j - 2, 0)))
                    dve.tensor_tensor(img(zg[:, j % 3]), img(o1[j]), n2[:, j, :].unsqueeze(2).to_broadcast([128, IMG, NTOK]),
                                      ALU.mult).then_inc(S3["g"].sem, 1)
                    if j >= 2 and not last:
                        norm_of(c + 1, j - 2)
                    if j >= 3 and last:
                        gates_dve(dve, M1, 0, j - 3, False)
                if not last:
                    for j in range(QJ - 2, QJ):
                        norm_of(c + 1, j)
                    normed(c + 1)
                dve.wait_ge(bo_done.sem, bo_done.at(c, 1))
                for q in range(2):
                    dve.wait_ge(S3["po"].sem, S3["po"].at(c, q + 1))
                    dve.tensor_tensor(hc(c * NP + 2 * q, 2), hc(c * NP + 2 * q, 2), turned_back(q), ALU.add).then_inc(att1_h.sem, 1)
                if last:
                    gates_out(dve, M1, 0, 0)

            for j in range(QJ):
                dve.tensor_copy(heads(j), const[0:NH, C_SB + 128 * j:C_SB + 128 * (j + 1)]).then_inc(heads_done, 1)
            for j in range(QJ):
                norm_of(0, j)
            normed(0)
            with dve.Fori(0, NC - 1) as c:
                chunk(c)
            chunk(NC - 1, True)

        @block.tensor
        def _(pe):
            def features(n, j):
                if j >= 3:
                    pe.wait_ge(w_sq.sem, w_sq.at(n, j - 2))
                split_pass(pe, banks[:, W_BANK[j % 3], 0:NT], [w[:, 128 * j:128 * j + 128] for w in qk],
                           (xh[:, 0], xl[:, 0], xr[:, 0])).then_inc(w_done.sem, 1)

            def chunk(c, last=False):
                following = 2 * NC + 1 + c
                for j in range(QJ):
                    pe.wait_ge(w_nrm.sem, w_nrm.at(c, j + 1))
                    mm = pe.matmul(banks[0:NH, 4, 0:NT], const[:, C_B + NH * j:C_B + NH * (j + 1)], wn[:, j],
                                   start=(j == 0), stop=(j == QJ - 1))
                mm.then_inc(l_done.sem, 1)
                pe.wait_ge(att1_h.sem, att1_h.at(c, 0))
                turn_pe(pe, following, xn, MISC)
                pe.wait_ge(pq_split.sem, pq_split.at(c, 2))
                for j in range(QJ):
                    if j >= 2:
                        pe.wait_ge(d_st.sem, d_st.at(c, j - 1))
                    head = heads(j)
                    pe.matmul(banks[:, 4 + j % 2, 0:NT + IMG], head, pq_h, start=True, stop=False)
                    pe.matmul(banks[:, 4 + j % 2, 0:NT + IMG], head, pq_l, start=False, stop=True).then_inc(pb_done.sem, 1)
                    if j == 2:
                        pe.wait_ge(PREP["xl"].sem, PREP["xl"].at(following, 1))
                        turn_rest_pe(pe, following, xn, MISC)
                turned_wait(pe, following)
                if not last:
                    for j in range(3):
                        features(c + 1, j)
                if last:
                    logits(pe, 0, 0)
                for j in range(QJ):
                    down_pe(pe, S3, c, j, QJ, wo_h, wo_l, wo_r)
                    if j < 3 and not last:
                        features(c + 1, j + 3)
                if not last:
                    pe.wait_ge(w_sq.sem, w_sq.at(c + 1, QJ))
                else:
                    pe.wait_ge(M1["gs"].sem, M1["gs"].at(0, 1))
                post_pe(pe, S3, c)
                if last:
                    pe.wait_ge(att1_h.sem, att1_h.at(c, 2))
                    gates_pe(pe, M1, 0)

            turned_wait(pe, 2 * NC)
            for j in range(QJ):
                features(0, j)
            pe.wait_ge(heads_done, QJ)
            with pe.Fori(0, NC - 1) as c:
                chunk(c)
            chunk(NC - 1, True)

    out_done = sem("stored")
    gu = [w[:, o:o + SZ_GU] for o in (0, SZ_GU) for w in (big1_h, big1_l)]
    dn_h, dn_l = big1_h[:, 2 * SZ_GU:], big1_l[:, 2 * SZ_GU:]
    A1 = plan(stats=(0, 1), moments=2, norm=(3, 4), turn=5, turned=6, rest=7, rested=8, logits=9, gates0=10, gexp=11, gates1=11,
              gates2=12, gturn=13, gout=14)

    with nc.Block() as block:
        @block.sync
        def _(sp):
            start_at_one(sp)
            for c in range(NC):
                sp.wait_ge(M1["ph"].sem, M1["ph"].at(c, 2))
                sp.dma_start(a["out"][c], h[:, c * NP:(c + 1) * NP, :]).then_inc(out_done, 16)
            sp.wait_ge(out_done, 16 * NC)

        @block.gpsimd
        def _(pool):
            def chunk(i, u):
                for t in range(T1):
                    z_low(pool, M1, 2 * i + u, t)
                    if t == A1["moments"]:
                        norm_pool(pool, 3 * NC + ahead(i, u)[0])

            with pool.Fori(0, 2) as i:
                for u in range(2):
                    chunk(i, u)

        @block.scalar
        def _(act):
            def chunk(i, u):
                c = 2 * i + u
                nxt, _ = ahead(i, u)

                def silu(t):
                    act.wait_ge(M1["hd"].sem, M1["hd"].at(c, t + 1))
                    act.wait_ge(M1["u"].sem, M1["u"].at(c, max(t - 1, 0)))
                    act.activation(zbuf[:, t % 2], banks[:, 2 + t % 2, 0:NT], ACT.Silu).then_inc(M1["z"].sem, 1)

                silu(0)
                for t in range(T1):
                    if t + 1 < T1:
                        silu(t + 1)
                    z_high(act, M1, c, t)
                    if t == A1["norm"][1]:
                        norm_act(act, 3 * NC + nxt, xn)
                    if t == A1["turned"]:
                        turned_act(act, 3 * NC + nxt, (u + 1) % 2, MISC)
                    if t == A1["rested"]:
                        rest_act(act, 3 * NC + nxt, (u + 1) % 2, MISC)
                    if t == A1["gexp"]:
                        gates_act(act, M1, nxt, False)
                post_act(act, M1, c)

            with act.Fori(0, 2) as i:
                for u in range(2):
                    chunk(i, u)

        @block.vector
        def _(dve):
            def chunk(i, u):
                c = 2 * i + u
                nxt, tile = ahead(i, u)
                for t in range(T1):
                    zz = t % 3
                    dve.wait_ge(M1["z"].sem, M1["z"].at(c, t + 1))
                    dve.wait_ge(M1["zl"].sem, M1["zl"].at(c, max(t - 2, 0)))
                    dve.tensor_tensor(zg[:, zz], zbuf[:, t % 2], banks[:, 4 + t % 2, 0:NT], ALU.mult).then_inc(M1["u"].sem, 1)
                    dve.wait_ge(M1["u"].sem, M1["u"].at(c, t + 1))
                    dve.wait_ge(M1["gb"].sem, M1["gb"].at(c, min(t, T1R) + 1))
                    dve.tensor_tensor(zg[:, zz], zg[:, zz], banks[:, GB, 0:NT], ALU.mult).then_inc(M1["g"].sem, 1)
                    if t in A1["stats"]:
                        dve.wait_ge(M1["ph"].sem, M1["ph"].at(c, 0))
                        plain(dve)
                        k = 2 * A1["stats"].index(t)
                        norm_stats(dve, 3 * NC + nxt, tile, (k, k + 1))
                    if t == A1["moments"]:
                        norm_moments(dve, 3 * NC + nxt)
                    if t in A1["norm"]:
                        k = 2 * A1["norm"].index(t)
                        norm_dve2(dve, 3 * NC + nxt, tile, xn, (k, k + 1))
                    if t == A1["turned"]:
                        turned_dve(dve, 3 * NC + nxt, (u + 1) % 2, MISC)
                    if t == A1["rested"]:
                        rest_dve(dve, 3 * NC + nxt, (u + 1) % 2, MISC)
                    for k in range(3):
                        if t == A1["gates%d" % k]:
                            gates_dve(dve, M1, nxt, k, False)
                    if t == A1["gout"]:
                        gates_out(dve, M1, nxt, (u + 1) % 2)
                for q in range(2):
                    dve.wait_ge(M1["po"].sem, M1["po"].at(c, q + 1))
                    dve.tensor_tensor(hc(c * NP + 2 * q, 2), hc(c * NP + 2 * q, 2), turned_back(q), ALU.add).then_inc(M1["ph"].sem, 1)

            with dve.Fori(0, 2) as i:
                for u in range(2):
                    chunk(i, u)

        @block.tensor
        def _(pe):
            def hidden(c, u, t):
                pe.wait_ge(M1["u"].sem, M1["u"].at(c, max(t - 1, 0)))
                for k in range(2):
                    mm = split_pass(pe, banks[:, 2 + 2 * k + t % 2, 0:NT],
                                    [w[:, 256 * t + 128 * k:256 * t + 128 * k + 128] for w in gu],
                                    (xh[:, u], xl[:, u], xr[:, u]))
                mm.then_inc(M1["hd"].sem, 1)

            def chunk(i, u):
                c = 2 * i + u
                nxt, _ = ahead(i, u)
                def spread(e):
                    if e:
                        pe.wait_ge(M1["g"].sem, M1["g"].at(c, e))
                    else:
                        pe.wait_ge(M1["ph"].sem, M1["ph"].at(c, 0))
                    pe.matmul(banks[:, GB, 0:NT], sel1[:, 128 * e:128 * e + 128], gT[:, u],
                              start=True, stop=True).then_inc(M1["gb"].sem, 1)

                pe.wait_ge(M1["gl"].sem, M1["gl"].at(c, 1))
                spread(0)
                for t in range(T1 + 1):
                    if t + 1 < T1:
                        hidden(c, u, t + 1)
                    if t:
                        down_pe(pe, M1, c, t - 1, T1, dn_h, dn_l, dn1_r)
                    if t + 1 <= T1R:
                        spread(t + 1)
                    if t == A1["turn"]:
                        turn_pe(pe, 3 * NC + nxt, xn, MISC)
                    if t == A1["rest"]:
                        pe.wait_ge(PREP["xl"].sem, PREP["xl"].at(3 * NC + nxt, 1))
                        turn_rest_pe(pe, 3 * NC + nxt, xn, MISC)
                    if t == A1["logits"]:
                        logits(pe, nxt, (u + 1) % 2)
                    if t == A1["gturn"]:
                        gates_pe(pe, M1, nxt)
                hidden(nxt, (u + 1) % 2, 0)
                pe.wait_ge(M1["gl"].sem, M1["gl"].at(nxt, 1))
                post_pe(pe, M1, c)

            hidden(0, 0, 0)
            with pe.Fori(0, 2) as i:
                for u in range(2):
                    chunk(i, u)


def constants(np):
    c = np.zeros((128, C_ALL), np.float32)
    c[:, C_ID:C_ID + 128] = np.eye(128)
    c[:, C_II:C_II + DR] = np.tile(np.eye(DR), (2, 1))
    for j in range(QJ):
        for q in range(128):
            c[q, C_B + NH * j + 2 * j + q // 64] = 1
            c[2 * j + q // 64, C_SB + 128 * j + q] = 1
    for q in range(VR):
        c[q, C_VM + q // NTOK] = 1
    c[0:NTOK, C_MAB] = 1
    c[NTOK:RT, C_MAB + 1] = 1
    c[:, C_IOTA:C_IOTA + E0] = np.arange(E0)
    return c


def selectors(np):
    s = np.zeros((SELW, NSEL), np.float32)
    for n in range(NSEL):
        t, m = divmod(n, 128)
        e = t if t < E0 else ((128 * (t - E0) + m) // D if t - E0 < T1R else E0)
        s[e, n] = s[32 + e, n] = 1
    return s


def kernel(**inputs):
    import numpy as np
    import concourse.bacc as bacc
    from concourse.bass_utils import run_bass_kernel_spmd as run

    i = {k: np.asarray(v) for k, v in inputs.items()}
    cat = np.concatenate

    def twice(w):
        return cat([w, w], 0)

    x = i["x"].reshape(NI, 6, 16, 6, 16, 3).transpose(0, 1, 3, 2, 4, 5).reshape(NI, 36, 768)
    x = cat([np.zeros((NI, 1, 768), np.float32), x], 1)
    x = x.reshape(NC, IMG * NTOK, KP, 128).transpose(0, 3, 2, 1).reshape(NC * 128, KP * NT)

    def tiles(w):
        return w.reshape(-1, 128, w.shape[1]).transpose(1, 0, 2)

    basis = np.tile(i["L0_attn_basis_w"].T, (1, 2))
    val = i["L0_attn_value_w"].T
    dn0 = i["L0_ffn_down_w"].transpose(1, 0, 2).reshape(D, T0 * 128)
    up0 = tiles(i["L0_ffn_up_w"].reshape(T0 * 128, D))
    wo = tiles(i["L1_attn_w_out"])
    qkv = i["L1_attn_w_qkv"]
    gate = cat([i["L1_ffn_w_gate"].transpose(1, 0, 2).reshape(D, -1), i["L1_ffn_ws_gate"]], 1)
    up = cat([i["L1_ffn_w_up"].transpose(1, 0, 2).reshape(D, -1), i["L1_ffn_ws_up"]], 1)
    gu = np.stack([gate.reshape(D, T1, 128), up.reshape(D, T1, 128)], 2).reshape(D, SZ_GU)
    dn1 = tiles(cat([i["L1_ffn_w_down"].reshape(-1, D), i["L1_ffn_ws_down"]], 0))
    rt = cat([i["L1_ffn_router_w"], i["L1_ffn_sg_w"], np.zeros((D, 1), np.float32)], 1)
    pack = np.zeros((128, K_ALL), np.float32)
    pack[0:RT, K_ROWS:K_ROWS + D] = np.tile(i["L0_tok_pos_embedding"].reshape(NTOK, D), (2, 1))
    proj = np.tile(i["L0_tok_b_proj"], (NTOK, 1))
    proj[0] = i["L0_tok_cls_token"].reshape(D)
    for k, v in enumerate([np.tile(proj, (2, 1)), i["L0_attn_value_b"], i["L0_ffn_gamma"], i["L0_ffn_beta"],
                           i["L1_attn_b_out"]], 1):
        pack[0:RT, K_ROWS + D * k:K_ROWS + D * (k + 1)] = v
    pack[0:RT, K_B2:K_B2 + E0] = i["L0_ffn_b2"]
    pack[0:RT, K_SGB] = i["L1_ffn_sg_b"][0]
    pack[0:96, K_B1] = i["L0_ffn_b1"]
    pack[:, K_DB:K_DB + T0] = i["L0_ffn_down_b"].reshape(T0, 128).T
    pack[0:96, K_W2:K_W2 + E0] = i["L0_ffn_w2"]
    pack[0:NH, K_TEMP:K_TEMP + 1] = i["L1_attn_temp"].reshape(NH, 1)

    def k192(w):
        return cat([w[0:128], twice(w[128:])], 1)

    def main(w):
        return w[:, :, 0:128].reshape(128, -1)

    def rest(w):
        return w[:, :, 128:].reshape(128, -1)

    arrays = {
        "const": constants(np), "sel": selectors(np), "pack": pack, "patches": x,
        "w_tok": tiles(i["L0_tok_W_proj"]).reshape(128, -1),
        "w_att0": cat([k192(basis), k192(val)], 1),
        "w_ffn0": cat([k192(dn0), main(up0)], 1), "w_up0_r": rest(up0), "w_w1": k192(i["L0_ffn_w1"]),
        "w_att1": cat([k192(qkv), main(wo)], 1), "w_wo_r": rest(wo),
        "w_ffn1": cat([k192(gu), main(dn1)], 1), "w_dn1_r": rest(dn1), "w_rt": k192(rt),
        "hrt": twice(cat([i["L0_attn_head_residual"].transpose(2, 0, 1).reshape(RK, NH * RK), i["L0_attn_core"].T], 1)),
    }
    nc = bacc.Bacc("TRN2", target_bir_lowering=False, num_devices=1)
    fed, a = {}, {}
    for name, v in arrays.items():
        v = np.ascontiguousarray(v)
        fed["in_" + name] = v
        a[name] = nc.dram_tensor("in_" + name, v.shape, F32, kind="ExternalInput").ap()
    a["out"] = nc.dram_tensor("out_0", (NC, RT, NP, D), F32, kind="ExternalOutput").ap()
    tower(nc, a)
    r = run(nc, [fed], core_ids=[0])
    got = r.results[0]["out_0"]
    return got.transpose(0, 2, 1, 3).reshape(NI, NTOK, D)
```
